# Optimizing a Trainium2 kernel written in Bass

```python
import numpy as np
import jax
import jax.numpy as jnp

def _softmax(x, axis=-1):
    return jax.nn.softmax(x, axis=axis)
def _gelu(x):
    return jax.nn.gelu(x, approximate=True)
def _silu(x):
    return jax.nn.silu(x)
def _sigmoid(x):
    return jax.nn.sigmoid(x)
def _layernorm(x, axis=-1, eps=1e-5):
    m = jnp.mean(x, axis=axis, keepdims=True)
    v = jnp.var(x, axis=axis, keepdims=True)
    return (x - m) / jnp.sqrt(v + eps)
def _scatter_add(tgt, idx, src, axis=0):
    return tgt.at[idx].add(src)
def _segment_sum(src, seg, n):
    return jax.ops.segment_sum(src, seg, n)

kernel_name = 'mk_adj_preln_d4_adj_256_8db07b'

def setup_inputs(seed: int = 0):
    np.random.seed(seed)
    _w = jnp.asarray
    def _rec_inputs():
        import jax
        import jax.numpy as jnp
        _gk = jax.random.key(seed)
        x = -0.000125 + 0.9999 * jax.random.normal(jax.random.fold_in(_gk, 1), (128, 64, 256), jnp.float32)
        _w = (1.0 + jnp.arange(64, dtype=jnp.float32)) ** -0.5
        _w = _w / _w.mean()
        _pij = jnp.clip(0.125 * _w[:, None] * _w[None, :], 0.0, 1.0)
        _a = jax.random.uniform(jax.random.fold_in(_gk, 2), (64, 64)) < _pij
        _a = jnp.logical_or(_a, jnp.swapaxes(_a, -1, -2))
        _a = jnp.logical_or(_a, jnp.eye(64, dtype=bool))
        _af = _a.astype(jnp.float32)
        _af = _af * jax.random.uniform(jax.random.fold_in(_gk, 3), (64, 64), jnp.float32, 0.05, 0.000488281)
        adj = _af
        return x, adj
    x, adj = _rec_inputs()
    def _L0_gnn_setup():
        import jax, jax.numpy as jnp
        import numpy as np
        B, T, D, H = (64, 2048, 256, 256)
        MAX_SKIP = 4

        def _lstm_last(Wih, Whh, bih, bhh, xs):
            N, _, Hd = xs.shape
            bias = bih + bhh

            def step(carry, x_t):
                h, c = carry
                g = x_t @ Wih.T + h @ Whh.T + bias
                i, f, gg, o = jnp.split(g, 4, axis=-1)
                c = jax.nn.sigmoid(f) * c + jax.nn.sigmoid(i) * jnp.tanh(gg)
                h = jax.nn.sigmoid(o) * jnp.tanh(c)
                return ((h, c), None)
            init = (jnp.zeros((N, Hd), xs.dtype), jnp.zeros((N, Hd), xs.dtype))
            (h_last, _), _ = jax.lax.scan(step, init, jnp.swapaxes(xs, 0, 1))
            return h_last
        key = jax.random.key(seed)
        ks = jax.random.split(key, 8)
        s = 0.05
        x = jax.random.normal(ks[0], (B, T, D), jnp.float32)
        adj = jax.random.uniform(ks[1], (T, T), jnp.float32) / T
        Wg0 = jax.random.normal(ks[2], (D, H), jnp.float32) * s
        bg0 = jnp.zeros((H,), jnp.float32)
        Wg1 = jax.random.normal(ks[3], (H, H), jnp.float32) * s
        bg1 = jnp.zeros((H,), jnp.float32)
        Wih = jax.random.normal(ks[4], (MAX_SKIP, 4 * H, H), jnp.float32) * s
        Whh = jax.random.normal(ks[5], (MAX_SKIP, 4 * H, H), jnp.float32) * s
        bih = jax.random.normal(ks[6], (MAX_SKIP, 4 * H), jnp.float32) * s
        bhh = jax.random.normal(ks[7], (MAX_SKIP, 4 * H), jnp.float32) * s
        return dict(x=x, adj=adj, Wg0=Wg0, bg0=bg0, Wg1=Wg1, bg1=bg1, Wih=Wih, Whh=Whh, bih=bih, bhh=bhh)
    _L0_gnn_all = _L0_gnn_setup()
    _L0_gnn_in = {k: v for k, v in _L0_gnn_all.items() if k in ('Wg0', 'bg0', 'Wg1', 'bg1', 'Wih', 'Whh', 'bih', 'bhh', )}
    del _L0_gnn_all

    def _L1_gnn_setup():
        import jax, jax.numpy as jnp
        import numpy as np
        BT, N, D, HEADS, E = (1024, 64, 256, 4, 512)
        LRELU_SLOPE = 0.2
        EPS = 1e-08
        key = jax.random.key(seed)
        ks = jax.random.split(key, 8)
        d = D
        return {'H': jax.random.normal(ks[0], (BT, N, d), jnp.float32), 'W_lin': jax.random.normal(ks[1], (d, d), jnp.float32) / np.sqrt(d).astype(np.float32), 'W_val': jax.random.normal(ks[2], (d, d), jnp.float32) / np.sqrt(d).astype(np.float32), 'a': jax.random.normal(ks[3], (HEADS, d // HEADS), jnp.float32), 'W_out': jax.random.normal(ks[4], (d, d), jnp.float32) / np.sqrt(d).astype(np.float32), 'A0': jax.random.uniform(ks[5], (N, N), jnp.float32), 'src': jax.random.randint(ks[6], (E,), 0, N, jnp.int32), 'dst': jax.random.randint(ks[7], (E,), 0, N, jnp.int32)}
    _L1_gnn_all = _L1_gnn_setup()
    _L1_gnn_in = {k: v for k, v in _L1_gnn_all.items() if k in ('W_lin', 'W_val', 'a', 'W_out', 'src', 'dst', )}
    del _L1_gnn_all

    def _L2_gnn_setup():
        import jax, jax.numpy as jnp
        import numpy as np
        EPS = 1e-05

        def _batchnorm(x, gamma, beta):
            mu = jnp.mean(x, axis=0)
            var = jnp.var(x, axis=0)
            return (x - mu) * jax.lax.rsqrt(var + EPS) * gamma + beta
        key = jax.random.key(seed)
        ks = jax.random.split(key, 4)
        b, n, d, h, o = (32, 2048, 256, 512, 256)
        features = jax.random.normal(ks[0], (b, n, d), dtype=jnp.float32)
        A = jax.random.uniform(ks[1], (n, n), dtype=jnp.float32)
        lim1 = float(np.sqrt(6.0 / (d + h)))
        W1 = jax.random.uniform(ks[2], (h, d), minval=-lim1, maxval=lim1, dtype=jnp.float32)
        b1 = jnp.zeros((h,), jnp.float32)
        lim2 = float(np.sqrt(6.0 / (h + o)))
        W2 = jax.random.uniform(ks[3], (o, h), minval=-lim2, maxval=lim2, dtype=jnp.float32)
        b2 = jnp.zeros((o,), jnp.float32)
        g1 = jnp.ones((h,), jnp.float32)
        be1 = jnp.zeros((h,), jnp.float32)
        g2 = jnp.ones((o,), jnp.float32)
        be2 = jnp.zeros((o,), jnp.float32)
        return {'features': features, 'A': A, 'W1': W1, 'b1': b1, 'g1': g1, 'be1': be1, 'W2': W2, 'b2': b2, 'g2': g2, 'be2': be2}
    _L2_gnn_all = _L2_gnn_setup()
    _L2_gnn_in = {k: v for k, v in _L2_gnn_all.items() if k in ('W1', 'b1', 'g1', 'be1', 'W2', 'b2', 'g2', 'be2', )}
    del _L2_gnn_all

    def _L3_gnn_setup():
        import jax, jax.numpy as jnp
        import numpy as np
        ALPHA = 0.2
        key = jax.random.key(seed)
        k1, k2, k3, k4 = jax.random.split(key, 4)
        B, N, Fin, Fout = (8, 2048, 256, 256)
        h = jax.random.normal(k1, (B, N, Fin), dtype=jnp.float32)
        adj = jax.random.randint(k2, (N, N), 0, 2).astype(jnp.float32)
        adj = jnp.maximum(adj, jnp.eye(N, dtype=jnp.float32))

        def xavier(k, shape, gain=1.414):
            fan_in, fan_out = (shape[0], shape[1])
            a = gain * np.sqrt(6.0 / (fan_in + fan_out))
            return jax.random.uniform(k, shape, dtype=jnp.float32, minval=-a, maxval=a)
        W = xavier(k3, (Fin, Fout))
        a = xavier(k4, (2 * Fout, 1))
        return {'h': h, 'adj_matrix': adj, 'W': W, 'a': a}
    _L3_gnn_all = _L3_gnn_setup()
    _L3_gnn_in = {k: v for k, v in _L3_gnn_all.items() if k in ('W', 'a', )}
    del _L3_gnn_all

    return {
        "x": x,
        "adj": adj,
        "L0_gnn_Wg0": _L0_gnn_in["Wg0"],
        "L0_gnn_bg0": _L0_gnn_in["bg0"],
        "L0_gnn_Wg1": _L0_gnn_in["Wg1"],
        "L0_gnn_bg1": _L0_gnn_in["bg1"],
        "L0_gnn_Wih": _L0_gnn_in["Wih"],
        "L0_gnn_Whh": _L0_gnn_in["Whh"],
        "L0_gnn_bih": _L0_gnn_in["bih"],
        "L0_gnn_bhh": _L0_gnn_in["bhh"],
        "L1_gnn_W_lin": _L1_gnn_in["W_lin"],
        "L1_gnn_W_val": _L1_gnn_in["W_val"],
        "L1_gnn_a": _L1_gnn_in["a"],
        "L1_gnn_W_out": _L1_gnn_in["W_out"],
        "L1_gnn_src": _L1_gnn_in["src"],
        "L1_gnn_dst": _L1_gnn_in["dst"],
        "L2_gnn_W1": _L2_gnn_in["W1"],
        "L2_gnn_b1": _L2_gnn_in["b1"],
        "L2_gnn_g1": _L2_gnn_in["g1"],
        "L2_gnn_be1": _L2_gnn_in["be1"],
        "L2_gnn_W2": _L2_gnn_in["W2"],
        "L2_gnn_b2": _L2_gnn_in["b2"],
        "L2_gnn_g2": _L2_gnn_in["g2"],
        "L2_gnn_be2": _L2_gnn_in["be2"],
        "L3_gnn_W": _L3_gnn_in["W"],
        "L3_gnn_a": _L3_gnn_in["a"],
    }

def reference(x, adj, L0_gnn_Wg0, L0_gnn_bg0, L0_gnn_Wg1, L0_gnn_bg1, L0_gnn_Wih, L0_gnn_Whh, L0_gnn_bih, L0_gnn_bhh, L1_gnn_W_lin, L1_gnn_W_val, L1_gnn_a, L1_gnn_W_out, L1_gnn_src, L1_gnn_dst, L2_gnn_W1, L2_gnn_b1, L2_gnn_g1, L2_gnn_be1, L2_gnn_W2, L2_gnn_b2, L2_gnn_g2, L2_gnn_be2, L3_gnn_W, L3_gnn_a):
    import jax
    import jax.numpy as jnp
    def _L0_gnn_ref(x, adj, Wg0, bg0, Wg1, bg1, Wih, Whh, bih, bhh):
        import jax, jax.numpy as jnp
        import numpy as np
        B, T, D, H = (64, 2048, 256, 256)
        MAX_SKIP = 4

        def _lstm_last(Wih, Whh, bih, bhh, xs):
            N, _, Hd = xs.shape
            bias = bih + bhh

            def step(carry, x_t):
                h, c = carry
                g = x_t @ Wih.T + h @ Whh.T + bias
                i, f, gg, o = jnp.split(g, 4, axis=-1)
                c = jax.nn.sigmoid(f) * c + jax.nn.sigmoid(i) * jnp.tanh(gg)
                h = jax.nn.sigmoid(o) * jnp.tanh(c)
                return ((h, c), None)
            init = (jnp.zeros((N, Hd), xs.dtype), jnp.zeros((N, Hd), xs.dtype))
            (h_last, _), _ = jax.lax.scan(step, init, jnp.swapaxes(xs, 0, 1))
            return h_last
        h = jax.nn.relu(jnp.einsum('ts,bsh->bth', adj, x @ Wg0 + bg0))
        h = jax.nn.relu(jnp.einsum('ts,bsh->bth', adj, h @ Wg1 + bg1))
        Bv, Tv, Hd = h.shape
        for p in range(1, MAX_SKIP + 1):
            nw = Tv // p
            wins = h[:, :nw * p, :].reshape(Bv * nw, p, Hd)
            last = _lstm_last(Wih[p - 1], Whh[p - 1], bih[p - 1], bhh[p - 1], wins)
            idx = jnp.arange(nw) * p + (p - 1)
            h = h.at[:, idx, :].set(last.reshape(Bv, nw, Hd))
        return h

    def _L1_gnn_ref(H, W_lin, W_val, a, W_out, A0, src, dst):
        import jax, jax.numpy as jnp
        import numpy as np
        BT, N, D, HEADS, E = (1024, 64, 256, 4, 512)
        LRELU_SLOPE = 0.2
        EPS = 1e-08
        bt, n, d = H.shape
        h, dh = a.shape
        Xq = (H @ W_lin.T).reshape(bt, n, h, dh)
        Xv = (H @ W_val.T).reshape(bt, n, h, dh)
        Qs = Xq[:, src]
        Kt = Xq[:, dst]
        e = jnp.einsum('behd,hd->beh', jax.nn.leaky_relu(Qs + Kt, LRELU_SLOPE), a)
        e = e + jnp.log(A0[src, dst] + EPS)[None, :, None]
        e_t = e.transpose(1, 0, 2)
        m = jax.ops.segment_max(e_t, src, num_segments=n)
        ex = jnp.exp(e_t - m[src])
        denom = jax.ops.segment_sum(ex, src, num_segments=n)
        attn = ex / denom[src]
        Vt = Xv[:, dst].transpose(1, 0, 2, 3)
        Y = jax.ops.segment_sum(attn[..., None] * Vt, src, num_segments=n)
        Y = Y.transpose(1, 0, 2, 3).reshape(bt, n, d)
        return Y @ W_out.T

    def _L2_gnn_ref(features, A, W1, b1, g1, be1, W2, b2, g2, be2):
        import jax, jax.numpy as jnp
        import numpy as np
        EPS = 1e-05

        def _batchnorm(x, gamma, beta):
            mu = jnp.mean(x, axis=0)
            var = jnp.var(x, axis=0)
            return (x - mu) * jax.lax.rsqrt(var + EPS) * gamma + beta
        b, n, d = features.shape
        A_norm = A + jnp.eye(n, dtype=A.dtype)
        deg = jnp.sum(A_norm, axis=0) + jnp.sum(A_norm, axis=1) - jnp.diagonal(A_norm)
        dinv = jax.lax.rsqrt(deg)
        A_hat = A_norm * dinv[:, None] * dinv[None, :]
        agg = jnp.einsum('nm,bmd->bnd', A_hat, features)
        x = agg.reshape(-1, d)
        h = jax.nn.relu(_batchnorm(x @ W1.T + b1, g1, be1))
        out = h @ W2.T + b2
        out = _batchnorm(out, g2, be2)
        return out.reshape(b, n, -1)

    def _L3_gnn_ref(h, adj_matrix, W, a):
        import jax, jax.numpy as jnp
        import numpy as np
        ALPHA = 0.2
        Fout = W.shape[1]
        Wh = jnp.einsum('bnf,fo->bno', h, W)
        a1, a2 = (a[:Fout, 0], a[Fout:, 0])
        s1 = Wh @ a1
        s2 = Wh @ a2
        e = s1[:, :, None] + s2[:, None, :]
        e = jnp.where(e >= 0, e, ALPHA * e)
        e = jnp.where(adj_matrix[None] == 0, -jnp.inf, e)
        attention = jax.nn.softmax(e, axis=-1)
        h_prime = jnp.einsum('bij,bjo->bio', attention, Wh)
        return h_prime

    h = jnp.maximum(_layernorm(x, axis=-1), 0.0)
    x = x + _L0_gnn_ref(h, adj, L0_gnn_Wg0, L0_gnn_bg0, L0_gnn_Wg1, L0_gnn_bg1, L0_gnn_Wih, L0_gnn_Whh, L0_gnn_bih, L0_gnn_bhh)
    h = jnp.maximum(_layernorm(x, axis=-1), 0.0)
    x = x + _L1_gnn_ref(h, L1_gnn_W_lin, L1_gnn_W_val, L1_gnn_a, L1_gnn_W_out, adj, L1_gnn_src, L1_gnn_dst)
    h = jnp.maximum(_layernorm(x, axis=-1), 0.0)
    x = x + _L2_gnn_ref(h, adj, L2_gnn_W1, L2_gnn_b1, L2_gnn_g1, L2_gnn_be1, L2_gnn_W2, L2_gnn_b2, L2_gnn_g2, L2_gnn_be2)
    h = jnp.maximum(_layernorm(x, axis=-1), 0.0)
    x = x + _L3_gnn_ref(h, adj, L3_gnn_W, L3_gnn_a)
    return x


_drawn_inputs = setup_inputs


def setup_inputs(seed=0):
    import zlib

    import numpy as np

    out = dict(_drawn_inputs(seed))
    spreads = {'L0_gnn_bg0': (0.0, 0.8),
     'L0_gnn_bg1': (0.0, 0.8),
     'L2_gnn_b1': (0.0, 0.8),
     'L2_gnn_g1': (1.0, 0.2),
     'L2_gnn_be1': (0.0, 0.1),
     'L2_gnn_b2': (0.0, 0.8),
     'L2_gnn_g2': (1.0, 0.2),
     'L2_gnn_be2': (0.0, 0.1)}
    factors = {'L0_gnn_Wg0': 6.206, 'L0_gnn_Wg1': 5.341, 'L0_gnn_Wih': 3.504, 'L0_gnn_Whh': 6.624}
    for name, (base, spread) in spreads.items():
        noise = np.random.default_rng([zlib.crc32(name.encode()), seed]).standard_normal(out[name].shape)
        drawn = base * np.exp(spread * noise) if base else spread * noise
        out[name] = jnp.asarray(drawn.astype(out[name].dtype))
    for name, factor in factors.items():
        out[name] = (out[name] * factor).astype(out[name].dtype)
    return out
```

```python
from contextlib import ExitStack

import concourse.bass as bass
from concourse import mybir

F32 = mybir.dt.float32
F32R = mybir.dt.float32r
I32 = mybir.dt.int32
ALU = mybir.AluOpType
ACT = mybir.ActivationFunctionType
AX = mybir.AxisListType

P = 128
BATCH, NODES, D = 128, 64, 256
ROWS = BATCH * NODES
KD = D // P
TILE_GRAPHS = P // NODES
GT = 4
GROWS = GT * P
NG = ROWS // GROWS
EDGES = 512
EC = EDGES // P
HEADS, DH = 4, 64
SKIPS = 4
HID2 = 512
KH = HID2 // P
EPS = 1e-5
LOG_EPS = 1e-8
LEAK = 0.2
BIG = 3.0e38


def wait(eng, sem, value):
    if isinstance(value, int) and value <= 0:
        return
    eng.wait_ge(sem, value)


def f32(ap):
    return ap.bitcast(F32)


def mm3(nc, out, w_hi, w_lo, x_hi, x_lo, first, last):
    nc.tensor.matmul(out, w_hi, x_hi, start=first, stop=False)
    nc.tensor.matmul(out, w_hi, x_lo, start=False, stop=False)
    return nc.tensor.matmul(out, w_lo, x_hi, start=False, stop=last)


class Core:

    def __init__(self, nc, ctx):
        self.nc, self.ctx = nc, ctx

    def sem(self, name):
        return self.ctx.enter_context(self.nc.semaphore(name))


def allocator(nc, ctx):
    def sb(name, shape, dt=F32):
        return ctx.enter_context(nc.sbuf_tensor(name, shape, dt))

    def ps(name, shape, dt=F32):
        return ctx.enter_context(nc.psum_tensor(name, shape, dt))

    return sb, ps


def both_ends(eng, n, body):
    body(0)
    with eng.Fori(1, n - 1) as i:
        body(i)
    body(n - 1)


def peeled(eng, n, body):
    body(0)
    with eng.Fori(1, n) as i:
        body(i)


class Chain:

    def __init__(self, eng, sem):
        self.eng, self.sem, self.n = eng, sem, 0

    def __call__(self, ins):
        self.n += 1
        ins.then_inc(self.sem, 1)
        self.eng.wait_ge(self.sem, self.n)


def gcn_phase(core, x, w, bg, adj_t, ident_in, HT):
    nc = core.nc
    NI = NG // 2
    with ExitStack() as ctx:
        sb, ps = allocator(nc, ctx)
        ident = sb("a_ident", [P, P])
        w_raw = sb("a_w_raw", [P, 2, KD, D])
        w_hi = sb("a_w_hi", [P, 2, KD, D], F32R)
        w_lo = sb("a_w_lo", [P, 2, KD, D], F32R)
        bias = sb("a_bias", [P, 2, D])
        adj_raw = sb("a_adj_raw", [P, P])
        adj_hi = sb("a_adj_hi", [P, P], F32R)
        adj_lo = sb("a_adj_lo", [P, P], F32R)
        mhalf = sb("a_mhalf", [P, GT])
        xt = [sb(f"a_xt{b}", [P, GT, D]) for b in range(2)]
        xn = [sb(f"a_xn{b}", [P, GT, D]) for b in range(2)]
        st = [sb(f"a_st{b}", [P, GT, 6]) for b in range(2)]
        mv = [sb(f"a_mv{b}", [P, GT, 2]) for b in range(2)]
        ve = [sb(f"a_ve{b}", [P, GT]) for b in range(2)]
        rstd = [sb(f"a_rstd{b}", [P, GT]) for b in range(2)]
        hT_hi = [sb(f"a_hThi{b}", [P, KD, GROWS], F32R) for b in range(2)]
        hT_lo = [sb(f"a_hTlo{b}", [P, KD, GROWS], F32R) for b in range(2)]
        u = [sb(f"a_u{b}", [P, GT, D]) for b in range(2)]
        u_hi = [sb(f"a_uhi{b}", [P, GT, D], F32R) for b in range(2)]
        u_lo = [sb(f"a_ulo{b}", [P, GT, D], F32R) for b in range(2)]
        pV = [ps(f"a_pV{b}", [P, KD, GROWS]) for b in range(2)]
        pU = [ps(f"a_pU{b}", [P, GT, D]) for b in range(2)]
        consts = core.sem("a_consts")
        zeroed = core.sem("a_zeroed")
        w_ready = core.sem("a_w_ready")
        x_in = [core.sem(f"a_x_in{b}") for b in range(2)]
        stats, moments = core.sem("a_stats"), core.sem("a_moments")
        var_eps, rstd_ready = core.sem("a_var_eps"), core.sem("a_rstd")
        normed, turned = core.sem("a_normed"), core.sem("a_turned")
        hi_done = [core.sem(f"a_hi{l}") for l in range(2)]
        lo_done = [core.sem(f"a_lo{l}") for l in range(2)]
        u_mm = [core.sem(f"a_u_mm{l}") for l in range(2)]
        u_sum = [core.sem(f"a_u_sum{l}") for l in range(2)]
        u_hi_done = [core.sem(f"a_u_hi{l}") for l in range(2)]
        u_lo_done = [core.sem(f"a_u_lo{l}") for l in range(2)]
        v_mm = [core.sem(f"a_v_mm{l}") for l in range(2)]
        out_done = core.sem("a_out")
        HTg = HT.rearrange("p k (g c) -> p k g c", c=GROWS)

        def n(it, b):
            return 2 * it + b + 1

        with nc.Block() as block:
            @block.sync
            def _(sp):
                sp.dma_start(ident[:, :], ident_in).then_inc(consts, 16)
                for l in range(2):
                    sp.dma_start(w_raw[:, l], w[l]).then_inc(consts, 16)
                    sp.dma_start(bias[:, l], bg[l]).then_inc(consts, 16)
                sp.wait_ge(zeroed, 1)
                for g in range(TILE_GRAPHS):
                    r = slice(g * NODES, (g + 1) * NODES)
                    sp.dma_start(adj_raw[r, r], adj_t).then_inc(consts, 16)

                def body(it):
                    for b in range(2):
                        wait(sp, normed, n(it, b) - 2)
                        sp.dma_start(xt[b][:, :, :], x[2 * it + b]).then_inc(x_in[b], 16)

                peeled(sp, NI, body)

            @block.gpsimd
            def _(pool):
                nc.gpsimd.memset(adj_raw[:, :], 0.0).then_inc(zeroed, 1)
                nc.gpsimd.memset(mhalf[:, :], -0.5).then_inc(zeroed, 1)
                pool.wait_ge(zeroed, 2)

                def body(it):
                    for b in range(2):
                        pool.wait_ge(var_eps, n(it, b))
                        wait(pool, normed, n(it, b) - 2)
                        nc.gpsimd.tensor_tensor(rstd[b][:, :], ve[b][:, :], mhalf[:, :], ALU.pow).then_inc(rstd_ready, 1)
                    for l in range(2):
                        for b in range(2):
                            pool.wait_ge(u_hi_done[l], n(it, b))
                            nc.gpsimd.tensor_tensor(u_lo[b][:, :, :], u[b][:, :, :], f32(u_hi[b][:, :, :]),
                                                    ALU.subtract).then_inc(u_lo_done[l], 1)

                peeled(pool, NI, body)

            @block.vector
            def _(dve):
                dve.wait_ge(consts, 16 * 7)
                dve.wait_ge(zeroed, 2)
                nc.vector.tensor_copy(w_hi[:, :, :, :], w_raw[:, :, :, :]).then_inc(w_ready, 1)
                nc.vector.tensor_copy(adj_hi[:, :], adj_raw[:, :]).then_inc(w_ready, 1)
                dve.wait_ge(w_ready, 2)
                nc.vector.tensor_tensor(w_lo[:, :, :, :], w_raw[:, :, :, :], f32(w_hi[:, :, :, :]), ALU.subtract).then_inc(w_ready, 1)
                nc.vector.tensor_tensor(adj_lo[:, :], adj_raw[:, :], f32(adj_hi[:, :]), ALU.subtract).then_inc(w_ready, 1)

                def body(it):
                    for b in range(2):
                        dve.wait_ge(x_in[b], 16 * it + 16)
                        wait(dve, moments, n(it, b) - 2)
                        for j in range(GT):
                            last = nc.vector.bn_stats(st[b][:, j, :], xt[b][:, j, :])
                        last.then_inc(stats, 1)
                        dve.wait_ge(stats, n(it, b))
                        wait(dve, rstd_ready, n(it, b) - 2)
                        nc.vector.memset(ve[b][:, :], EPS)
                        for j in range(GT):
                            last = nc.vector.bn_aggr(mv[b][:, j, :], st[b][:, j, :])
                        last.then_inc(moments, 1)
                    for b in range(2):
                        dve.wait_ge(moments, n(it, b))
                        nc.vector.tensor_tensor(ve[b][:, :], ve[b][:, :], mv[b][:, :, 1], ALU.add).then_inc(var_eps, 1)
                    for b in range(2):
                        dve.wait_ge(rstd_ready, n(it, b))
                        dve.wait_ge(moments, n(it, b))
                        wait(dve, turned, n(it, b) - 2)
                        for j in range(GT):
                            last = nc.vector.tensor_scalar(xn[b][:, j, :], xt[b][:, j, :], mv[b][:, j, 0:1],
                                                           rstd[b][:, j:j + 1], ALU.subtract, ALU.mult)
                        last.then_inc(normed, 1)
                    for l in range(2):
                        for b in range(2):
                            dve.wait_ge(hi_done[l], n(it, b))
                            nc.vector.scalar_tensor_tensor(out=hT_lo[b][:, :, :], in0=pV[b][:, :, :], scalar=0.0,
                                                           in1=f32(hT_hi[b][:, :, :]), op0=ALU.max,
                                                           op1=ALU.subtract).then_inc(lo_done[l], 1)
                        for b in range(2):
                            dve.wait_ge(u_mm[l], n(it, b))
                            if l == 0:
                                wait(dve, u_lo_done[1], n(it, b) - 2)
                            else:
                                dve.wait_ge(u_lo_done[0], n(it, b))
                            nc.vector.tensor_tensor(u[b][:, :, :], pU[b][:, :, :],
                                                    bias[:, l, :].unsqueeze(1).to_broadcast([P, GT, D]),
                                                    ALU.add).then_inc(u_sum[l], 1)

                peeled(dve, NI, body)

            @block.scalar
            def _(act):
                def body(it):
                    for l in range(2):
                        for b in range(2):
                            act.wait_ge(turned if l == 0 else v_mm[0], n(it, b))
                            nc.scalar.activation(hT_hi[b][:, :, :], pV[b][:, :, :], ACT.Relu).then_inc(hi_done[l], 1)
                        for b in range(2):
                            act.wait_ge(u_sum[l], n(it, b))
                            nc.scalar.activation(u_hi[b][:, :, :], u[b][:, :, :], ACT.Copy).then_inc(u_hi_done[l], 1)
                    for b in range(2):
                        act.wait_ge(v_mm[1], n(it, b))
                        nc.scalar.activation(HTg[:, :, 2 * it + b, :], pV[b][:, :, :], ACT.Relu).then_inc(out_done, 1)

                peeled(act, NI, body)

            @block.tensor
            def _(pe):
                pe.wait_ge(w_ready, 4)

                def body(it):
                    for b in range(2):
                        pe.wait_ge(normed, n(it, b))
                        wait(pe, out_done, n(it, b) - 2)
                        for j in range(GT):
                            for k in range(KD):
                                last = nc.tensor.transpose(pV[b][:, k, j * P:(j + 1) * P],
                                                           xn[b][:, j, k * P:(k + 1) * P], ident[:, :])
                        last.then_inc(turned, 1)
                    for l in range(2):
                        for b in range(2):
                            pe.wait_ge(hi_done[l], n(it, b))
                            pe.wait_ge(lo_done[l], n(it, b))
                            for j in range(GT):
                                c = slice(j * P, (j + 1) * P)
                                for k in range(KD):
                                    last = mm3(nc, pU[b][:, j, :], hT_hi[b][:, k, c], hT_lo[b][:, k, c],
                                               w_hi[:, l, k, :], w_lo[:, l, k, :], k == 0, k == KD - 1)
                            last.then_inc(u_mm[l], 1)
                        for b in range(2):
                            pe.wait_ge(u_hi_done[l], n(it, b))
                            pe.wait_ge(u_lo_done[l], n(it, b))
                            for k in range(KD):
                                c = slice(k * P, (k + 1) * P)
                                for j in range(GT):
                                    last = mm3(nc, pV[b][:, k, j * P:(j + 1) * P], u_hi[b][:, j, c], u_lo[b][:, j, c],
                                               adj_hi[:, :], adj_lo[:, :], True, True)
                            last.then_inc(v_mm[l], 1)

                peeled(pe, NI, body)


def lstm_phase(core, wih, whh, bih, bhh, HT):
    nc = core.nc
    NC4 = 4 * D
    I, F, G, O = range(4)
    SIG = {I: ACT.Sigmoid, F: ACT.Sigmoid, G: ACT.Tanh, O: ACT.Sigmoid}
    with ExitStack() as ctx:
        sb, ps = allocator(nc, ctx)
        raw = [sb(f"b_raw{m}", [P, KD, NC4]) for m in range(2)]
        w_hi = [[sb(f"b_whi{s}{m}", [P, KD, NC4], F32R) for m in range(2)] for s in range(2)]
        w_lo = [[sb(f"b_wlo{s}{m}", [P, KD, NC4], F32R) for m in range(2)] for s in range(2)]
        bias = sb("b_bias", [P, SKIPS, 8])
        bias2 = sb("b_bias2", [P, SKIPS, 8])
        xs_hi = [sb(f"b_xshi{b}", [P, KD, GROWS], F32R) for b in range(2)]
        xs_lo = [sb(f"b_xslo{b}", [P, KD, GROWS], F32R) for b in range(2)]
        hs_hi = [sb(f"b_hshi{b}", [P, KD, GROWS], F32R) for b in range(2)]
        hs_lo = [sb(f"b_hslo{b}", [P, KD, GROWS], F32R) for b in range(2)]
        cell = [sb(f"b_cell{b}", [P, KD, GROWS]) for b in range(2)]
        gate = [sb(f"b_gate{s}", [P, 4, GROWS]) for s in range(2)]
        tc = [sb(f"b_tc{s}", [P, GROWS]) for s in range(2)]
        pG = [ps(f"b_pG{s}", [P, 4, GROWS]) for s in range(2)]
        bias_in, raw_in = core.sem("b_bias_in"), core.sem("b_raw_in")
        bias_ready, w_part, w_ready = core.sem("b_bias_ready"), core.sem("b_w_part"), core.sem("b_w_ready")
        gate_mm, gate_act = core.sem("b_gate_mm"), core.sem("b_gate_act")
        xs_part, xs_ready = core.sem("b_xs_part"), core.sem("b_xs_ready")
        hs_part, hs_ready = core.sem("b_hs_part"), core.sem("b_hs_ready")
        ig_ready, fc_ready, cell_ready = core.sem("b_ig"), core.sem("b_fc"), core.sem("b_cell_ready")
        tanh_ready, h_ready = core.sem("b_tanh"), core.sem("b_h_ready")

        class Plan:

            def __init__(self, p, before):
                self.p = p
                self.nw = NODES // p
                self.graphs = GROWS // NODES if p == 1 else 2 * GROWS // NODES
                self.n = self.graphs * self.nw
                self.its = BATCH // (2 * self.graphs)
                self.units = 4 * p
                self.gates = 12 + 16 * (p - 1)
                if before is None:
                    self.u0 = self.g0 = self.x0 = self.h0 = self.i0 = self.w0 = 0
                else:
                    q = before
                    self.u0 = q.u0 + q.its * q.units
                    self.g0 = q.g0 + q.its * q.gates
                    self.x0 = q.x0 + 2 + q.its * 2 * q.p
                    self.h0 = q.h0 + q.its * 2 * (q.p - 1)
                    self.i0 = q.i0 + q.its * 4 * (q.p - 1)
                    self.w0 = q.w0 + (1 if q.p == 1 else 0) + (0 if q.p == 1 else q.wn)
                self.wn = 0

            def unit(self, it, t, b, s):
                return self.u0 + it * self.units + (2 * t + b) * 2 + s

            def gate(self, it, t, b, s):
                before = (2 * b + s) * 3 if t == 0 else 12 + 16 * (t - 1) + (2 * b + s) * 4
                return self.g0 + it * self.gates + before

            def later(self, it, t, b, s):
                return self.i0 + it * 4 * (self.p - 1) + (t - 1) * 4 + 2 * b + s

            def x(self, it, t, b):
                return self.x0 + it * 2 * self.p + 2 * t + b

            def h(self, it, t, b):
                return self.h0 + it * 2 * (self.p - 1) + 2 * t + b

            def order(self, t):
                return (I, G, O) if t == 0 else (I, G, F, O)

            def windows(self, it, b, k, t):
                v = HT.rearrange("p k (i g c) -> p k i g c", g=self.graphs, c=NODES)[:, k, 2 * it + b, :, :]
                return v[:, :, t:t + (self.nw - 1) * self.p + 1:self.p]

            def flat(self, ap):
                return ap[:, 0:self.n].rearrange("p (g w) -> p g w", w=self.nw)

        plans = []
        for p in range(1, SKIPS + 1):
            plans.append(Plan(p, plans[-1] if plans else None))
        w_count = [1]
        for q in plans[:-1]:
            w_count.append(w_count[-1] + q.its)

        def loop(eng, plan, body):
            if plan.p == 1:
                peeled(eng, plan.its, body)
            else:
                with eng.Fori(0, plan.its) as it:
                    body(it)

        with nc.Block() as block:
            @block.sync
            def _(sp):
                sp.dma_start(bias[:, :, :], bih).then_inc(bias_in, 16)
                sp.dma_start(bias2[:, :, :], bhh).then_inc(bias_in, 16)
                for p in range(SKIPS):
                    if p >= 1:
                        sp.wait_ge(w_ready, w_count[p - 1])
                    for m, src in enumerate((wih, whh)):
                        sp.dma_start(raw[m][:, :, :], src[p]).then_inc(raw_in, 16)

            @block.tensor
            def _(pe):
                for plan in plans:
                    slot = plan.p % 2
                    pe.wait_ge(w_ready, w_count[plan.p - 1])

                    def body(it, plan=plan, slot=slot):
                        for t in range(plan.p):
                            for b in range(2):
                                for s in range(2):
                                    if s == 0:
                                        pe.wait_ge(xs_ready, plan.x(it, t, b) + 1)
                                        if t:
                                            pe.wait_ge(hs_ready, plan.h(it, t - 1, b) + 1)
                                    ahead = 3 if t == 0 and (b or s) else 4
                                    if t == 0 and b == 0 and s == 0 and plan.p <= 2:
                                        ahead = 3
                                    if t == 1 and b == 0 and s == 0:
                                        ahead = 3
                                    wait(pe, gate_act, plan.gate(it, t, b, s) - ahead)
                                    for g in plan.order(t):
                                        c = slice(g * D + s * P, g * D + s * P + P)
                                        out = pG[s][:, g, 0:plan.n]
                                        pairs = [(0, xs_hi[b], xs_lo[b], k) for k in range(KD)]
                                        if t:
                                            pairs += [(1, hs_hi[b], hs_lo[b], k) for k in range(KD)]
                                        for i, (m, hi, lo, k) in enumerate(pairs):
                                            last = mm3(nc, out, w_hi[slot][m][:, k, c], w_lo[slot][m][:, k, c],
                                                       hi[:, k, 0:plan.n], lo[:, k, 0:plan.n],
                                                       i == 0, i == len(pairs) - 1)
                                        last.then_inc(gate_mm, 1)

                    loop(pe, plan, body)

            @block.scalar
            def _(act):
                act.wait_ge(bias_ready, 1)
                for plan in plans:
                    def body(it, plan=plan):
                        for t in range(plan.p):
                            for b in range(2):
                                for s in range(2):
                                    wait(act, h_ready, plan.unit(it, t, b, s) - 1)
                                    for i, g in enumerate(plan.order(t)):
                                        act.wait_ge(gate_mm, plan.gate(it, t, b, s) + i + 1)
                                        nc.scalar.activation(gate[s][:, g, 0:plan.n], pG[s][:, g, 0:plan.n], SIG[g],
                                                             bias=bias[:, plan.p - 1, 2 * g + s:2 * g + s + 1])\
                                            .then_inc(gate_act, 1)
                                    act.wait_ge(cell_ready, plan.unit(it, t, b, s) + 1)
                                    pt, pb = (t, 0) if b else (t - 1, 1)
                                    if 0 <= pt < plan.p - 1:
                                        act.wait_ge(hs_ready, plan.h(it, pt, pb) + 1)
                                    nc.scalar.activation(tc[s][:, 0:plan.n], cell[b][:, s, 0:plan.n],
                                                         ACT.Tanh).then_inc(tanh_ready, 1)

                    loop(act, plan, body)

            @block.gpsimd
            def _(pool):
                for plan in plans[1:]:
                    def body(it, plan=plan):
                        for t in range(1, plan.p):
                            for b in range(2):
                                for s in range(2):
                                    pool.wait_ge(gate_act, plan.gate(it, t, b, s) + 2)
                                    nc.gpsimd.tensor_tensor(gate[s][:, I, 0:plan.n], gate[s][:, I, 0:plan.n],
                                                            gate[s][:, G, 0:plan.n], ALU.mult).then_inc(ig_ready, 1)

                    loop(pool, plan, body)

            @block.vector
            def _(dve):
                dve.wait_ge(bias_in, 32)
                nc.vector.tensor_tensor(bias[:, :, :], bias[:, :, :], bias2[:, :, :], ALU.add).then_inc(bias_ready, 1)
                parts = [0, 0, 0]

                def split_w(slot, cols, last_sem):
                    for m in range(2):
                        nc.vector.tensor_copy(w_hi[slot][m][:, :, cols], raw[m][:, :, cols]).then_inc(w_part, 1)

                def split_w_lo(slot, cols):
                    for m in range(2):
                        last = nc.vector.tensor_tensor(w_lo[slot][m][:, :, cols], raw[m][:, :, cols],
                                                       f32(w_hi[slot][m][:, :, cols]), ALU.subtract)
                    last.then_inc(w_ready, 1)

                dve.wait_ge(raw_in, 32)
                split_w(1, slice(0, NC4), None)
                dve.wait_ge(w_part, 2)
                split_w_lo(1, slice(0, NC4))

                def split_x(plan, it, t, b, count):
                    for k in range(KD):
                        nc.vector.tensor_copy(plan.flat(xs_hi[b][:, k, :]), plan.windows(it, b, k, t))\
                            .then_inc(xs_part, 1)
                    dve.wait_ge(xs_part, KD * (count + 1))
                    for k in range(KD):
                        last = nc.vector.tensor_tensor(plan.flat(xs_lo[b][:, k, :]), plan.windows(it, b, k, t),
                                                       plan.flat(f32(xs_hi[b][:, k, :])), ALU.subtract)
                    last.then_inc(xs_ready, 1)

                for plan in plans:
                    n, T = plan.n, plan.p
                    wait(dve, h_ready, plan.u0)
                    wait(dve, xs_ready, plan.x0)
                    for b in range(2):
                        split_x(plan, 0, 0, b, plan.x0 + b)

                    def body(it, plan=plan, n=n, T=T):
                        for t in range(T):
                            for b in range(2):
                                for s in range(2):
                                    un, g0, ng = plan.unit(it, t, b, s), plan.gate(it, t, b, s), len(plan.order(t))
                                    c = cell[b][:, s, 0:n]
                                    if s == 1:
                                        dve.wait_ge(gate_mm, g0 + ng)
                                        if t < T - 1:
                                            split_x(plan, it, t + 1, b, plan.x(it, t + 1, b))
                                        else:
                                            wait(dve, h_ready, plan.u0 + it * plan.units)
                                            split_x(plan, (it + 1) & (plan.its - 1), 0, b, plan.x(it, T, b))
                                    if t == 0:
                                        dve.wait_ge(gate_act, g0 + 2)
                                        nc.vector.tensor_tensor(c, gate[s][:, I, 0:n], gate[s][:, G, 0:n],
                                                                ALU.mult).then_inc(cell_ready, 1)
                                    else:
                                        dve.wait_ge(gate_act, g0 + 3)
                                        nc.vector.tensor_tensor(c, gate[s][:, F, 0:n], c, ALU.mult).then_inc(fc_ready, 1)
                                        dve.wait_ge(fc_ready, plan.later(it, t, b, s) + 1)
                                        dve.wait_ge(ig_ready, plan.later(it, t, b, s) + 1)
                                        nc.vector.tensor_tensor(c, c, gate[s][:, I, 0:n], ALU.add).then_inc(cell_ready, 1)
                                    dve.wait_ge(gate_act, g0 + ng)
                                    dve.wait_ge(tanh_ready, un + 1)
                                    if t == T - 1:
                                        nc.vector.tensor_tensor(plan.windows(it, b, s, t), plan.flat(gate[s][:, O, :]),
                                                                plan.flat(tc[s][:, :]), ALU.mult).then_inc(h_ready, 1)
                                    else:
                                        nc.vector.tensor_tensor(tc[s][:, 0:n], gate[s][:, O, 0:n], tc[s][:, 0:n],
                                                                ALU.mult).then_inc(h_ready, 1)
                                if t < T - 1:
                                    for s in range(2):
                                        dve.wait_ge(h_ready, plan.unit(it, t, b, s) + 1)
                                        nc.vector.tensor_copy(hs_hi[b][:, s, 0:n], tc[s][:, 0:n]).then_inc(hs_part, 1)
                                    dve.wait_ge(hs_part, 2 * (plan.h(it, t, b) + 1))
                                    for s in range(2):
                                        last = nc.vector.tensor_tensor(hs_lo[b][:, s, 0:n], tc[s][:, 0:n],
                                                                       f32(hs_hi[b][:, s, 0:n]), ALU.subtract)
                                    last.then_inc(hs_ready, 1)
                        if plan.p < SKIPS:
                            wc = NC4 // plan.its
                            cols = bass.ds(it * wc, wc)
                            dve.wait_ge(raw_in, 32 * (plan.p + 1))
                            split_w(1 - plan.p % 2, cols, None)
                            done = w_count[plan.p - 1] + it
                            dve.wait_ge(w_part, 2 * (done + 1))
                            split_w_lo(1 - plan.p % 2, cols)

                    loop(dve, plan, body)



def edge_tables(core, a, tab):
    nc = core.nc
    with ExitStack() as ctx:
        sb, ps = allocator(nc, ctx)
        ints = {n: sb(f"s_{n}_i", [P, w], I32) for n, w in (("src_row", EDGES), ("dst_row", EDGES), ("src_col", EC), ("dst_col", EC))}
        flt = {n: sb(f"s_{n}_f", list(t.shape)) for n, t in ints.items()}
        iota_row, iota_col = sb("s_iota_row", [P, EDGES]), sb("s_iota_col", [P, EC])
        node_col = sb("s_node_col", [P, 1])
        adj = sb("s_adj", [NODES, NODES])
        a_row, a_col = sb("s_a_row", [P, D]), sb("s_a_col", [P, KD])
        w_raw = sb("s_w_raw", [P, 3, KD, D])
        key_row, key_col = sb("s_key_row", [P, EDGES]), sb("s_key_col", [P, EC])
        less, rank = sb("s_less", [P, EC, EDGES]), sb("s_rank", [P, EC])
        perm = sb("s_perm", [P, EC, EDGES])
        spread = sb("s_spread", [P, 2, EC, P])
        s_row, d_row = sb("s_s_row", [P, EDGES]), sb("s_d_row", [P, EDGES])
        oh_s, oh_d = sb("s_oh_s", [P, EDGES]), sb("s_oh_d", [P, EDGES])
        s_col = sb("s_s_col", [P, EC])
        picked = sb("s_picked", [NODES, EDGES])
        ones = sb("s_ones", [NODES, P])
        weight = sb("s_weight", [P, EDGES])
        a_abs = sb("s_a_abs", [P, D])
        prod = sb("s_prod", [P, KD, D])
        wq = sb("s_wq", [P, KD, D])
        wl = sb("s_wl", [P, KD, HEADS])
        pos, neg, sgn = sb("s_pos", [P, KD]), sb("s_neg", [P, KD]), sb("s_sgn", [P, KD])
        pA, pB = ps("s_pA", [P, EDGES]), ps("s_pB", [P, EDGES])
        pC, pD = ps("s_pC", [P, EC, P]), ps("s_pD", [P, EDGES])
        pW = ps("s_pW", [P, EDGES])
        landed, step = core.sem("s_landed"), core.sem("s_step")
        ranked, sorted_mm = core.sem("s_ranked"), core.sem("s_sorted_mm")
        onehot, turned = core.sem("s_onehot"), core.sem("s_turned")
        picked_ready, weight_mm = core.sem("s_picked_ready"), core.sem("s_weight_mm")
        weight_ready = core.sem("s_weight_ready")
        loads = [(ints["src_row"], a["src_row"]), (ints["dst_row"], a["dst_row"]), (ints["src_col"], a["src_col"]),
                 (ints["dst_col"], a["dst_col"]), (iota_row, a["iota_row"]), (iota_col, a["iota_col"]),
                 (node_col, a["node_col"]), (adj, a["adj"]), (a_row, a["a_row"]), (a_col, a["a_col"]),
                 (tab["ident"], a["ident"])]
        with nc.Block() as block:
            @block.sync
            def _(sp):
                for t, src in loads:
                    sp.dma_start(t[:, :], src).then_inc(landed, 16)
                for i, src in enumerate((a["w_lin"], a["w_val"], a["w_out"])):
                    sp.dma_start(w_raw[:, i], src).then_inc(landed, 16)

            @block.vector
            def _(dve):
                link = Chain(dve, step)
                V = nc.vector
                dve.wait_ge(landed, 16 * (len(loads) + 3))
                for n in ints:
                    link(V.tensor_copy(flt[n][:, :], ints[n][:, :]))
                link(V.scalar_tensor_tensor(out=key_row[:, :], in0=flt["src_row"][:, :], scalar=float(EDGES),
                                            in1=iota_row[:, :], op0=ALU.mult, op1=ALU.add))
                link(V.scalar_tensor_tensor(out=key_col[:, :], in0=flt["src_col"][:, :], scalar=float(EDGES),
                                            in1=iota_col[:, :], op0=ALU.mult, op1=ALU.add))
                for c in range(EC):
                    link(V.tensor_scalar(less[:, c, :], key_row[:, :], key_col[:, c:c + 1], None, ALU.is_lt))
                link(V.tensor_reduce(rank[:, :], less[:, :, :], AX.X, ALU.add))
                for c in range(EC):
                    link(V.tensor_scalar(perm[:, c, :], iota_row[:, :], rank[:, c:c + 1], None, ALU.is_equal))
                link(V.tensor_copy(spread[:, 0], flt["src_col"][:, :].unsqueeze(2).to_broadcast([P, EC, P])))
                V.tensor_copy(spread[:, 1], flt["dst_col"][:, :].unsqueeze(2).to_broadcast([P, EC, P])).then_inc(ranked, 1)

                link(V.scalar_tensor_tensor(out=a_abs[:, :], in0=a_row[:, :], scalar=-1.0, in1=a_row[:, :],
                                            op0=ALU.mult, op1=ALU.max))
                for k in range(KD):
                    link(V.scalar_tensor_tensor(out=wq[:, k, :], in0=w_raw[:, 0, k, :], scalar=1.0 - LEAK,
                                                in1=a_abs[:, :], op0=ALU.mult, op1=ALU.mult))
                    link(V.scalar_tensor_tensor(out=prod[:, k, :], in0=w_raw[:, 0, k, :], scalar=LEAK,
                                                in1=a_row[:, :], op0=ALU.mult, op1=ALU.mult))
                link(V.tensor_reduce(wl[:, :, :], prod[:, :, :].rearrange("p k (h d) -> p k h d", h=HEADS), AX.X, ALU.add))
                splits = [(tab["wqv_hi"][:, :, 0:D], tab["wqv_lo"][:, :, 0:D], wq[:, :, :]),
                          (tab["wqv_hi"][:, :, D:2 * D], tab["wqv_lo"][:, :, D:2 * D], w_raw[:, 1]),
                          (tab["wo_hi"][:, :, :], tab["wo_lo"][:, :, :], w_raw[:, 2]),
                          (tab["wl_hi"][:, :, :], tab["wl_lo"][:, :, :], wl[:, :, :])]
                for hi, lo, full in splits:
                    link(V.tensor_copy(hi, full))
                    link(V.tensor_tensor(lo, full, f32(hi), ALU.subtract))
                link(V.tensor_scalar(pos[:, :], a_col[:, :], 0.0, None, ALU.is_gt))
                link(V.tensor_scalar(neg[:, :], a_col[:, :], 0.0, None, ALU.is_lt))
                link(V.tensor_tensor(sgn[:, :], pos[:, :], neg[:, :], ALU.subtract))
                link(V.memset(f32(tab["sign"][:, :, :]), 0.0))
                for k in range(KD):
                    for h in range(2):
                        r, col = slice(h * DH, (h + 1) * DH), P - HEADS + 2 * k + h
                        link(V.tensor_copy(tab["sign"][r, k, col:col + 1], sgn[r, k:k + 1]))

                dve.wait_ge(sorted_mm, 1)
                link(V.tensor_copy(s_row[:, :], pA[:, :]))
                link(V.tensor_copy(d_row[:, :], pB[:, :]))
                link(V.tensor_scalar(oh_s[:, :], s_row[:, :], node_col[:, 0:1], None, ALU.is_equal))
                link(V.tensor_scalar(oh_d[:, :], d_row[:, :], node_col[:, 0:1], None, ALU.is_equal))
                link(V.memset(ones[:, :], 1.0))
                V.tensor_tensor(tab["both"][:, :], oh_s[:, :], oh_d[:, :], ALU.add).then_inc(onehot, 1)
                link(V.tensor_copy(tab["dst"][:, :], oh_d[:, :]))
                for n, at, a0, a1 in (("fwd", 0, 1, 0), ("bwd", EDGES - 1, 0, 1)):
                    link(V.memset(tab["same_" + n][:, at:at + 1], 0.0))
                    w = EDGES - 1
                    link(V.tensor_tensor(tab["same_" + n][:, a0:a0 + w], s_row[:, 1:], s_row[:, 0:w], ALU.is_equal))
                    link(V.tensor_scalar(tab["cut_" + n][:, :], tab["same_" + n][:, :], 1.0, BIG, ALU.subtract, ALU.mult))
                dve.wait_ge(turned, 1)
                V.tensor_tensor(picked[:, :], pD[0:NODES, :], oh_d[0:NODES, :], ALU.mult).then_inc(picked_ready, 1)
                link(V.tensor_copy(s_col[:, :], pC[:, :, 0]))
                for c in range(EC):
                    link(V.tensor_scalar(tab["src"][:, c, :], iota_row[:, 0:NODES], s_col[:, c:c + 1], None, ALU.is_equal))
                dve.wait_ge(weight_mm, 1)
                V.tensor_scalar(weight[:, :], pW[:, :], LOG_EPS, None, ALU.add).then_inc(weight_ready, 1)

            @block.scalar
            def _(act):
                act.wait_ge(weight_ready, 1)
                nc.scalar.activation(tab["log_w"][:, :], weight[:, :], ACT.Ln)

            @block.tensor
            def _(pe):
                pe.wait_ge(ranked, 1)
                for i, out in enumerate((pA, pB)):
                    for c in range(EC):
                        last = nc.tensor.matmul(out[:, :], spread[:, i, c, :], perm[:, c, :], start=c == 0, stop=c == EC - 1)
                last.then_inc(sorted_mm, 1)
                pe.wait_ge(onehot, 1)
                for c in range(EC):
                    nc.tensor.transpose(pC[:, c, :], s_row[:, c * P:(c + 1) * P], tab["ident"][:, :])
                nc.tensor.matmul(pD[0:NODES, :], adj[:, :], oh_s[0:NODES, :], start=True, stop=True).then_inc(turned, 1)
                pe.wait_ge(picked_ready, 1)
                nc.tensor.matmul(pW[:, :], ones[:, :], picked[:, :], start=True, stop=True).then_inc(weight_mm, 1)


def edge_attention(core, x, x2, tab, HT):
    nc = core.nc
    NQ, QG, QT = 4, 32, 16
    GG = GT * TILE_GRAPHS
    NJ = QT // GT
    with ExitStack() as ctx:
        sb, ps = allocator(nc, ctx)
        mhalf = sb("c_mhalf", [P, GT])
        xt = [sb(f"c_xt{b}", [P, GT, D]) for b in range(2)]
        hst = [sb(f"c_hst{b}", [P, KD, GROWS]) for b in range(2)]
        x1 = sb("c_x1", [P, QT, D])
        st, mv, ve, rstd = sb("c_st", [P, GT, 6]), sb("c_mv", [P, GT, 2]), sb("c_ve", [P, GT]), sb("c_rstd", [P, GT])
        hT_hi, hT_lo = sb("c_hThi", [P, KD, GROWS], F32R), sb("c_hTlo", [P, KD, GROWS], F32R)
        S = sb("c_S", [P, GG + QG, D], F32R)
        lin = sb("c_lin", [P, P], F32R)
        r_hi = [sb(f"c_rhi{b}", [P, KD, EDGES], F32R) for b in range(2)]
        r_lo = [sb(f"c_rlo{b}", [P, KD, EDGES], F32R) for b in range(2)]
        work = sb("c_work", [P, 4, EDGES])
        wv = [work[:, 2 * b:2 * b + 2, :].rearrange("p a (c f) -> p (a c) f", f=D) for b in range(2)]
        attn_T = sb("c_attnT", [P, EC, P])
        pT = ps("c_pT", [P, KD, GROWS])
        pZ = [ps(f"c_pZ{b}", [P, KD, EDGES]) for b in range(2)]
        pUE = ps("c_pUE", [P, 2, EDGES])
        pTr = pT[:, :, :].rearrange("p k (a d) -> p (k a) d", d=D)
        pO = pUE[:, :, :].rearrange("p k (a d) -> p (k a) d", d=D)
        pU, pE = pUE[:, 0, :], pUE[:, 1, :]
        names = ("half_set t1 x1_done stats moments var_eps rstd_ready normed t2 h_hi h_lo u_mm s_hi s_lo "
                 "lin_mm lin_part lin_done z_mm r_hi_done r_lo_done e_mm soft exp_done at_mm attn_ready "
                 "vg_mm wv_done y_mm y_hi y_lo o_mm x2_done").split()
        sem = {n: core.sem("c_" + n) for n in names}
        landed = [core.sem(f"c_landed{b}") for b in range(2)]
        stored = [core.sem(f"c_stored{j}") for j in range(NJ)]
        HTg = HT.rearrange("p k (g c) -> p k g c", c=GROWS)

        def slots(gi):
            g8 = gi % GG
            step = GG + gi - g8
            return slice(g8, g8 + step + 1, step)

        with nc.Block() as block:
            @block.sync
            def _(sp):
                def body(q):
                    for j in range(NJ):
                        b, g = j % 2, 4 * q + j
                        wait(sp, sem["normed"], g - 1)
                        wait(sp, sem["t2"], g - 1)
                        sp.dma_start(xt[b][:, :, :], x[g]).then_inc(landed[b], 16)
                        sp.dma_start(hst[b][:, :, :], HTg[:, :, g, :]).then_inc(landed[b], 16)
                    for j in range(NJ):
                        sp.wait_ge(sem["x2_done"], 4 * q + j + 1)
                        sp.dma_start(x2[4 * q + j], x1[:, GT * j:GT * (j + 1), :]).then_inc(stored[j], 16)

                peeled(sp, NQ, body)
                for j in range(NJ):
                    sp.wait_ge(stored[j], 16 * NQ)

            @block.gpsimd
            def _(pool):
                nc.gpsimd.memset(mhalf[:, :], -0.5).then_inc(sem["half_set"], 1)
                pool.wait_ge(sem["half_set"], 1)
                with pool.Fori(0, NG) as g:
                    pool.wait_ge(sem["var_eps"], g + 1)
                    nc.gpsimd.tensor_tensor(rstd[:, :], ve[:, :], mhalf[:, :], ALU.pow).then_inc(sem["rstd_ready"], 1)

            @block.tensor
            def _(pe):
                def turn_back(q, j):
                    g = 4 * q + j
                    pe.wait_ge(landed[j % 2], 32 * (2 * q + j // 2 + 1))
                    wait(pe, sem["lin_done"], g)
                    for t in range(GT):
                        for k in range(KD):
                            last = nc.tensor.transpose(pTr[:, t, k * P:(k + 1) * P],
                                                       hst[j % 2][:, k, t * P:(t + 1) * P], tab["ident"][:, :])
                    last.then_inc(sem["t1"], 1)

                def turn(q, j):
                    pe.wait_ge(sem["normed"], 4 * q + j + 1)
                    xn = hst[j % 2][:, :, :].rearrange("p k (a d) -> p (k a) d", d=D)
                    for t in range(GT):
                        for k in range(KD):
                            last = nc.tensor.transpose(pT[:, k, t * P:(t + 1) * P], xn[:, t, k * P:(k + 1) * P],
                                                       tab["ident"][:, :])
                    last.then_inc(sem["t2"], 1)

                def project(q, j):
                    g = 4 * q + j
                    pe.wait_ge(sem["h_hi"], g + 1)
                    pe.wait_ge(sem["h_lo"], g + 1)
                    for t in range(GT):
                        if t == 0 and j == 0:
                            wait(pe, sem["x2_done"], 4 * q)
                        wait(pe, sem["s_lo"], QT * q + GT * j + t)
                        c = slice(t * P, (t + 1) * P)
                        for k in range(KD):
                            last = mm3(nc, pU, hT_hi[:, k, c], hT_lo[:, k, c], tab["wqv_hi"][:, k, :],
                                       tab["wqv_lo"][:, k, :], k == 0, k == KD - 1)
                        last.then_inc(sem["u_mm"], 1)
                    for i in range(GG):
                        c = slice(i * NODES, (i + 1) * NODES)
                        for k in range(KD):
                            last = mm3(nc, pT[0:NODES, 0, HEADS * i:HEADS * (i + 1)], hT_hi[:, k, c], hT_lo[:, k, c],
                                       tab["wl_hi"][:, k, :], tab["wl_lo"][:, k, :], k == 0, k == KD - 1)
                    last.then_inc(sem["lin_mm"], 1)

                def gather(q, gi):
                    pe.wait_ge(sem["s_lo"], QT * q + gi // 2 + 1)
                    if gi < 2:
                        wait(pe, sem["wv_done"], QG * q)
                    else:
                        pe.wait_ge(sem["r_lo_done"], QG * q + gi - 1)
                    for k in range(KD):
                        last = nc.tensor.matmul(pZ[gi % 2][:, k, :], S[:, gi % GG, k * P:(k + 1) * P], tab["both"][:, :],
                                                start=True, stop=True)
                    last.then_inc(sem["z_mm"], 1)

                def score(q, gi):
                    pe.wait_ge(sem["r_lo_done"], QG * q + gi + 1)
                    pe.wait_ge(sem["r_hi_done"], QG * q + gi + 1)
                    at = P - HEADS - HEADS * gi
                    for k in range(KD):
                        for i, r in enumerate((r_hi, r_lo)):
                            nc.tensor.matmul(pE, tab["sign"][:, k, at:at + P], r[gi % 2][:, k, :],
                                                    start=gi == 0 and k == 0 and i == 0, stop=False)

                def values(q, gi):
                    if gi >= 2:
                        pe.wait_ge(sem["wv_done"], QG * q + gi - 1)
                    vg = pZ[gi % 2][:, :, :].rearrange("p k (a d) -> p (k a) d", d=D)
                    for c in range(EC):
                        last = nc.tensor.matmul(vg[:, c, :], tab["dst"][:, c * P:(c + 1) * P], S[:, GG + gi, :],
                                                start=True, stop=True)
                    last.then_inc(sem["vg_mm"], 1)

                def scatter(q, gi):
                    pe.wait_ge(sem["wv_done"], QG * q + gi + 1)
                    at = (gi % GG) * NODES
                    for k in range(KD):
                        for c in range(EC):
                            last = nc.tensor.matmul(pT[:, k, at:at + NODES], wv[gi % 2][:, c, k * P:(k + 1) * P],
                                                    tab["src"][:, c, :], start=c == 0, stop=c == EC - 1)
                    if gi % GG == GG - 1:
                        last.then_inc(sem["y_mm"], 1)

                def project_out(q, j):
                    g = 4 * q + j
                    pe.wait_ge(sem["y_hi"], g + 1)
                    pe.wait_ge(sem["y_lo"], g + 1)
                    wait(pe, sem["x2_done"], g)
                    for t in range(GT):
                        c = slice(t * P, (t + 1) * P)
                        for k in range(KD):
                            last = mm3(nc, pO[:, t, :], hT_hi[:, k, c], hT_lo[:, k, c], tab["wo_hi"][:, k, :],
                                       tab["wo_lo"][:, k, :], k == 0, k == KD - 1)
                    last.then_inc(sem["o_mm"], 1)

                def body(q):
                    turn_back(q, 0)
                    turn(q, 0)
                    project(q, 0)
                    for j in range(NJ):
                        for i in range(GG):
                            if j + 1 < NJ and i == 0:
                                turn_back(q, j + 1)
                            if j + 1 < NJ and i == GG // 2:
                                turn(q, j + 1)
                            gather(q, GG * j + i)
                            if i:
                                score(q, GG * j + i - 1)
                        score(q, GG * j + GG - 1)
                        if j + 1 < NJ:
                            project(q, j + 1)
                    pe.wait_ge(sem["lin_done"], 4 * q + 4)
                    nc.tensor.matmul(pE, lin[:, :], tab["both"][:, :], start=False, stop=True).then_inc(sem["e_mm"], 1)
                    values(q, 0)
                    values(q, 1)
                    pe.wait_ge(sem["soft"], 8 * q + 8)
                    for c in range(EC):
                        last = nc.tensor.transpose(pT[:, 0, c * P:(c + 1) * P], work[:, 0, c * P:(c + 1) * P], tab["ident"][:, :])
                    last.then_inc(sem["at_mm"], 1)
                    for gi in range(QG):
                        if gi >= 1 and gi + 1 < QG:
                            values(q, gi + 1)
                        scatter(q, gi)
                        if gi % GG == GG - 1:
                            project_out(q, gi // GG)

                peeled(pe, NQ, body)

            @block.scalar
            def _(act):
                def hi_halves(q, j):
                    act.wait_ge(sem["t2"], 4 * q + j + 1)
                    nc.scalar.activation(hT_hi[:, :, :], pT[:, :, :], ACT.Relu).then_inc(sem["h_hi"], 1)

                def split_hi(q, j):
                    for t in range(GT):
                        gi = GG * j + 2 * t
                        act.wait_ge(sem["u_mm"], QT * q + GT * j + t + 1)
                        for i, r in enumerate((slice(0, NODES), slice(NODES, P))):
                            nc.scalar.activation(S[r, slots(gi + i), :], pU[r, :].rearrange("p (a d) -> p a d", d=D),
                                                 ACT.Copy).then_inc(sem["s_hi"], 1)

                def relu(q, gi):
                    act.wait_ge(sem["z_mm"], QG * q + gi + 1)
                    nc.scalar.activation(r_hi[gi % 2][:, :, :], pZ[gi % 2][:, :, :], ACT.Relu).then_inc(sem["r_hi_done"], 1)

                def body(q):
                    hi_halves(q, 0)
                    split_hi(q, 0)
                    for j in range(NJ):
                        for i in range(GG):
                            relu(q, GG * j + i)
                            if i == GG // 2 - 1 and j + 1 < NJ:
                                hi_halves(q, j + 1)
                        if j + 1 < NJ:
                            split_hi(q, j + 1)
                    act.wait_ge(sem["soft"], 8 * q + 4)
                    nc.scalar.activation(work[:, 1, :], work[:, 0, :], ACT.Exp).then_inc(sem["exp_done"], 1)
                    act.wait_ge(sem["at_mm"], q + 1)
                    wait(act, sem["wv_done"], QG * q)
                    nc.scalar.activation(attn_T[:, :, :], pT[:, 0, :].rearrange("p (c r) -> p c r", c=EC), ACT.Copy)\
                        .then_inc(sem["attn_ready"], 1)
                    for j in range(NJ):
                        act.wait_ge(sem["y_mm"], 4 * q + j + 1)
                        nc.scalar.activation(hT_hi[:, :, :], pT[:, :, :], ACT.Copy).then_inc(sem["y_hi"], 1)

                peeled(act, NQ, body)

            @block.vector
            def _(dve):
                V = nc.vector

                def add_x(q, j):
                    g = 4 * q + j
                    dve.wait_ge(sem["t1"], g + 1)
                    wait(dve, stored[j], 16 * q)
                    V.tensor_tensor(x1[:, GT * j:GT * (j + 1), :], pTr, xt[j % 2][:, :, :], ALU.add).then_inc(sem["x1_done"], 1)
                    dve.wait_ge(sem["x1_done"], g + 1)
                    for t in range(GT):
                        last = V.bn_stats(st[:, t, :], x1[:, GT * j + t, :])
                    last.then_inc(sem["stats"], 1)
                    dve.wait_ge(sem["stats"], g + 1)
                    wait(dve, sem["rstd_ready"], g)
                    V.memset(ve[:, :], EPS)
                    for t in range(GT):
                        last = V.bn_aggr(mv[:, t, :], st[:, t, :])
                    last.then_inc(sem["moments"], 1)
                    dve.wait_ge(sem["moments"], g + 1)
                    V.tensor_tensor(ve[:, :], ve[:, :], mv[:, :, 1], ALU.add).then_inc(sem["var_eps"], 1)

                def normalise(q, j):
                    g = 4 * q + j
                    dve.wait_ge(sem["rstd_ready"], g + 1)
                    xn = hst[j % 2][:, :, :].rearrange("p k (a d) -> p (k a) d", d=D)
                    for t in range(GT):
                        last = V.tensor_scalar(xn[:, t, :], x1[:, GT * j + t, :], mv[:, t, 0:1], rstd[:, t:t + 1],
                                               ALU.subtract, ALU.mult)
                    last.then_inc(sem["normed"], 1)

                def lo_halves(q, j):
                    dve.wait_ge(sem["h_hi"], 4 * q + j + 1)
                    V.scalar_tensor_tensor(out=hT_lo[:, :, :], in0=pT[:, :, :], scalar=0.0, in1=f32(hT_hi[:, :, :]),
                                           op0=ALU.max, op1=ALU.subtract).then_inc(sem["h_lo"], 1)

                def split_lo(q, j):
                    halves = (slice(0, NODES), slice(NODES, P))
                    for t in range(GT):
                        gi = GG * j + 2 * t
                        dve.wait_ge(sem["s_hi"], 2 * (QT * q + GT * j + t + 1))
                        for i in range(2):
                            last = V.tensor_tensor(S[halves[1 - i], slots(gi + i), :],
                                                   pU[halves[i], :].rearrange("p (a d) -> p a d", d=D),
                                                   f32(S[halves[i], slots(gi + i), :]), ALU.subtract)
                        last.then_inc(sem["s_lo"], 1)
                    g, cols = 4 * q + j, slice(GG * HEADS * j, GG * HEADS * (j + 1))
                    dve.wait_ge(sem["lin_mm"], g + 1)
                    part = pT[0:NODES, 0, 0:GG * HEADS]
                    V.tensor_copy(lin[0:NODES, cols], part).then_inc(sem["lin_part"], 1)
                    dve.wait_ge(sem["lin_part"], g + 1)
                    V.tensor_tensor(lin[NODES:P, cols], part, f32(lin[0:NODES, cols]), ALU.subtract).then_inc(sem["lin_done"], 1)

                def relu_lo(q, gi):
                    dve.wait_ge(sem["r_hi_done"], QG * q + gi + 1)
                    V.scalar_tensor_tensor(out=r_lo[gi % 2][:, :, :], in0=pZ[gi % 2][:, :, :], scalar=0.0,
                                           in1=f32(r_hi[gi % 2][:, :, :]), op0=ALU.max,
                                           op1=ALU.subtract).then_inc(sem["r_lo_done"], 1)

                def softmax(q):
                    w = [work[:, i, :] for i in range(4)]
                    n = [0]

                    def step(ins):
                        n[0] += 1
                        ins.then_inc(sem["soft"], 1)
                        dve.wait_ge(sem["soft"], 8 * q + n[0])

                    dve.wait_ge(sem["e_mm"], q + 1)
                    step(V.tensor_tensor(w[0], pE, tab["log_w"][:, :], ALU.add))
                    step(V.tensor_tensor_scan(w[1], tab["cut_fwd"][:, :], w[0], 0.0, ALU.add, ALU.max))
                    step(V.tensor_tensor_scan(w[2][:, ::-1], tab["cut_bwd"][:, ::-1], w[1][:, ::-1], 0.0, ALU.add, ALU.max))
                    step(V.tensor_tensor(w[0], w[0], w[2], ALU.subtract))
                    dve.wait_ge(sem["exp_done"], q + 1)
                    step(V.tensor_tensor_scan(w[2], tab["same_fwd"][:, :], w[1], 0.0, ALU.mult, ALU.add))
                    step(V.tensor_tensor_scan(w[3][:, ::-1], tab["same_bwd"][:, ::-1], w[2][:, ::-1], 0.0, ALU.mult, ALU.max))
                    step(V.reciprocal(w[2], w[3]))
                    step(V.tensor_tensor(w[0], w[1], w[2], ALU.mult))

                def weigh(q, gi):
                    dve.wait_ge(sem["vg_mm"], QG * q + gi + 1)
                    if gi == 0:
                        dve.wait_ge(sem["attn_ready"], q + 1)
                    shape = [P, EC, HEADS, DH]
                    V.tensor_tensor(wv[gi % 2].rearrange("p c (h d) -> p c h d", h=HEADS),
                                    pZ[gi % 2][:, :, :].rearrange("p k (a h d) -> p (k a) h d", h=HEADS, d=DH),
                                    attn_T[:, :, HEADS * gi:HEADS * (gi + 1)].unsqueeze(3).to_broadcast(shape),
                                    ALU.mult).then_inc(sem["wv_done"], 1)

                def body(q):
                    add_x(q, 0)
                    normalise(q, 0)
                    lo_halves(q, 0)
                    split_lo(q, 0)
                    for j in range(NJ):
                        more = j + 1 < NJ
                        if more:
                            add_x(q, j + 1)
                        for i in range(GG):
                            relu_lo(q, GG * j + i)
                            if more and i == 1:
                                normalise(q, j + 1)
                            if more and i == GG // 2:
                                lo_halves(q, j + 1)
                        if more:
                            split_lo(q, j + 1)
                    softmax(q)
                    for j in range(NJ):
                        for i in range(GG):
                            weigh(q, GG * j + i)
                        g = 4 * q + j
                        dve.wait_ge(sem["y_hi"], g + 1)
                        V.tensor_tensor(hT_lo[:, :, :], pT[:, :, :], f32(hT_hi[:, :, :]), ALU.subtract).then_inc(sem["y_lo"], 1)
                        dve.wait_ge(sem["o_mm"], g + 1)
                        part = x1[:, GT * j:GT * (j + 1), :]
                        V.tensor_tensor(part, pO, part, ALU.add).then_inc(sem["x2_done"], 1)

                peeled(dve, NQ, body)


def attention_layer(core, a, x, x2, HT):
    with ExitStack() as ctx:
        sb, _ = allocator(core.nc, ctx)
        tab = {"ident": sb("t_ident", [P, P]), "both": sb("t_both", [P, EDGES], F32R), "dst": sb("t_dst", [P, EDGES], F32R),
               "src": sb("t_src", [P, EC, NODES]), "sign": sb("t_sign", [P, KD, 2 * P - HEADS], F32R),
               "log_w": sb("t_log_w", [P, EDGES]),
               "wqv_hi": sb("t_wqv_hi", [P, KD, 2 * D], F32R), "wqv_lo": sb("t_wqv_lo", [P, KD, 2 * D], F32R),
               "wo_hi": sb("t_wo_hi", [P, KD, D], F32R), "wo_lo": sb("t_wo_lo", [P, KD, D], F32R),
               "wl_hi": sb("t_wl_hi", [P, KD, HEADS], F32R), "wl_lo": sb("t_wl_lo", [P, KD, HEADS], F32R)}
        for n in ("same_fwd", "same_bwd", "cut_fwd", "cut_bwd"):
            tab[n] = sb("t_" + n, [P, EDGES])
        edge_tables(core, a, tab)
        edge_attention(core, x, x2, tab, HT)


def conv_first(core, a, x2, H1, st1, W2):
    nc = core.nc
    NI = NG // 2
    with ExitStack() as ctx:
        sb, ps = allocator(nc, ctx)
        mhalf = sb("d_mhalf", [P, GT])
        an_t, an = sb("d_an_t", [NODES, NODES]), sb("d_an", [NODES, NODES])
        eye = sb("d_eye", [P, P])
        both, diag = sb("d_both", [NODES, NODES]), sb("d_diag", [NODES, NODES])
        ones = sb("d_ones", [NODES, P])
        deg, dinv, dcol = sb("d_deg", [P, NODES]), sb("d_dinv", [P, NODES]), sb("d_dcol", [P, 1])
        pick = sb("d_pick", [P, NODES])
        hat = sb("d_hat", [P, P])
        an_t2 = sb("d_an_t2", [P, NODES])
        eye2 = sb("d_eye2", [P, NODES])
        hat_hi, hat_lo = sb("d_hat_hi", [P, P], F32R), sb("d_hat_lo", [P, P], F32R)
        w1 = sb("d_w1", [P, KD, HID2])
        w1_hi, w1_lo = sb("d_w1_hi", [P, KD, HID2], F32R), sb("d_w1_lo", [P, KD, HID2], F32R)
        w2 = sb("d_w2", [P, KH, D])
        b1 = sb("d_b1", [P, KH])
        xt = [sb(f"d_xt{b}", [P, GT, D]) for b in range(2)]
        st, mv, ve, rstd = sb("d_st", [P, GT, 6]), sb("d_mv", [P, GT, 2]), sb("d_ve", [P, GT]), sb("d_rstd", [P, GT])
        h_hi = [sb(f"d_hhi{b}", [P, GT, D], F32R) for b in range(2)]
        h_lo = [sb(f"d_hlo{b}", [P, GT, D], F32R) for b in range(2)]
        g_hi = [sb(f"d_ghi{b}", [P, KD, GROWS], F32R) for b in range(2)]
        g_lo = [sb(f"d_glo{b}", [P, KD, GROWS], F32R) for b in range(2)]
        pA = [ps(f"d_pA{b}", [P, KD, GROWS]) for b in range(2)]
        pW = ps("d_pW", [P, KH, GROWS])
        names = ("consts half_set step deg_ready deg_mm root_ready hat_ready stats moments var_eps rstd_ready normed "
                 "h_hi_done h_lo_done agg_mm g_hi_done g_lo_done w1_mm h1_done").split()
        sem = {n: core.sem("d_" + n) for n in names}
        landed = [core.sem(f"d_landed{b}") for b in range(2)]
        loads = [(eye[:, :], a["ident"]), (an_t[:, :], a["adj_t"]), (an[:, :], a["adj"]), (w1[:, :, :], a["w1"]),
                 (w2[:, :, :], a["w2"]), (b1[:, :], a["b1"])]
        for g in range(TILE_GRAPHS):
            r = slice(g * NODES, (g + 1) * NODES)
            loads += [(an_t2[r, :], a["adj_t"]), (eye2[r, :], a["ident"][0:NODES, 0:NODES])]
        H1g = H1.rearrange("p k (g c) -> p k g c", c=GROWS)

        with nc.Block() as block:
            @block.sync
            def _(sp):
                for t, src in loads:
                    sp.dma_start(t, src).then_inc(sem["consts"], 16)

                def body(it):
                    for b in range(2):
                        wait(sp, sem["h_lo_done"], 2 * it + b - 1)
                        sp.dma_start(xt[b][:, :, :], x2[2 * it + b]).then_inc(landed[b], 16)

                peeled(sp, NI, body)

            @block.gpsimd
            def _(pool):
                nc.gpsimd.memset(mhalf[:, :], -0.5).then_inc(sem["half_set"], 1)
                pool.wait_ge(sem["half_set"], 1)
                pool.wait_ge(sem["deg_ready"], 1)
                nc.gpsimd.tensor_tensor(dinv[:, :], deg[:, :], mhalf[:, 0:1].to_broadcast([P, NODES]), ALU.pow)\
                    .then_inc(sem["root_ready"], 1)
                with pool.Fori(0, NG) as g:
                    pool.wait_ge(sem["var_eps"], g + 1)
                    nc.gpsimd.tensor_tensor(rstd[:, :], ve[:, :], mhalf[:, :], ALU.pow).then_inc(sem["rstd_ready"], 1)

            @block.tensor
            def _(pe):
                pe.wait_ge(sem["step"], 6)
                nc.tensor.matmul(pA[0][:, 0, 0:NODES], ones[:, :], both[:, :], start=True, stop=True).then_inc(sem["deg_mm"], 1)
                pe.wait_ge(sem["hat_ready"], 1)

                def aggregate(g, b):
                    pe.wait_ge(sem["h_lo_done"], g + 1)
                    pe.wait_ge(sem["h_hi_done"], g + 1)
                    for k in range(KD):
                        c = slice(k * P, (k + 1) * P)
                        for t in range(GT):
                            last = mm3(nc, pA[b][:, k, t * P:(t + 1) * P], h_hi[b][:, t, c], h_lo[b][:, t, c],
                                       hat_hi[:, :], hat_lo[:, :], True, True)
                    last.then_inc(sem["agg_mm"], 1)

                def first(g, b):
                    pe.wait_ge(sem["g_hi_done"], g + 1)
                    pe.wait_ge(sem["g_lo_done"], g + 1)
                    for m in range(KH):
                        wait(pe, sem["h1_done"], KH * (g - 1) + m + 1)
                        c = slice(m * P, (m + 1) * P)
                        for k in range(KD):
                            last = mm3(nc, pW[:, m, :], w1_hi[:, k, c], w1_lo[:, k, c], g_hi[b][:, k, :], g_lo[b][:, k, :],
                                       k == 0, k == KD - 1)
                        last.then_inc(sem["w1_mm"], 1)

                def body(it):
                    for b in range(2):
                        g = 2 * it + b
                        aggregate(g, b)
                        if not (isinstance(g, int) and g == 0):
                            first(g - 1, 1 - b)

                peeled(pe, NI, body)
                first(NG - 1, 1)

            @block.scalar
            def _(act):
                act.wait_ge(sem["consts"], 16 * len(loads))

                def keep(g):
                    for m in range(KH):
                        act.wait_ge(sem["w1_mm"], KH * g + m + 1)
                        nc.scalar.activation(H1g[:, m, g, :], pW[:, m, :], ACT.Identity, bias=b1[:, m:m + 1])\
                            .then_inc(sem["h1_done"], 1)

                def body(it):
                    for b in range(2):
                        g = 2 * it + b
                        act.wait_ge(sem["normed"], g + 1)
                        wait(act, sem["agg_mm"], g - 1)
                        nc.scalar.activation(h_hi[b][:, :, :], xt[b][:, :, :], ACT.Relu).then_inc(sem["h_hi_done"], 1)
                        act.wait_ge(sem["agg_mm"], g + 1)
                        nc.scalar.activation(g_hi[b][:, :, :], pA[b][:, :, :], ACT.Copy).then_inc(sem["g_hi_done"], 1)
                        if not (isinstance(g, int) and g == 0):
                            keep(g - 1)

                peeled(act, NI, body)
                keep(NG - 1)

            @block.vector
            def _(dve):
                V = nc.vector
                link = Chain(dve, sem["step"])
                dve.wait_ge(sem["consts"], 16 * len(loads))
                link(V.tensor_tensor(an_t[:, :], an_t[:, :], eye[0:NODES, 0:NODES], ALU.add))
                link(V.tensor_tensor(an[:, :], an[:, :], eye[0:NODES, 0:NODES], ALU.add))
                link(V.tensor_tensor(diag[:, :], an[:, :], eye[0:NODES, 0:NODES], ALU.mult))
                link(V.tensor_tensor(both[:, :], an[:, :], an_t[:, :], ALU.add))
                link(V.tensor_tensor(both[:, :], both[:, :], diag[:, :], ALU.subtract))
                link(V.memset(ones[:, :], 1.0))
                for raw, hi, lo in ((w1, w1_hi, w1_lo), (w2, W2[0], W2[1])):
                    link(V.tensor_copy(hi[:, :, :], raw[:, :, :]))
                    link(V.tensor_tensor(lo[:, :, :], raw[:, :, :], f32(hi[:, :, :]), ALU.subtract))
                dve.wait_ge(sem["deg_mm"], 1)
                V.tensor_copy(deg[:, :], pA[0][:, 0, 0:NODES]).then_inc(sem["deg_ready"], 1)
                dve.wait_ge(sem["root_ready"], 1)
                link(V.tensor_tensor(pick[:, :], dinv[:, :], eye2[:, :], ALU.mult))
                link(V.tensor_reduce(dcol[:, :], pick[:, :], AX.X, ALU.add))
                link(V.tensor_tensor(an_t2[:, :], an_t2[:, :], eye2[:, :], ALU.add))
                link(V.memset(hat[:, :], 0.0))
                for g in range(TILE_GRAPHS):
                    r = slice(g * NODES, (g + 1) * NODES)
                    link(V.scalar_tensor_tensor(out=hat[r, r], in0=an_t2[r, :], scalar=dcol[r, 0:1], in1=dinv[r, :],
                                                op0=ALU.mult, op1=ALU.mult))
                link(V.tensor_copy(hat_hi[:, :], hat[:, :]))
                V.tensor_tensor(hat_lo[:, :], hat[:, :], f32(hat_hi[:, :]), ALU.subtract).then_inc(sem["hat_ready"], 1)

                def norm(g, b):
                    dve.wait_ge(landed[b], 8 * (g - b) + 16)
                    for t in range(GT):
                        last = V.bn_stats(st[:, t, :], xt[b][:, t, :])
                    last.then_inc(sem["stats"], 1)
                    dve.wait_ge(sem["stats"], g + 1)
                    wait(dve, sem["rstd_ready"], g)
                    V.memset(ve[:, :], EPS)
                    for t in range(GT):
                        last = V.bn_aggr(mv[:, t, :], st[:, t, :])
                    last.then_inc(sem["moments"], 1)
                    dve.wait_ge(sem["moments"], g + 1)
                    V.tensor_tensor(ve[:, :], ve[:, :], mv[:, :, 1], ALU.add).then_inc(sem["var_eps"], 1)
                    dve.wait_ge(sem["rstd_ready"], g + 1)
                    for t in range(GT):
                        last = V.tensor_scalar(xt[b][:, t, :], xt[b][:, t, :], mv[:, t, 0:1], rstd[:, t:t + 1],
                                               ALU.subtract, ALU.mult)
                    last.then_inc(sem["normed"], 1)
                    dve.wait_ge(sem["h_hi_done"], g + 1)
                    V.scalar_tensor_tensor(out=h_lo[b][:, :, :], in0=xt[b][:, :, :], scalar=0.0, in1=f32(h_hi[b][:, :, :]),
                                           op0=ALU.max, op1=ALU.subtract).then_inc(sem["h_lo_done"], 1)

                def measure(g):
                    for m in range(KH):
                        dve.wait_ge(sem["h1_done"], KH * g + m + 1)
                        V.bn_stats(st1[:, m, g, :], H1g[:, m, g, :])

                norm(0, 0)

                def body(it):
                    for b in range(2):
                        g = 2 * it + b
                        end = isinstance(g, int) and g == NG - 1
                        dve.wait_ge(sem["g_hi_done"], g + 1)
                        V.tensor_tensor(g_lo[b][:, :, :], pA[b][:, :, :], f32(g_hi[b][:, :, :]), ALU.subtract)\
                            .then_inc(sem["g_lo_done"], 1)
                        if not end:
                            norm(g + 1, 1 - b)
                        if not (isinstance(g, int) and g == 0):
                            measure(g - 1)

                both_ends(dve, NI, body)
                measure(NG - 1)


def conv_second(core, a, H1, st1, st2, W2):
    nc = core.nc
    NI = NG // 2
    with ExitStack() as ctx:
        sb, ps = allocator(nc, ctx)
        mhalf = sb("f_mhalf", [P, KH])
        g1, be1, b2 = sb("f_g1", [P, KH]), sb("f_be1", [P, KH]), sb("f_b2", [P, KD])
        mv, ve, rstd = sb("f_mv", [P, KH, 2]), sb("f_ve", [P, KH]), sb("f_rstd", [P, KH])
        scale, shift, moved = sb("f_scale", [P, KH]), sb("f_shift", [P, KH]), sb("f_moved", [P, KH])
        r = [sb(f"f_r{b}", [P, KH, GROWS]) for b in range(2)]
        r_hi = [sb(f"f_rhi{b}", [P, KH, GROWS], F32R) for b in range(2)]
        r_lo = [sb(f"f_rlo{b}", [P, KH, GROWS], F32R) for b in range(2)]
        pO = [ps(f"f_pO{b}", [P, KD, GROWS]) for b in range(2)]
        names = "consts half_set step ve_ready rstd_ready affine_ready relu_done hi_done lo_done o_mm o_done".split()
        sem = {n: core.sem("f_" + n) for n in names}
        H1g = H1.rearrange("p k (g c) -> p k g c", c=GROWS)
        loads = [(g1, a["g1"]), (be1, a["be1"]), (b2, a["b2"])]
        with nc.Block() as block:
            @block.sync
            def _(sp):
                for t, src in loads:
                    sp.dma_start(t[:, :], src).then_inc(sem["consts"], 16)

            @block.gpsimd
            def _(pool):
                nc.gpsimd.memset(mhalf[:, :], -0.5).then_inc(sem["half_set"], 1)
                pool.wait_ge(sem["half_set"], 1)
                pool.wait_ge(sem["ve_ready"], 1)
                nc.gpsimd.tensor_tensor(rstd[:, :], ve[:, :], mhalf[:, :], ALU.pow).then_inc(sem["rstd_ready"], 1)

            @block.vector
            def _(dve):
                V = nc.vector
                link = Chain(dve, sem["step"])
                dve.wait_ge(sem["consts"], 16 * len(loads))
                for m in range(KH):
                    link(V.bn_aggr(mv[:, m, :], st1[:, m, :, :].rearrange("p g s -> p (g s)")))
                V.tensor_scalar(ve[:, :], mv[:, :, 1], EPS, None, ALU.add).then_inc(sem["ve_ready"], 1)
                dve.wait_ge(sem["rstd_ready"], 1)
                link(V.tensor_tensor(scale[:, :], g1[:, :], rstd[:, :], ALU.mult))
                link(V.tensor_tensor(moved[:, :], mv[:, :, 0], scale[:, :], ALU.mult))
                V.tensor_tensor(shift[:, :], be1[:, :], moved[:, :], ALU.subtract).then_inc(sem["affine_ready"], 1)

                def split(g, b):
                    dve.wait_ge(sem["relu_done"], g + 1)
                    wait(dve, sem["o_mm"], g - 1)
                    V.tensor_copy(r_hi[b][:, :, :], r[b][:, :, :]).then_inc(sem["hi_done"], 1)
                    dve.wait_ge(sem["hi_done"], g + 1)
                    V.tensor_tensor(r_lo[b][:, :, :], r[b][:, :, :], f32(r_hi[b][:, :, :]), ALU.subtract)\
                        .then_inc(sem["lo_done"], 1)

                def measure(g, b):
                    dve.wait_ge(sem["o_mm"], g + 1)
                    for m in range(KD):
                        last = V.tensor_scalar(H1g[:, m, g, :], pO[b][:, m, :], b2[:, m:m + 1], None, ALU.add)
                    last.then_inc(sem["o_done"], 1)
                    dve.wait_ge(sem["o_done"], g + 1)
                    for m in range(KD):
                        V.bn_stats(st2[:, m, g, :], H1g[:, m, g, :])

                split(0, 0)

                def body(it):
                    for b in range(2):
                        g = 2 * it + b
                        if not (isinstance(g, int) and g == NG - 1):
                            split(g + 1, 1 - b)
                        measure(g, b)

                both_ends(dve, NI, body)

            @block.scalar
            def _(act):
                act.wait_ge(sem["affine_ready"], 1)

                def relu(g, b):
                    wait(act, sem["lo_done"], g - 1)
                    for m in range(KH):
                        last = nc.scalar.activation(r[b][:, m, :], H1g[:, m, g, :], ACT.Relu, bias=shift[:, m:m + 1],
                                                    scale=scale[:, m:m + 1])
                    last.then_inc(sem["relu_done"], 1)

                relu(0, 0)

                def body(it):
                    for b in range(2):
                        g = 2 * it + b
                        if not (isinstance(g, int) and g == NG - 1):
                            relu(g + 1, 1 - b)

                both_ends(act, NI, body)

            @block.tensor
            def _(pe):
                def body(it):
                    for b in range(2):
                        g = 2 * it + b
                        pe.wait_ge(sem["lo_done"], g + 1)
                        wait(pe, sem["o_done"], g - 1)
                        for m in range(KD):
                            c = slice(m * P, (m + 1) * P)
                            for k in range(KH):
                                last = mm3(nc, pO[b][:, m, :], W2[0][:, k, c], W2[1][:, k, c], r_hi[b][:, k, :],
                                           r_lo[b][:, k, :], k == 0, k == KH - 1)
                        last.then_inc(sem["o_mm"], 1)

                peeled(pe, NI, body)


def dense_attention(core, a, x2, out, H1, st2):
    nc = core.nc
    NI = NG // 2
    WE = D + 2
    with ExitStack() as ctx:
        sb, ps = allocator(nc, ctx)
        mhalf = sb("e_mhalf", [P, GT])
        ident = sb("e_ident", [P, P])
        g2, be2 = sb("e_g2", [P, KD]), sb("e_be2", [P, KD])
        mv2, ve2, rstd2 = sb("e_mv2", [P, KD, 2]), sb("e_ve2", [P, KD]), sb("e_rstd2", [P, KD])
        scale, shift, moved = sb("e_scale", [P, KD]), sb("e_shift", [P, KD]), sb("e_moved", [P, KD])
        w_ext = sb("e_w_ext", [P, KD, WE])
        w_hi, w_lo = sb("e_w_hi", [P, KD, WE], F32R), sb("e_w_lo", [P, KD, WE], F32R)
        a_hi, a_lo = sb("e_a_hi", [P, KD, P], F32R), sb("e_a_lo", [P, KD, P], F32R)
        a_row = sb("e_a_row", [P, 2, D])
        prod = sb("e_prod", [P, KD, 2, D])
        adj2, mask = sb("e_adj2", [P, NODES]), sb("e_mask", [P, NODES])
        y = sb("e_y", [P, KD, GROWS])
        xt = [sb(f"e_xt{b}", [P, GT, D]) for b in range(2)]
        xn = sb("e_xn", [P, GT, D])
        st, mv, ve, rstd = sb("e_st", [P, GT, 6]), sb("e_mv", [P, GT, 2]), sb("e_ve", [P, GT]), sb("e_rstd", [P, GT])
        hT_hi, hT_lo = sb("e_hThi", [P, KD, GROWS], F32R), sb("e_hTlo", [P, KD, GROWS], F32R)
        v_hi, v_lo = sb("e_vhi", [P, GT, D], F32R), sb("e_vlo", [P, GT, D], F32R)
        s1 = sb("e_s1", [P, GT])
        e = sb("e_e", [P, GT, NODES])
        top, total, inv = sb("e_top", [P, GT]), sb("e_total", [P, GT]), sb("e_inv", [P, GT])
        prob = sb("e_prob", [P, GT, P])
        p_hi, p_lo = sb("e_phi", [P, GT, P], F32R), sb("e_plo", [P, GT, P], F32R)
        pT = ps("e_pT", [P, KD, GROWS])
        pW = ps("e_pW", [P, GT, GROWS])
        pS = ps("e_pS", [P, GT, P])
        pTr = pT[:, :, :].rearrange("p k (a d) -> p (k a) d", d=D)
        pO = pW[:, 0:2, :].rearrange("p k (a d) -> p (k a) d", d=D)
        names = ("consts half_set step ve2_ready rstd2_ready ready y_done t1 x3_done stats moments var_eps "
                 "rstd_ready normed t2 h_hi h_lo w_mm s_mm v_hi_done soft exp_done prob_done t3 p_hi_done "
                 "p_lo_done o_mm out_done").split()
        sem = {n: core.sem("e_" + n) for n in names}
        landed = [core.sem(f"e_landed{b}") for b in range(2)]
        stored = [core.sem(f"e_stored{b}") for b in range(2)]
        H1g = H1.rearrange("p k (g c) -> p k g c", c=GROWS)
        loads = [(ident[:, :], a["ident"]), (g2[:, :], a["g2"]), (be2[:, :], a["be2"]), (w_ext[:, :, 0:D], a["w3"]),
                 (a_row[:, :, :], a["a3"].rearrange("p (h d) -> p h d", h=2))]
        for g in range(TILE_GRAPHS):
            loads.append((adj2[g * NODES:(g + 1) * NODES, :], a["adj"]))
        SOFT = 9

        with nc.Block() as block:
            @block.sync
            def _(sp):
                for t, src in loads:
                    sp.dma_start(t, src).then_inc(sem["consts"], 16)

                for b in range(2):
                    sp.dma_start(xt[b][:, :, :], x2[b]).then_inc(landed[b], 16)

                def body(it):
                    for b in range(2):
                        g = 2 * it + b
                        sp.wait_ge(sem["out_done"], g + 1)
                        sp.dma_start(out[g], xt[b][:, :, :]).then_inc(stored[b], 16)
                        if not (isinstance(it, int) and it == NI - 1):
                            sp.wait_ge(stored[b], 16 * it + 16)
                            sp.dma_start(xt[b][:, :, :], x2[g + 2]).then_inc(landed[b], 16)

                both_ends(sp, NI, body)
                for b in range(2):
                    sp.wait_ge(stored[b], 16 * NI)

            @block.gpsimd
            def _(pool):
                nc.gpsimd.memset(mhalf[:, :], -0.5).then_inc(sem["half_set"], 1)
                pool.wait_ge(sem["half_set"], 1)
                pool.wait_ge(sem["ve2_ready"], 1)
                nc.gpsimd.tensor_tensor(rstd2[:, :], ve2[:, :], mhalf[:, 0:KD], ALU.pow).then_inc(sem["rstd2_ready"], 1)
                with pool.Fori(0, NG) as g:
                    pool.wait_ge(sem["var_eps"], g + 1)
                    nc.gpsimd.tensor_tensor(rstd[:, :], ve[:, :], mhalf[:, :], ALU.pow).then_inc(sem["rstd_ready"], 1)

            @block.tensor
            def _(pe):
                def rows(g):
                    pe.wait_ge(sem["y_done"], g + 1)
                    for t in range(GT):
                        for k in range(KD):
                            last = nc.tensor.transpose(pTr[:, t, k * P:(k + 1) * P], y[:, k, t * P:(t + 1) * P], ident[:, :])
                    last.then_inc(sem["t1"], 1)
                    pe.wait_ge(sem["normed"], g + 1)
                    for t in range(GT):
                        for k in range(KD):
                            last = nc.tensor.transpose(pT[:, k, t * P:(t + 1) * P], xn[:, t, k * P:(k + 1) * P], ident[:, :])
                    last.then_inc(sem["t2"], 1)

                def project(g):
                    pe.wait_ge(sem["h_lo"], g + 1)
                    pe.wait_ge(sem["h_hi"], g + 1)
                    wait(pe, sem["out_done"], g)
                    for t in range(GT):
                        c = slice(t * P, (t + 1) * P)
                        for k in range(KD):
                            last = mm3(nc, pW[:, t, 0:WE], hT_hi[:, k, c], hT_lo[:, k, c], w_hi[:, k, :], w_lo[:, k, :],
                                       k == 0, k == KD - 1)
                    last.then_inc(sem["w_mm"], 1)
                    for k in range(KD):
                        last = mm3(nc, pS[:, :, :].rearrange("p t r -> p (t r)"), a_hi[:, k, :], a_lo[:, k, :],
                                   hT_hi[:, k, :], hT_lo[:, k, :], k == 0, k == KD - 1)
                    last.then_inc(sem["s_mm"], 1)

                def attend(g):
                    pe.wait_ge(sem["prob_done"], g + 1)
                    for t in range(GT):
                        last = nc.tensor.transpose(pT[:, 0, t * P:(t + 1) * P], prob[:, t, :], ident[:, :])
                    last.then_inc(sem["t3"], 1)
                    pe.wait_ge(sem["p_hi_done"], g + 1)
                    pe.wait_ge(sem["p_lo_done"], g + 1)
                    for t in range(GT):
                        last = mm3(nc, pO[:, t, :], p_hi[:, t, :], p_lo[:, t, :], v_hi[:, t, :], v_lo[:, t, :], True, True)
                    last.then_inc(sem["o_mm"], 1)

                pe.wait_ge(sem["consts"], 16 * len(loads))
                rows(0)
                pe.wait_ge(sem["ready"], 1)

                def body(it):
                    for b in range(2):
                        g = 2 * it + b
                        project(g)
                        if not (isinstance(g, int) and g == NG - 1):
                            rows(g + 1)
                            pe.wait_ge(sem["h_lo"], g + 2)
                        attend(g)

                both_ends(pe, NI, body)

            @block.scalar
            def _(act):
                def second_norm(g):
                    wait(act, sem["t1"], g)
                    for k in range(KD):
                        last = nc.scalar.activation(y[:, k, :], H1g[:, k, g, :], ACT.Identity, bias=shift[:, k:k + 1],
                                                    scale=scale[:, k:k + 1])
                    last.then_inc(sem["y_done"], 1)

                def relu(g):
                    act.wait_ge(sem["t2"], g + 1)
                    nc.scalar.activation(hT_hi[:, :, :], pT[:, :, :], ACT.Relu).then_inc(sem["h_hi"], 1)

                act.wait_ge(sem["step"], KD + 3)
                second_norm(0)
                relu(0)

                def body(it):
                    for b in range(2):
                        g = 2 * it + b
                        end = isinstance(g, int) and g == NG - 1
                        act.wait_ge(sem["w_mm"], g + 1)
                        nc.scalar.activation(v_hi[:, :, :], pW[:, :, 0:D], ACT.Copy).then_inc(sem["v_hi_done"], 1)
                        if not end:
                            second_norm(g + 1)
                        act.wait_ge(sem["soft"], SOFT * g + 6)
                        nc.scalar.activation(e[:, :, :], e[:, :, :], ACT.Exp).then_inc(sem["exp_done"], 1)
                        if not end:
                            relu(g + 1)
                        act.wait_ge(sem["t3"], g + 1)
                        nc.scalar.activation(p_hi[:, :, :], pT[:, 0, :].rearrange("p (t r) -> p t r", t=GT), ACT.Copy)\
                            .then_inc(sem["p_hi_done"], 1)

                both_ends(act, NI, body)

            @block.vector
            def _(dve):
                V = nc.vector
                link = Chain(dve, sem["step"])
                dve.wait_ge(sem["consts"], 16 * len(loads))
                for m in range(KD):
                    link(V.bn_aggr(mv2[:, m, :], st2[:, m, :, :].rearrange("p g s -> p (g s)")))
                V.tensor_scalar(ve2[:, :], mv2[:, :, 1], EPS, None, ALU.add).then_inc(sem["ve2_ready"], 1)
                dve.wait_ge(sem["rstd2_ready"], 1)
                link(V.tensor_tensor(scale[:, :], g2[:, :], rstd2[:, :], ALU.mult))
                link(V.tensor_tensor(moved[:, :], mv2[:, :, 0], scale[:, :], ALU.mult))
                link(V.tensor_tensor(shift[:, :], be2[:, :], moved[:, :], ALU.subtract))
                for i in range(2):
                    link(V.tensor_tensor(prod[:, :, i, :], w_ext[:, :, 0:D],
                                         a_row[:, i, :].unsqueeze(1).to_broadcast([P, KD, D]), ALU.mult))
                    link(V.tensor_reduce(w_ext[:, :, D + i:D + i + 1], prod[:, :, i, :], AX.X, ALU.add))
                link(V.tensor_copy(w_hi[:, :, :], w_ext[:, :, :]))
                link(V.tensor_tensor(w_lo[:, :, :], w_ext[:, :, :], f32(w_hi[:, :, :]), ALU.subtract))
                link(V.tensor_copy(a_hi[:, :, :], f32(w_hi[:, :, D + 1:D + 2]).to_broadcast([P, KD, P])))
                link(V.tensor_copy(a_lo[:, :, :], f32(w_lo[:, :, D + 1:D + 2]).to_broadcast([P, KD, P])))
                link(V.tensor_scalar(mask[:, :], adj2[:, :], 0.0, -BIG, ALU.is_equal, ALU.mult))
                V.memset(prob[:, :, :], 0.0).then_inc(sem["ready"], 1)

                def norm(g, b):
                    dve.wait_ge(sem["t1"], g + 1)
                    dve.wait_ge(landed[b], 8 * (g - b) + 16)
                    V.tensor_tensor(xt[b][:, :, :], pTr, xt[b][:, :, :], ALU.add).then_inc(sem["x3_done"], 1)
                    dve.wait_ge(sem["x3_done"], g + 1)
                    for t in range(GT):
                        last = V.bn_stats(st[:, t, :], xt[b][:, t, :])
                    last.then_inc(sem["stats"], 1)
                    dve.wait_ge(sem["stats"], g + 1)
                    wait(dve, sem["rstd_ready"], g)
                    V.memset(ve[:, :], EPS)
                    for t in range(GT):
                        last = V.bn_aggr(mv[:, t, :], st[:, t, :])
                    last.then_inc(sem["moments"], 1)
                    dve.wait_ge(sem["moments"], g + 1)
                    V.tensor_tensor(ve[:, :], ve[:, :], mv[:, :, 1], ALU.add).then_inc(sem["var_eps"], 1)
                    dve.wait_ge(sem["rstd_ready"], g + 1)
                    for t in range(GT):
                        last = V.tensor_scalar(xn[:, t, :], xt[b][:, t, :], mv[:, t, 0:1], rstd[:, t:t + 1],
                                               ALU.subtract, ALU.mult)
                    last.then_inc(sem["normed"], 1)
                    dve.wait_ge(sem["h_hi"], g + 1)
                    V.scalar_tensor_tensor(out=hT_lo[:, :, :], in0=pT[:, :, :], scalar=0.0, in1=f32(hT_hi[:, :, :]),
                                           op0=ALU.max, op1=ALU.subtract).then_inc(sem["h_lo"], 1)

                def softmax(g):
                    n = [0]

                    def step(ins):
                        n[0] += 1
                        ins.then_inc(sem["soft"], 1)
                        dve.wait_ge(sem["soft"], SOFT * g + n[0])

                    def over(col):
                        return col[:, :].unsqueeze(2).to_broadcast([P, GT, NODES])

                    dve.wait_ge(sem["v_hi_done"], g + 1)
                    step(V.tensor_copy(s1[:, :], pW[:, :, D]))
                    dve.wait_ge(sem["s_mm"], g + 1)
                    for h in range(2):
                        r = slice(h * NODES, (h + 1) * NODES)
                        ins = V.tensor_tensor(e[r, :, :], pS[r, :, r], s1[r, :].unsqueeze(2).to_broadcast([NODES, GT, NODES]),
                                              ALU.add)
                    step(ins)
                    step(V.scalar_tensor_tensor(out=e[:, :, :], in0=e[:, :, :], scalar=LEAK, in1=e[:, :, :],
                                                op0=ALU.mult, op1=ALU.max))
                    step(V.tensor_tensor(e[:, :, :], e[:, :, :], mask[:, :].unsqueeze(1).to_broadcast([P, GT, NODES]), ALU.add))
                    step(V.tensor_reduce(top[:, :], e[:, :, :], AX.X, ALU.max))
                    step(V.tensor_tensor(e[:, :, :], e[:, :, :], over(top), ALU.subtract))
                    dve.wait_ge(sem["v_hi_done"], g + 1)
                    V.tensor_tensor(v_lo[:, :, :], pW[:, :, 0:D], f32(v_hi[:, :, :]), ALU.subtract)
                    dve.wait_ge(sem["exp_done"], g + 1)
                    step(V.tensor_reduce(total[:, :], e[:, :, :], AX.X, ALU.add))
                    step(V.reciprocal(inv[:, :], total[:, :]))
                    for h in range(2):
                        r = slice(h * NODES, (h + 1) * NODES)
                        ins = V.tensor_tensor(prob[r, :, r], e[r, :, :], inv[r, :].unsqueeze(2).to_broadcast([NODES, GT, NODES]),
                                              ALU.mult)
                        if h == 0:
                            step(ins)
                    ins.then_inc(sem["prob_done"], 1)

                norm(0, 0)

                def body(it):
                    for b in range(2):
                        g = 2 * it + b
                        softmax(g)
                        if not (isinstance(g, int) and g == NG - 1):
                            norm(g + 1, 1 - b)
                        dve.wait_ge(sem["p_hi_done"], g + 1)
                        V.tensor_tensor(p_lo[:, :, :], pT[:, 0, :].rearrange("p (t r) -> p t r", t=GT), f32(p_hi[:, :, :]),
                                        ALU.subtract).then_inc(sem["p_lo_done"], 1)
                        dve.wait_ge(sem["o_mm"], g + 1)
                        V.tensor_tensor(xt[b][:, :, :], pO, xt[b][:, :, :], ALU.add).then_inc(sem["out_done"], 1)

                both_ends(dve, NI, body)


def later_layers(core, a, x2, out):
    with ExitStack() as ctx:
        sb, _ = allocator(core.nc, ctx)
        H1 = sb("H1", [P, KH, ROWS])[:, :, :]
        st1, st2 = sb("st1", [P, KH, NG, 6]), sb("st2", [P, KD, NG, 6])
        with ExitStack() as inner:
            sb2, _ = allocator(core.nc, inner)
            W2 = [sb2(f"w2_{n}", [P, KH, D], F32R) for n in ("hi", "lo")]
            conv_first(core, a, x2, H1, st1, W2)
            conv_second(core, a, H1, st1, st2, W2)
        dense_attention(core, a, x2, out, H1, st2)


def build(nc, args):
    with ExitStack() as ctx:
        core = Core(nc, ctx)

        def groups(rows):
            return rows.rearrange("(g t p) d -> g p t d", t=GT, p=P)

        x = groups(args["x"].rearrange("b n d -> (b n) d"))
        out = groups(args["out"].rearrange("b n d -> (b n) d"))
        x2 = groups(nc.dram_tensor("x2_scratch", [ROWS, D], F32).ap())
        with ExitStack() as first:
            HT = first.enter_context(nc.sbuf_tensor("HT", [P, KD, ROWS], F32))[:, :, :]
            gcn_phase(core, x, args["gcn_w"], args["gcn_b"], args["adj_t"], args["ident"], HT)
            lstm_phase(core, args["wih"], args["whh"], args["bih"], args["bhh"], HT)
            attention_layer(core, args, x, x2, HT)
        later_layers(core, args, x2, out)


def layouts(inp):
    import numpy as np

    def chunks(w):
        return np.ascontiguousarray(w.reshape(-1, P, w.shape[1]).transpose(1, 0, 2))

    def alike(v):
        return np.ascontiguousarray(np.broadcast_to(v.reshape(1, -1), (P, v.size)))

    def columns(v):
        return np.ascontiguousarray(v.reshape(-1, P).T)

    def gates(b):
        return np.ascontiguousarray(b.reshape(SKIPS, -1, P).transpose(2, 0, 1))

    i = {k: np.asarray(v) for k, v in inp.items()}
    edge = np.arange(EDGES, dtype=np.float32)
    return {
        "x": i["x"], "adj": i["adj"], "adj_t": np.ascontiguousarray(i["adj"].T), "ident": np.eye(P, dtype=np.float32),
        "gcn_w": np.stack([chunks(i["L0_gnn_Wg0"]), chunks(i["L0_gnn_Wg1"])]),
        "gcn_b": np.stack([alike(i["L0_gnn_bg0"]), alike(i["L0_gnn_bg1"])]),
        "wih": np.stack([chunks(w.T) for w in i["L0_gnn_Wih"]]), "whh": np.stack([chunks(w.T) for w in i["L0_gnn_Whh"]]),
        "bih": gates(i["L0_gnn_bih"]), "bhh": gates(i["L0_gnn_bhh"]),
        "src_row": alike(i["L1_gnn_src"]), "dst_row": alike(i["L1_gnn_dst"]),
        "src_col": columns(i["L1_gnn_src"]), "dst_col": columns(i["L1_gnn_dst"]),
        "iota_row": alike(edge), "iota_col": columns(edge),
        "node_col": np.tile(np.arange(NODES, dtype=np.float32), TILE_GRAPHS).reshape(P, 1),
        "a_row": alike(i["L1_gnn_a"]), "a_col": columns(i["L1_gnn_a"]),
        "w_lin": chunks(i["L1_gnn_W_lin"].T), "w_val": chunks(i["L1_gnn_W_val"].T), "w_out": chunks(i["L1_gnn_W_out"].T),
        "w1": chunks(i["L2_gnn_W1"].T), "w2": chunks(i["L2_gnn_W2"].T),
        "b1": columns(i["L2_gnn_b1"]), "g1": columns(i["L2_gnn_g1"]), "be1": columns(i["L2_gnn_be1"]),
        "b2": columns(i["L2_gnn_b2"]), "g2": columns(i["L2_gnn_g2"]), "be2": columns(i["L2_gnn_be2"]),
        "w3": chunks(i["L3_gnn_W"]), "a3": alike(i["L3_gnn_a"]),
    }


def kernel(**inputs):
    import numpy as np
    import concourse.bacc as bacc
    from concourse.bass_utils import run_bass_kernel_spmd

    nc = bacc.Bacc("TRN2", target_bir_lowering=False, num_devices=1)
    arrays, args = {}, {}
    for name, a in layouts(inputs).items():
        arrays[f"in_{name}"] = a
        args[name] = nc.dram_tensor(f"in_{name}", a.shape, mybir.dt.from_np(a.dtype), kind="ExternalInput").ap()
    args["out"] = nc.dram_tensor("out", [BATCH, NODES, D], F32, kind="ExternalOutput").ap()
    build(nc, args)
    r = run_bass_kernel_spmd(nc, [arrays], core_ids=[0])
    return np.asarray(r.results[0]["out"])
```

```python
from contextlib import ExitStack

import concourse.bass as bass
from concourse import mybir

F32 = mybir.dt.float32
F32R = mybir.dt.float32r
I32 = mybir.dt.int32
ALU = mybir.AluOpType
ACT = mybir.ActivationFunctionType
AX = mybir.AxisListType

P = 128
BATCH, NODES, D = 128, 64, 256
ROWS = BATCH * NODES
KD = D // P
TILE_GRAPHS = P // NODES
GT = 4
GROWS = GT * P
NG = ROWS // GROWS
EDGES = 512
EC = EDGES // P
HEADS, DH = 4, 64
SKIPS = 4
HID2 = 512
KH = HID2 // P
EPS = 1e-5
LOG_EPS = 1e-8
LEAK = 0.2
BIG = 3.0e38


def wait(eng, sem, value):
    if isinstance(value, int) and value <= 0:
        return
    eng.wait_ge(sem, value)


def f32(ap):
    return ap.bitcast(F32)


def mm3(nc, out, w_hi, w_lo, x_hi, x_lo, first, last):
    nc.tensor.matmul(out, w_hi, x_hi, start=first, stop=False)
    nc.tensor.matmul(out, w_hi, x_lo, start=False, stop=False)
    return nc.tensor.matmul(out, w_lo, x_hi, start=False, stop=last)


class Core:

    def __init__(self, nc, ctx):
        self.nc, self.ctx = nc, ctx

    def sem(self, name):
        return self.ctx.enter_context(self.nc.semaphore(name))


def allocator(nc, ctx):
    def sb(name, shape, dt=F32):
        return ctx.enter_context(nc.sbuf_tensor(name, shape, dt))

    def ps(name, shape, dt=F32):
        return ctx.enter_context(nc.psum_tensor(name, shape, dt))

    return sb, ps


def both_ends(eng, n, body):
    body(0)
    with eng.Fori(1, n - 1) as i:
        body(i)
    body(n - 1)


def peeled(eng, n, body):
    body(0)
    with eng.Fori(1, n) as i:
        body(i)


class Chain:

    def __init__(self, eng, sem):
        self.eng, self.sem, self.n = eng, sem, 0

    def __call__(self, ins):
        self.n += 1
        ins.then_inc(self.sem, 1)
        self.eng.wait_ge(self.sem, self.n)


def gcn_phase(core, x, w, bg, adj_t, ident_in, HT):
    nc = core.nc
    NI = NG // 2
    with ExitStack() as ctx:
        sb, ps = allocator(nc, ctx)
        ident = sb("a_ident", [P, P])
        w_raw = sb("a_w_raw", [P, 2, KD, D])
        w_hi = sb("a_w_hi", [P, 2, KD, D], F32R)
        w_lo = sb("a_w_lo", [P, 2, KD, D], F32R)
        bias = sb("a_bias", [P, 2, D])
        adj_raw = sb("a_adj_raw", [P, P])
        adj_hi = sb("a_adj_hi", [P, P], F32R)
        adj_lo = sb("a_adj_lo", [P, P], F32R)
        mhalf = sb("a_mhalf", [P, GT])
        xt = [sb(f"a_xt{b}", [P, GT, D]) for b in range(2)]
        xn = [sb(f"a_xn{b}", [P, GT, D]) for b in range(2)]
        st = [sb(f"a_st{b}", [P, GT, 6]) for b in range(2)]
        mv = [sb(f"a_mv{b}", [P, GT, 2]) for b in range(2)]
        ve = [sb(f"a_ve{b}", [P, GT]) for b in range(2)]
        rstd = [sb(f"a_rstd{b}", [P, GT]) for b in range(2)]
        hT_hi = [sb(f"a_hThi{b}", [P, KD, GROWS], F32R) for b in range(2)]
        hT_lo = [sb(f"a_hTlo{b}", [P, KD, GROWS], F32R) for b in range(2)]
        u = [sb(f"a_u{b}", [P, GT, D]) for b in range(2)]
        u_hi = [sb(f"a_uhi{b}", [P, GT, D], F32R) for b in range(2)]
        u_lo = [sb(f"a_ulo{b}", [P, GT, D], F32R) for b in range(2)]
        pV = [ps(f"a_pV{b}", [P, KD, GROWS]) for b in range(2)]
        pU = [ps(f"a_pU{b}", [P, GT, D]) for b in range(2)]
        consts = core.sem("a_consts")
        zeroed = core.sem("a_zeroed")
        w_ready = core.sem("a_w_ready")
        x_in = [core.sem(f"a_x_in{b}") for b in range(2)]
        stats, moments = core.sem("a_stats"), core.sem("a_moments")
        var_eps, rstd_ready = core.sem("a_var_eps"), core.sem("a_rstd")
        normed, turned = core.sem("a_normed"), core.sem("a_turned")
        hi_done = [core.sem(f"a_hi{l}") for l in range(2)]
        lo_done = [core.sem(f"a_lo{l}") for l in range(2)]
        u_mm = [core.sem(f"a_u_mm{l}") for l in range(2)]
        u_sum = [core.sem(f"a_u_sum{l}") for l in range(2)]
        u_hi_done = [core.sem(f"a_u_hi{l}") for l in range(2)]
        u_lo_done = [core.sem(f"a_u_lo{l}") for l in range(2)]
        v_mm = [core.sem(f"a_v_mm{l}") for l in range(2)]
        out_done = core.sem("a_out")
        HTg = HT.rearrange("p k (g c) -> p k g c", c=GROWS)

        def n(it, b):
            return 2 * it + b + 1

        with nc.Block() as block:
            @block.sync
            def _(sp):
                sp.dma_start(ident[:, :], ident_in).then_inc(consts, 16)
                for l in range(2):
                    sp.dma_start(w_raw[:, l], w[l]).then_inc(consts, 16)
                    sp.dma_start(bias[:, l], bg[l]).then_inc(consts, 16)
                sp.wait_ge(zeroed, 1)
                for g in range(TILE_GRAPHS):
                    r = slice(g * NODES, (g + 1) * NODES)
                    sp.dma_start(adj_raw[r, r], adj_t).then_inc(consts, 16)

                def body(it):
                    for b in range(2):
                        wait(sp, normed, n(it, b) - 2)
                        sp.dma_start(xt[b][:, :, :], x[2 * it + b]).then_inc(x_in[b], 16)

                peeled(sp, NI, body)

            @block.gpsimd
            def _(pool):
                nc.gpsimd.memset(adj_raw[:, :], 0.0).then_inc(zeroed, 1)
                nc.gpsimd.memset(mhalf[:, :], -0.5).then_inc(zeroed, 1)
                pool.wait_ge(zeroed, 2)

                def body(it):
                    for b in range(2):
                        pool.wait_ge(var_eps, n(it, b))
                        wait(pool, normed, n(it, b) - 2)
                        nc.gpsimd.tensor_tensor(rstd[b][:, :], ve[b][:, :], mhalf[:, :], ALU.pow).then_inc(rstd_ready, 1)
                    for l in range(2):
                        for b in range(2):
                            pool.wait_ge(u_hi_done[l], n(it, b))
                            nc.gpsimd.tensor_tensor(u_lo[b][:, :, :], u[b][:, :, :], f32(u_hi[b][:, :, :]),
                                                    ALU.subtract).then_inc(u_lo_done[l], 1)

                peeled(pool, NI, body)

            @block.vector
            def _(dve):
                dve.wait_ge(consts, 16 * 7)
                dve.wait_ge(zeroed, 2)
                nc.vector.tensor_copy(w_hi[:, :, :, :], w_raw[:, :, :, :]).then_inc(w_ready, 1)
                nc.vector.tensor_copy(adj_hi[:, :], adj_raw[:, :]).then_inc(w_ready, 1)
                dve.wait_ge(w_ready, 2)
                nc.vector.tensor_tensor(w_lo[:, :, :, :], w_raw[:, :, :, :], f32(w_hi[:, :, :, :]), ALU.subtract).then_inc(w_ready, 1)
                nc.vector.tensor_tensor(adj_lo[:, :], adj_raw[:, :], f32(adj_hi[:, :]), ALU.subtract).then_inc(w_ready, 1)

                def body(it):
                    for b in range(2):
                        dve.wait_ge(x_in[b], 16 * it + 16)
                        wait(dve, moments, n(it, b) - 2)
                        for j in range(GT):
                            last = nc.vector.bn_stats(st[b][:, j, :], xt[b][:, j, :])
                        last.then_inc(stats, 1)
                        dve.wait_ge(stats, n(it, b))
                        wait(dve, rstd_ready, n(it, b) - 2)
                        nc.vector.memset(ve[b][:, :], EPS)
                        for j in range(GT):
                            last = nc.vector.bn_aggr(mv[b][:, j, :], st[b][:, j, :])
                        last.then_inc(moments, 1)
                    for b in range(2):
                        dve.wait_ge(moments, n(it, b))
                        nc.vector.tensor_tensor(ve[b][:, :], ve[b][:, :], mv[b][:, :, 1], ALU.add).then_inc(var_eps, 1)
                    for b in range(2):
                        dve.wait_ge(rstd_ready, n(it, b))
                        dve.wait_ge(moments, n(it, b))
                        wait(dve, turned, n(it, b) - 2)
                        for j in range(GT):
                            last = nc.vector.tensor_scalar(xn[b][:, j, :], xt[b][:, j, :], mv[b][:, j, 0:1],
                                                           rstd[b][:, j:j + 1], ALU.subtract, ALU.mult)
                        last.then_inc(normed, 1)
                    for l in range(2):
                        for b in range(2):
                            dve.wait_ge(hi_done[l], n(it, b))
                            nc.vector.scalar_tensor_tensor(out=hT_lo[b][:, :, :], in0=pV[b][:, :, :], scalar=0.0,
                                                           in1=f32(hT_hi[b][:, :, :]), op0=ALU.max,
                                                           op1=ALU.subtract).then_inc(lo_done[l], 1)
                        for b in range(2):
                            dve.wait_ge(u_mm[l], n(it, b))
                            if l == 0:
                                wait(dve, u_lo_done[1], n(it, b) - 2)
                            else:
                                dve.wait_ge(u_lo_done[0], n(it, b))
                            nc.vector.tensor_tensor(u[b][:, :, :], pU[b][:, :, :],
                                                    bias[:, l, :].unsqueeze(1).to_broadcast([P, GT, D]),
                                                    ALU.add).then_inc(u_sum[l], 1)

                peeled(dve, NI, body)

            @block.scalar
            def _(act):
                def body(it):
                    for l in range(2):
                        for b in range(2):
                            act.wait_ge(turned if l == 0 else v_mm[0], n(it, b))
                            nc.scalar.activation(hT_hi[b][:, :, :], pV[b][:, :, :], ACT.Relu).then_inc(hi_done[l], 1)
                        for b in range(2):
                            act.wait_ge(u_sum[l], n(it, b))
                            nc.scalar.activation(u_hi[b][:, :, :], u[b][:, :, :], ACT.Copy).then_inc(u_hi_done[l], 1)
                    for b in range(2):
                        act.wait_ge(v_mm[1], n(it, b))
                        nc.scalar.activation(HTg[:, :, 2 * it + b, :], pV[b][:, :, :], ACT.Relu).then_inc(out_done, 1)

                peeled(act, NI, body)

            @block.tensor
            def _(pe):
                pe.wait_ge(w_ready, 4)

                def body(it):
                    for b in range(2):
                        pe.wait_ge(normed, n(it, b))
                        wait(pe, out_done, n(it, b) - 2)
                        for j in range(GT):
                            for k in range(KD):
                                last = nc.tensor.transpose(pV[b][:, k, j * P:(j + 1) * P],
                                                           xn[b][:, j, k * P:(k + 1) * P], ident[:, :])
                        last.then_inc(turned, 1)
                    for l in range(2):
                        for b in range(2):
                            pe.wait_ge(hi_done[l], n(it, b))
                            pe.wait_ge(lo_done[l], n(it, b))
                            for j in range(GT):
                                c = slice(j * P, (j + 1) * P)
                                for k in range(KD):
                                    last = mm3(nc, pU[b][:, j, :], hT_hi[b][:, k, c], hT_lo[b][:, k, c],
                                               w_hi[:, l, k, :], w_lo[:, l, k, :], k == 0, k == KD - 1)
                            last.then_inc(u_mm[l], 1)
                        for b in range(2):
                            pe.wait_ge(u_hi_done[l], n(it, b))
                            pe.wait_ge(u_lo_done[l], n(it, b))
                            for k in range(KD):
                                c = slice(k * P, (k + 1) * P)
                                for j in range(GT):
                                    last = mm3(nc, pV[b][:, k, j * P:(j + 1) * P], u_hi[b][:, j, c], u_lo[b][:, j, c],
                                               adj_hi[:, :], adj_lo[:, :], True, True)
                            last.then_inc(v_mm[l], 1)

                peeled(pe, NI, body)


def lstm_phase(core, wih, whh, bih, bhh, HT):
    nc = core.nc
    NC4 = 4 * D
    I, F, G, O = range(4)
    SIG = {I: ACT.Sigmoid, F: ACT.Sigmoid, G: ACT.Tanh, O: ACT.Sigmoid}
    with ExitStack() as ctx:
        sb, ps = allocator(nc, ctx)
        raw = [sb(f"b_raw{m}", [P, KD, NC4]) for m in range(2)]
        w_hi = [[sb(f"b_whi{s}{m}", [P, KD, NC4], F32R) for m in range(2)] for s in range(2)]
        w_lo = [[sb(f"b_wlo{s}{m}", [P, KD, NC4], F32R) for m in range(2)] for s in range(2)]
        bias = sb("b_bias", [P, SKIPS, 8])
        bias2 = sb("b_bias2", [P, SKIPS, 8])
        xs_hi = [sb(f"b_xshi{b}", [P, KD, GROWS], F32R) for b in range(2)]
        xs_lo = [sb(f"b_xslo{b}", [P, KD, GROWS], F32R) for b in range(2)]
        hs_hi = [sb(f"b_hshi{b}", [P, KD, GROWS], F32R) for b in range(2)]
        hs_lo = [sb(f"b_hslo{b}", [P, KD, GROWS], F32R) for b in range(2)]
        cell = [sb(f"b_cell{b}", [P, KD, GROWS]) for b in range(2)]
        gate = [sb(f"b_gate{s}", [P, 4, GROWS]) for s in range(2)]
        tc = [sb(f"b_tc{s}", [P, GROWS]) for s in range(2)]
        pG = [ps(f"b_pG{s}", [P, 4, GROWS]) for s in range(2)]
        bias_in, raw_in = core.sem("b_bias_in"), core.sem("b_raw_in")
        bias_ready, w_part, w_ready = core.sem("b_bias_ready"), core.sem("b_w_part"), core.sem("b_w_ready")
        gate_mm, gate_act = core.sem("b_gate_mm"), core.sem("b_gate_act")
        xs_part, xs_ready = core.sem("b_xs_part"), core.sem("b_xs_ready")
        hs_part, hs_ready = core.sem("b_hs_part"), core.sem("b_hs_ready")
        ig_ready, fc_ready, cell_ready = core.sem("b_ig"), core.sem("b_fc"), core.sem("b_cell_ready")
        tanh_ready, h_ready = core.sem("b_tanh"), core.sem("b_h_ready")

        class Plan:

            def __init__(self, p, before):
                self.p = p
                self.nw = NODES // p
                self.graphs = GROWS // NODES if p == 1 else 2 * GROWS // NODES
                self.n = self.graphs * self.nw
                self.its = BATCH // (2 * self.graphs)
                self.units = 4 * p
                self.gates = 12 + 16 * (p - 1)
                if before is None:
                    self.u0 = self.g0 = self.x0 = self.h0 = self.i0 = self.w0 = 0
                else:
                    q = before
                    self.u0 = q.u0 + q.its * q.units
                    self.g0 = q.g0 + q.its * q.gates
                    self.x0 = q.x0 + 2 + q.its * 2 * q.p
                    self.h0 = q.h0 + q.its * 2 * (q.p - 1)
                    self.i0 = q.i0 + q.its * 4 * (q.p - 1)
                    self.w0 = q.w0 + (1 if q.p == 1 else 0) + (0 if q.p == 1 else q.wn)
                self.wn = 0

            def unit(self, it, t, b, s):
                return self.u0 + it * self.units + (2 * t + b) * 2 + s

            def gate(self, it, t, b, s):
                before = (2 * b + s) * 3 if t == 0 else 12 + 16 * (t - 1) + (2 * b + s) * 4
                return self.g0 + it * self.gates + before

            def later(self, it, t, b, s):
                return self.i0 + it * 4 * (self.p - 1) + (t - 1) * 4 + 2 * b + s

            def x(self, it, t, b):
                return self.x0 + it * 2 * self.p + 2 * t + b

            def h(self, it, t, b):
                return self.h0 + it * 2 * (self.p - 1) + 2 * t + b

            def order(self, t):
                return (I, G, O) if t == 0 else (I, G, F, O)

            def windows(self, it, b, k, t):
                v = HT.rearrange("p k (i g c) -> p k i g c", g=self.graphs, c=NODES)[:, k, 2 * it + b, :, :]
                return v[:, :, t:t + (self.nw - 1) * self.p + 1:self.p]

            def flat(self, ap):
                return ap[:, 0:self.n].rearrange("p (g w) -> p g w", w=self.nw)

        plans = []
        for p in range(1, SKIPS + 1):
            plans.append(Plan(p, plans[-1] if plans else None))
        w_count = [1]
        for q in plans[:-1]:
            w_count.append(w_count[-1] + q.its)

        def loop(eng, plan, body):
            if plan.p == 1:
                peeled(eng, plan.its, body)
            else:
                with eng.Fori(0, plan.its) as it:
                    body(it)

        with nc.Block() as block:
            @block.sync
            def _(sp):
                sp.dma_start(bias[:, :, :], bih).then_inc(bias_in, 16)
                sp.dma_start(bias2[:, :, :], bhh).then_inc(bias_in, 16)
                for p in range(SKIPS):
                    if p >= 1:
                        sp.wait_ge(w_ready, w_count[p - 1])
                    for m, src in enumerate((wih, whh)):
                        sp.dma_start(raw[m][:, :, :], src[p]).then_inc(raw_in, 16)

            @block.tensor
            def _(pe):
                for plan in plans:
                    slot = plan.p % 2
                    pe.wait_ge(w_ready, w_count[plan.p - 1])

                    def body(it, plan=plan, slot=slot):
                        for t in range(plan.p):
                            for b in range(2):
                                for s in range(2):
                                    if s == 0:
                                        pe.wait_ge(xs_ready, plan.x(it, t, b) + 1)
                                        if t:
                                            pe.wait_ge(hs_ready, plan.h(it, t - 1, b) + 1)
                                    ahead = 3 if t == 0 and (b or s) else 4
                                    if t == 0 and b == 0 and s == 0 and plan.p <= 2:
                                        ahead = 3
                                    if t == 1 and b == 0 and s == 0:
                                        ahead = 3
                                    wait(pe, gate_act, plan.gate(it, t, b, s) - ahead)
                                    for g in plan.order(t):
                                        c = slice(g * D + s * P, g * D + s * P + P)
                                        out = pG[s][:, g, 0:plan.n]
                                        pairs = [(0, xs_hi[b], xs_lo[b], k) for k in range(KD)]
                                        if t:
                                            pairs += [(1, hs_hi[b], hs_lo[b], k) for k in range(KD)]
                                        for i, (m, hi, lo, k) in enumerate(pairs):
                                            last = mm3(nc, out, w_hi[slot][m][:, k, c], w_lo[slot][m][:, k, c],
                                                       hi[:, k, 0:plan.n], lo[:, k, 0:plan.n],
                                                       i == 0, i == len(pairs) - 1)
                                        last.then_inc(gate_mm, 1)

                    loop(pe, plan, body)

            @block.scalar
            def _(act):
                act.wait_ge(bias_ready, 1)
                for plan in plans:
                    def body(it, plan=plan):
                        for t in range(plan.p):
                            for b in range(2):
                                for s in range(2):
                                    wait(act, h_ready, plan.unit(it, t, b, s) - 1)
                                    for i, g in enumerate(plan.order(t)):
                                        act.wait_ge(gate_mm, plan.gate(it, t, b, s) + i + 1)
                                        nc.scalar.activation(gate[s][:, g, 0:plan.n], pG[s][:, g, 0:plan.n], SIG[g],
                                                             bias=bias[:, plan.p - 1, 2 * g + s:2 * g + s + 1])\
                                            .then_inc(gate_act, 1)
                                    act.wait_ge(cell_ready, plan.unit(it, t, b, s) + 1)
                                    pt, pb = (t, 0) if b else (t - 1, 1)
                                    if 0 <= pt < plan.p - 1:
                                        act.wait_ge(hs_ready, plan.h(it, pt, pb) + 1)
                                    nc.scalar.activation(tc[s][:, 0:plan.n], cell[b][:, s, 0:plan.n],
                                                         ACT.Tanh).then_inc(tanh_ready, 1)

                    loop(act, plan, body)

            @block.gpsimd
            def _(pool):
                for plan in plans[1:]:
                    def body(it, plan=plan):
                        for t in range(1, plan.p):
                            for b in range(2):
                                for s in range(2):
                                    pool.wait_ge(gate_act, plan.gate(it, t, b, s) + 2)
                                    nc.gpsimd.tensor_tensor(gate[s][:, I, 0:plan.n], gate[s][:, I, 0:plan.n],
                                                            gate[s][:, G, 0:plan.n], ALU.mult).then_inc(ig_ready, 1)

                    loop(pool, plan, body)

            @block.vector
            def _(dve):
                dve.wait_ge(bias_in, 32)
                nc.vector.tensor_tensor(bias[:, :, :], bias[:, :, :], bias2[:, :, :], ALU.add).then_inc(bias_ready, 1)
                parts = [0, 0, 0]

                def split_w(slot, cols, last_sem):
                    for m in range(2):
                        nc.vector.tensor_copy(w_hi[slot][m][:, :, cols], raw[m][:, :, cols]).then_inc(w_part, 1)

                def split_w_lo(slot, cols):
                    for m in range(2):
                        last = nc.vector.tensor_tensor(w_lo[slot][m][:, :, cols], raw[m][:, :, cols],
                                                       f32(w_hi[slot][m][:, :, cols]), ALU.subtract)
                    last.then_inc(w_ready, 1)

                dve.wait_ge(raw_in, 32)
                split_w(1, slice(0, NC4), None)
                dve.wait_ge(w_part, 2)
                split_w_lo(1, slice(0, NC4))

                def split_x(plan, it, t, b, count):
                    for k in range(KD):
                        nc.vector.tensor_copy(plan.flat(xs_hi[b][:, k, :]), plan.windows(it, b, k, t))\
                            .then_inc(xs_part, 1)
                    dve.wait_ge(xs_part, KD * (count + 1))
                    for k in range(KD):
                        last = nc.vector.tensor_tensor(plan.flat(xs_lo[b][:, k, :]), plan.windows(it, b, k, t),
                                                       plan.flat(f32(xs_hi[b][:, k, :])), ALU.subtract)
                    last.then_inc(xs_ready, 1)

                for plan in plans:
                    n, T = plan.n, plan.p
                    wait(dve, h_ready, plan.u0)
                    wait(dve, xs_ready, plan.x0)
                    for b in range(2):
                        split_x(plan, 0, 0, b, plan.x0 + b)

                    def body(it, plan=plan, n=n, T=T):
                        for t in range(T):
                            for b in range(2):
                                for s in range(2):
                                    un, g0, ng = plan.unit(it, t, b, s), plan.gate(it, t, b, s), len(plan.order(t))
                                    c = cell[b][:, s, 0:n]
                                    if s == 1:
                                        dve.wait_ge(gate_mm, g0 + ng)
                                        if t < T - 1:
                                            split_x(plan, it, t + 1, b, plan.x(it, t + 1, b))
                                        else:
                                            wait(dve, h_ready, plan.u0 + it * plan.units)
                                            split_x(plan, (it + 1) & (plan.its - 1), 0, b, plan.x(it, T, b))
                                    if t == 0:
                                        dve.wait_ge(gate_act, g0 + 2)
                                        nc.vector.tensor_tensor(c, gate[s][:, I, 0:n], gate[s][:, G, 0:n],
                                                                ALU.mult).then_inc(cell_ready, 1)
                                    else:
                                        dve.wait_ge(gate_act, g0 + 3)
                                        nc.vector.tensor_tensor(c, gate[s][:, F, 0:n], c, ALU.mult).then_inc(fc_ready, 1)
                                        dve.wait_ge(fc_ready, plan.later(it, t, b, s) + 1)
                                        dve.wait_ge(ig_ready, plan.later(it, t, b, s) + 1)
                                        nc.vector.tensor_tensor(c, c, gate[s][:, I, 0:n], ALU.add).then_inc(cell_ready, 1)
                                    dve.wait_ge(gate_act, g0 + ng)
                                    dve.wait_ge(tanh_ready, un + 1)
                                    if t == T - 1:
                                        nc.vector.tensor_tensor(plan.windows(it, b, s, t), plan.flat(gate[s][:, O, :]),
                                                                plan.flat(tc[s][:, :]), ALU.mult).then_inc(h_ready, 1)
                                    else:
                                        nc.vector.tensor_tensor(tc[s][:, 0:n], gate[s][:, O, 0:n], tc[s][:, 0:n],
                                                                ALU.mult).then_inc(h_ready, 1)
                                if t < T - 1:
                                    for s in range(2):
                                        dve.wait_ge(h_ready, plan.unit(it, t, b, s) + 1)
                                        nc.vector.tensor_copy(hs_hi[b][:, s, 0:n], tc[s][:, 0:n]).then_inc(hs_part, 1)
                                    dve.wait_ge(hs_part, 2 * (plan.h(it, t, b) + 1))
                                    for s in range(2):
                                        last = nc.vector.tensor_tensor(hs_lo[b][:, s, 0:n], tc[s][:, 0:n],
                                                                       f32(hs_hi[b][:, s, 0:n]), ALU.subtract)
                                    last.then_inc(hs_ready, 1)
                        if plan.p < SKIPS:
                            wc = NC4 // plan.its
                            cols = bass.ds(it * wc, wc)
                            dve.wait_ge(raw_in, 32 * (plan.p + 1))
                            split_w(1 - plan.p % 2, cols, None)
                            done = w_count[plan.p - 1] + it
                            dve.wait_ge(w_part, 2 * (done + 1))
                            split_w_lo(1 - plan.p % 2, cols)

                    loop(dve, plan, body)



def edge_tables(core, a, tab):
    nc = core.nc
    with ExitStack() as ctx:
        sb, ps = allocator(nc, ctx)
        ints = {n: sb(f"s_{n}_i", [P, w], I32) for n, w in (("src_row", EDGES), ("dst_row", EDGES), ("src_col", EC), ("dst_col", EC))}
        flt = {n: sb(f"s_{n}_f", list(t.shape)) for n, t in ints.items()}
        iota_row, iota_col = sb("s_iota_row", [P, EDGES]), sb("s_iota_col", [P, EC])
        node_col = sb("s_node_col", [P, 1])
        adj = sb("s_adj", [NODES, NODES])
        a_row, a_col = sb("s_a_row", [P, D]), sb("s_a_col", [P, KD])
        w_raw = sb("s_w_raw", [P, 3, KD, D])
        key_row, key_col = sb("s_key_row", [P, EDGES]), sb("s_key_col", [P, EC])
        less, rank = sb("s_less", [P, EC, EDGES]), sb("s_rank", [P, EC])
        perm = sb("s_perm", [P, EC, EDGES])
        spread = sb("s_spread", [P, 2, EC, P])
        s_row, d_row = sb("s_s_row", [P, EDGES]), sb("s_d_row", [P, EDGES])
        oh_s, oh_d = sb("s_oh_s", [P, EDGES]), sb("s_oh_d", [P, EDGES])
        s_col = sb("s_s_col", [P, EC])
        picked = sb("s_picked", [NODES, EDGES])
        ones = sb("s_ones", [NODES, P])
        weight = sb("s_weight", [P, EDGES])
        a_abs = sb("s_a_abs", [P, D])
        prod = sb("s_prod", [P, KD, D])
        wq = sb("s_wq", [P, KD, D])
        wl = sb("s_wl", [P, KD, HEADS])
        pos, neg, sgn = sb("s_pos", [P, KD]), sb("s_neg", [P, KD]), sb("s_sgn", [P, KD])
        pA, pB = ps("s_pA", [P, EDGES]), ps("s_pB", [P, EDGES])
        pC, pD = ps("s_pC", [P, EC, P]), ps("s_pD", [P, EDGES])
        pW = ps("s_pW", [P, EDGES])
        landed, step = core.sem("s_landed"), core.sem("s_step")
        ranked, sorted_mm = core.sem("s_ranked"), core.sem("s_sorted_mm")
        onehot, turned = core.sem("s_onehot"), core.sem("s_turned")
        picked_ready, weight_mm = core.sem("s_picked_ready"), core.sem("s_weight_mm")
        weight_ready = core.sem("s_weight_ready")
        loads = [(ints["src_row"], a["src_row"]), (ints["dst_row"], a["dst_row"]), (ints["src_col"], a["src_col"]),
                 (ints["dst_col"], a["dst_col"]), (iota_row, a["iota_row"]), (iota_col, a["iota_col"]),
                 (node_col, a["node_col"]), (adj, a["adj"]), (a_row, a["a_row"]), (a_col, a["a_col"]),
                 (tab["ident"], a["ident"])]
        with nc.Block() as block:
            @block.sync
            def _(sp):
                for t, src in loads:
                    sp.dma_start(t[:, :], src).then_inc(landed, 16)
                for i, src in enumerate((a["w_lin"], a["w_val"], a["w_out"])):
                    sp.dma_start(w_raw[:, i], src).then_inc(landed, 16)

            @block.vector
            def _(dve):
                link = Chain(dve, step)
                V = nc.vector
                dve.wait_ge(landed, 16 * (len(loads) + 3))
                for n in ints:
                    link(V.tensor_copy(flt[n][:, :], ints[n][:, :]))
                link(V.scalar_tensor_tensor(out=key_row[:, :], in0=flt["src_row"][:, :], scalar=float(EDGES),
                                            in1=iota_row[:, :], op0=ALU.mult, op1=ALU.add))
                link(V.scalar_tensor_tensor(out=key_col[:, :], in0=flt["src_col"][:, :], scalar=float(EDGES),
                                            in1=iota_col[:, :], op0=ALU.mult, op1=ALU.add))
                for c in range(EC):
                    link(V.tensor_scalar(less[:, c, :], key_row[:, :], key_col[:, c:c + 1], None, ALU.is_lt))
                link(V.tensor_reduce(rank[:, :], less[:, :, :], AX.X, ALU.add))
                for c in range(EC):
                    link(V.tensor_scalar(perm[:, c, :], iota_row[:, :], rank[:, c:c + 1], None, ALU.is_equal))
                link(V.tensor_copy(spread[:, 0], flt["src_col"][:, :].unsqueeze(2).to_broadcast([P, EC, P])))
                V.tensor_copy(spread[:, 1], flt["dst_col"][:, :].unsqueeze(2).to_broadcast([P, EC, P])).then_inc(ranked, 1)

                link(V.scalar_tensor_tensor(out=a_abs[:, :], in0=a_row[:, :], scalar=-1.0, in1=a_row[:, :],
                                            op0=ALU.mult, op1=ALU.max))
                for k in range(KD):
                    link(V.scalar_tensor_tensor(out=wq[:, k, :], in0=w_raw[:, 0, k, :], scalar=1.0 - LEAK,
                                                in1=a_abs[:, :], op0=ALU.mult, op1=ALU.mult))
                    link(V.scalar_tensor_tensor(out=prod[:, k, :], in0=w_raw[:, 0, k, :], scalar=LEAK,
                                                in1=a_row[:, :], op0=ALU.mult, op1=ALU.mult))
                link(V.tensor_reduce(wl[:, :, :], prod[:, :, :].rearrange("p k (h d) -> p k h d", h=HEADS), AX.X, ALU.add))
                splits = [(tab["wqv_hi"][:, :, 0:D], tab["wqv_lo"][:, :, 0:D], wq[:, :, :]),
                          (tab["wqv_hi"][:, :, D:2 * D], tab["wqv_lo"][:, :, D:2 * D], w_raw[:, 1]),
                          (tab["wo_hi"][:, :, :], tab["wo_lo"][:, :, :], w_raw[:, 2]),
                          (tab["wl_hi"][:, :, :], tab["wl_lo"][:, :, :], wl[:, :, :])]
                for hi, lo, full in splits:
                    link(V.tensor_copy(hi, full))
                    link(V.tensor_tensor(lo, full, f32(hi), ALU.subtract))
                link(V.tensor_scalar(pos[:, :], a_col[:, :], 0.0, None, ALU.is_gt))
                link(V.tensor_scalar(neg[:, :], a_col[:, :], 0.0, None, ALU.is_lt))
                link(V.tensor_tensor(sgn[:, :], pos[:, :], neg[:, :], ALU.subtract))
                link(V.memset(f32(tab["sign"][:, :, :]), 0.0))
                for k in range(KD):
                    for h in range(2):
                        r, col = slice(h * DH, (h + 1) * DH), P - HEADS + 2 * k + h
                        link(V.tensor_copy(tab["sign"][r, k, col:col + 1], sgn[r, k:k + 1]))

                dve.wait_ge(sorted_mm, 1)
                link(V.tensor_copy(s_row[:, :], pA[:, :]))
                link(V.tensor_copy(d_row[:, :], pB[:, :]))
                link(V.tensor_scalar(oh_s[:, :], s_row[:, :], node_col[:, 0:1], None, ALU.is_equal))
                link(V.tensor_scalar(oh_d[:, :], d_row[:, :], node_col[:, 0:1], None, ALU.is_equal))
                link(V.memset(ones[:, :], 1.0))
                V.tensor_tensor(tab["both"][:, :], oh_s[:, :], oh_d[:, :], ALU.add).then_inc(onehot, 1)
                link(V.tensor_copy(tab["dst"][:, :], oh_d[:, :]))
                link(V.memset(tab["same"][:, 0:1], 0.0))
                link(V.memset(tab["same"][:, EDGES:], 0.0))
                link(V.tensor_tensor(tab["same"][:, 1:EDGES], s_row[:, 1:], s_row[:, 0:EDGES - 1], ALU.is_equal))
                link(V.tensor_scalar(tab["cut"][:, :], tab["same"][:, :], 1.0, BIG, ALU.subtract, ALU.mult))
                dve.wait_ge(turned, 1)
                V.tensor_tensor(picked[:, :], pD[0:NODES, :], oh_d[0:NODES, :], ALU.mult).then_inc(picked_ready, 1)
                link(V.tensor_copy(s_col[:, :], pC[:, :, 0]))
                link(V.memset(f32(tab["src"][:, :, :, :]), 0.0))
                for g in range(TILE_GRAPHS):
                    for c in range(EC):
                        link(V.tensor_scalar(tab["src"][:, g, c, g * NODES:(g + 1) * NODES], iota_row[:, 0:NODES],
                                             s_col[:, c:c + 1], None, ALU.is_equal))
                dve.wait_ge(weight_mm, 1)
                V.tensor_scalar(weight[:, :], pW[:, :], LOG_EPS, None, ALU.add).then_inc(weight_ready, 1)

            @block.scalar
            def _(act):
                act.wait_ge(weight_ready, 1)
                nc.scalar.activation(tab["log_w"][:, :], weight[:, :], ACT.Ln)

            @block.tensor
            def _(pe):
                pe.wait_ge(ranked, 1)
                for i, out in enumerate((pA, pB)):
                    for c in range(EC):
                        last = nc.tensor.matmul(out[:, :], spread[:, i, c, :], perm[:, c, :], start=c == 0, stop=c == EC - 1)
                last.then_inc(sorted_mm, 1)
                pe.wait_ge(onehot, 1)
                for c in range(EC):
                    nc.tensor.transpose(pC[:, c, :], s_row[:, c * P:(c + 1) * P], tab["ident"][:, :])
                nc.tensor.matmul(pD[0:NODES, :], adj[:, :], oh_s[0:NODES, :], start=True, stop=True).then_inc(turned, 1)
                pe.wait_ge(picked_ready, 1)
                nc.tensor.matmul(pW[:, :], ones[:, :], picked[:, :], start=True, stop=True).then_inc(weight_mm, 1)


def edge_attention(core, x, x2, tab, HT):
    nc = core.nc
    NQ, QG, QT = 4, 32, 16
    GG = GT * TILE_GRAPHS
    NJ = QT // GT
    AHEAD = 2
    HG = GG // 2
    NH = QG // HG
    with ExitStack() as ctx:
        sb, ps = allocator(nc, ctx)
        mhalf, unused = sb("c_mhalf", [P, GT]), sb("c_unused", [P, 1])
        xt = [sb(f"c_xt{b}", [P, GT, D]) for b in range(2)]
        hst = [sb(f"c_hst{b}", [P, KD, GROWS]) for b in range(2)]
        st, mv, ve, rstd = sb("c_st", [P, GT, 6]), sb("c_mv", [P, GT, 2]), sb("c_ve", [P, GT]), sb("c_rstd", [P, GT])
        hT_hi, hT_lo = sb("c_hThi", [P, KD, GROWS], F32R), sb("c_hTlo", [P, KD, GROWS], F32R)
        keys = sb("c_keys", [P, GG, D], F32R)
        vals = sb("c_vals", [P, QG + AHEAD * GG, D], F32R)
        lin = sb("c_lin", [P, (NJ + AHEAD) * GG * HEADS], F32R)
        r_hi = [sb(f"c_rhi{b}", [P, KD, EDGES], F32R) for b in range(2)]
        r_lo = [sb(f"c_rlo{b}", [P, KD, EDGES], F32R) for b in range(2)]
        work = sb("c_work", [P, 4, EDGES])
        wv = [work[:, 2 * b:2 * b + 2, :].rearrange("p a (c f) -> p (a c) f", f=D) for b in range(2)]
        wv_hi = [t[:, :, :].rearrange("p k (a d) -> p (k a) d", d=D) for t in r_hi]
        wv_lo = [t[:, :, :].rearrange("p k (a d) -> p (k a) d", d=D) for t in r_lo]
        attn_T = sb("c_attnT", [P, EC, P])
        y_rows = [sb(f"c_yrows{b}", [P, D]) for b in range(2)]
        yT_hi, yT_lo = ([t[:, :, b * HG * NODES:(b + 1) * HG * NODES] for b in range(2)] for t in (hT_hi, hT_lo))
        pT = ps("c_pT", [P, KD, GROWS])
        pZ = [ps(f"c_pZ{b}", [P, KD, EDGES]) for b in range(2)]
        pU, pE = (ps("c_" + n, [P, EDGES])[:, :] for n in ("pU", "pE"))
        pTr = pT[:, :, :].rearrange("p k (a d) -> p (k a) d", d=D)
        pY = [pT[:, b, 0:D] for b in range(2)]
        pYT = pU.rearrange("p (k c) -> p k c", k=KD)
        pO = pU[:, :].rearrange("p (a d) -> p a d", d=D)
        names = ("half_set t1 x1_done stats moments var_eps rstd_ready normed t2 h_hi h_lo u_mm s_hi s_lo "
                 "lin_mm lin_part lin_done z_mm r_hi_done r_lo_done e_mm soft exp_done at_mm attn_ready "
                 "vg_mm wv_done wv_hi_done wv_lo_done scattered y_rows yT_mm y_hi y_lo o_mm x2_done moved stored").split()
        sem = {n: core.sem("c_" + n) for n in names}
        landed = [core.sem(f"c_landed{b}") for b in range(2)]
        HTg = HT.rearrange("p k (g c) -> p k g c", c=GROWS)

        def x1_group(G):
            return HTg[:, :, G, :].rearrange("p k (a d) -> p k a d", d=D)

        def quad(ap):
            return ap.rearrange("p (k a) d -> p k a d", k=KD)

        with nc.Block() as block:
            @block.sync
            def _(sp):
                def load(G, m):
                    b = m % 2
                    wait(sp, sem["t2"], G - 1)
                    wait(sp, sem["x1_done"], G - 1)
                    sp.dma_start(xt[b][:, :, :], x[G]).then_inc(landed[b], 16)
                    sp.dma_start(hst[b][:, :, :], HTg[:, :, G, :]).then_inc(landed[b], 16)

                def body(q, last=False):
                    if not last:
                        for m in range(NJ):
                            load(NJ * q + NJ + m, m)
                    for h in range(NH):
                        G, k = NJ * q + h // KD, h % KD
                        sp.wait_ge(sem["x2_done"], NH * q + h + 1)
                        sp.dma_start(x2[G][:, KD * k:KD * (k + 1), :], x1_group(G)[:, k]).then_inc(sem["stored"], 16)
                        if not last and h == NH // 2:
                            w, lw = AHEAD * GG, AHEAD * GG * HEADS
                            sp.dma_start(f32(lin[:, 0:lw]), f32(lin[:, QG * HEADS:QG * HEADS + lw])).then_inc(sem["moved"], 16)
                            sp.dma_start(f32(vals[:, 0:w, :]), f32(vals[:, QG:QG + w, :])).then_inc(sem["moved"], 16)

                for m in range(NJ):
                    load(m, m)
                body(0)
                with sp.Fori(1, NQ - 1) as q:
                    body(q)
                body(NQ - 1, last=True)
                sp.wait_ge(sem["stored"], 16 * NQ * NH)

            @block.gpsimd
            def _(pool):
                nc.gpsimd.memset(mhalf[:, :], -0.5).then_inc(sem["half_set"], 1)
                pool.wait_ge(sem["half_set"], 1)

                def root(G):
                    pool.wait_ge(sem["var_eps"], G + 1)
                    nc.gpsimd.tensor_tensor(rstd[:, :], ve[:, :], mhalf[:, :], ALU.pow).then_inc(sem["rstd_ready"], 1)

                def body(q, last=False):
                    for m in range(3, NJ + 3):
                        if not last or m < NJ:
                            root(NJ * q + m)

                for G in range(3):
                    root(G)
                body(0)
                with pool.Fori(1, NQ - 1) as q:
                    body(q)
                body(NQ - 1, last=True)

            @block.tensor
            def _(pe):
                def turn_back(q, m):
                    pe.wait_ge(landed[m % 2], 32 * (NJ // 2 * q + m // 2 + 1))
                    wait(pe, sem["lin_done"], NJ * q + m)
                    for t in range(GT):
                        for k in range(KD):
                            last = nc.tensor.transpose(pTr[:, t, k * P:(k + 1) * P],
                                                       hst[m % 2][:, k, t * P:(t + 1) * P], tab["ident"][:, :])
                    last.then_inc(sem["t1"], 1)

                def turn(q, m):
                    pe.wait_ge(sem["normed"], NJ * q + m + 1)
                    if m == 2:
                        wait(pe, sem["y_rows"], QT * q)
                    xn = hst[m % 2][:, :, :].rearrange("p k (a d) -> p (k a) d", d=D)
                    for t in range(GT):
                        for k in range(KD):
                            last = nc.tensor.transpose(pT[:, k, t * P:(t + 1) * P], xn[:, t, k * P:(k + 1) * P],
                                                       tab["ident"][:, :])
                    last.then_inc(sem["t2"], 1)

                def linear(q, m):
                    G = NJ * q + m
                    pe.wait_ge(sem["h_hi"], G + 1)
                    pe.wait_ge(sem["h_lo"], G + 1)
                    for i in range(GG):
                        c = slice(i * NODES, (i + 1) * NODES)
                        for k in range(KD):
                            last = mm3(nc, pT[0:NODES, 0, HEADS * i:HEADS * (i + 1)], hT_hi[:, k, c], hT_lo[:, k, c],
                                       tab["wl_hi"][:, k, :], tab["wl_lo"][:, k, :], k == 0, k == KD - 1)
                    last.then_inc(sem["lin_mm"], 1)

                def project(q, m, t):
                    if m == 2 and t == 0:
                        wait(pe, sem["x2_done"], NH * q)
                    wait(pe, sem["s_lo"], QT * q + GT * m + t)
                    c = slice(t * P, (t + 1) * P)
                    for k in range(KD):
                        last = mm3(nc, pU, hT_hi[:, k, c], hT_lo[:, k, c], tab["wqv_hi"][:, k, :],
                                   tab["wqv_lo"][:, k, :], k == 0, k == KD - 1)
                    last.then_inc(sem["u_mm"], 1)

                def gather(q, m, i):
                    gi = QG * q + GG * m + i
                    pe.wait_ge(sem["s_lo"], QT * q + GT * m + i // 2 + 1)
                    if m == 1 and i < 2:
                        wait(pe, sem["wv_done"], QG * q)
                    wait(pe, sem["r_lo_done"], gi - 1)
                    for k in range(KD):
                        last = nc.tensor.matmul(pZ[i % 2][:, k, :], keys[:, i, k * P:(k + 1) * P], tab["both"][:, :],
                                                start=True, stop=True)
                    last.then_inc(sem["z_mm"], 1)

                def score(q, m, i):
                    gi, first = GG * m + i, m % NJ == 0 and i == 0
                    pe.wait_ge(sem["r_lo_done"], QG * q + gi + 1)
                    pe.wait_ge(sem["r_hi_done"], QG * q + gi + 1)
                    if first and m:
                        pe.wait_ge(sem["soft"], 8 * q + 1)
                    at = P - HEADS - HEADS * (gi % QG)
                    for k in range(KD):
                        for n, r in enumerate((r_hi, r_lo)):
                            nc.tensor.matmul(pE, tab["sign"][:, k, at:at + P], r[i % 2][:, k, :],
                                             start=first and k == 0 and n == 0, stop=False)

                def add_linear(q):
                    pe.wait_ge(sem["lin_done"], NJ * q + NJ)
                    wait(pe, sem["moved"], 32 * q)
                    nc.tensor.matmul(pE, lin[:, 0:P], tab["both"][:, :], start=False, stop=True).then_inc(sem["e_mm"], 1)

                def turn_attention(q):
                    pe.wait_ge(sem["soft"], 8 * q + 8)
                    for c in range(EC):
                        last = nc.tensor.transpose(pT[:, 0, c * P:(c + 1) * P], work[:, 0, c * P:(c + 1) * P], tab["ident"][:, :])
                    last.then_inc(sem["at_mm"], 1)

                def values(q, gi):
                    if gi >= 2:
                        pe.wait_ge(sem["wv_done"], QG * q + gi - 1)
                    elif gi == 0:
                        wait(pe, sem["moved"], 32 * q)
                    vg = pZ[gi % 2][:, :, :].rearrange("p k (a d) -> p (k a) d", d=D)
                    for c in range(EC):
                        last = nc.tensor.matmul(vg[:, c, :], tab["dst"][:, c * P:(c + 1) * P], vals[:, gi, :],
                                                start=True, stop=True)
                    last.then_inc(sem["vg_mm"], 1)

                def scatter(q, gi):
                    t, g = gi // TILE_GRAPHS, gi % TILE_GRAPHS
                    pe.wait_ge(sem["wv_hi_done"], QG * q + gi + 1)
                    pe.wait_ge(sem["wv_lo_done"], QG * q + gi + 1)
                    if g == 0 and t >= 2:
                        pe.wait_ge(sem["y_rows"], QT * q + t - 1)
                    for n, v in enumerate((wv_hi, wv_lo)):
                        for c in range(EC):
                            last = nc.tensor.matmul(pY[t % 2], tab["src"][:, g, c, :], v[gi % 2][:, c, :],
                                                    start=g == 0 and c == 0 and n == 0,
                                                    stop=g == TILE_GRAPHS - 1 and c == EC - 1 and n == 1)
                    last.then_inc(sem["scattered"], 1)

                def turn_sums(q, h, projected):
                    pe.wait_ge(sem["y_rows"], QT * q + 2 * h + 2)
                    if h == 0:
                        pe.wait_ge(sem["s_lo"], QT * q + projected)
                    else:
                        pe.wait_ge(sem["x2_done"], NH * q + h)
                    for t in range(2):
                        for k in range(KD):
                            last = nc.tensor.transpose(pYT[:, k, t * P:(t + 1) * P],
                                                       y_rows[t][:, k * P:(k + 1) * P], tab["ident"][:, :])
                    last.then_inc(sem["yT_mm"], 1)

                def project_out(q, h):
                    b, n = h % 2, NH * q + h
                    pe.wait_ge(sem["y_hi"], n + 1)
                    pe.wait_ge(sem["y_lo"], n + 1)
                    for t in range(GT // 2):
                        c = slice(t * P, (t + 1) * P)
                        for k in range(KD):
                            last = mm3(nc, pO[:, t, :], yT_hi[b][:, k, c], yT_lo[b][:, k, c], tab["wo_hi"][:, k, :],
                                       tab["wo_lo"][:, k, :], k == 0, k == KD - 1)
                    last.then_inc(sem["o_mm"], 1)

                def group(q, m, end=2 * NJ):
                    for i in range(GG):
                        gather(q, m, i)
                        if m + 1 < end:
                            if i == 0:
                                turn(q, m + 1)
                            if i == 1:
                                linear(q, m + 1)
                            if i % 2:
                                project(q, m + 1, i // 2)
                        if m + 2 < end and i == GG // 2:
                            turn_back(q, m + 2)
                        if i:
                            score(q, m, i - 1)
                        elif m > 1:
                            score(q, m - 1, GG - 1)
                            if m == NJ:
                                add_linear(q)

                def body(q, last=False):
                    top = NJ - 1 if last else NJ
                    projected = QT if last else QT + AHEAD * GT
                    for m in range(1, top + 1):
                        group(q, m, NJ if last else 2 * NJ)
                    if last:
                        score(q, top, GG - 1)
                        add_linear(q)
                    turn_attention(q)
                    values(q, 0)
                    if not last:
                        score(q, top, GG - 1)
                    values(q, 1)
                    for gi in range(QG):
                        if gi + 2 < QG:
                            values(q, gi + 2)
                        scatter(q, gi)
                        if gi % HG == 1 and gi > HG:
                            turn_sums(q, gi // HG - 1, projected)
                        if gi % HG == 3 and gi > HG:
                            project_out(q, gi // HG - 1)
                    turn_sums(q, NH - 1, projected)
                    project_out(q, NH - 1)

                turn_back(0, 0)
                turn(0, 0)
                linear(0, 0)
                turn_back(0, 1)
                for t in range(GT):
                    project(0, 0, t)
                group(0, 0)
                score(0, 0, GG - 1)
                body(0)
                with pe.Fori(1, NQ - 1) as q:
                    body(q)
                body(NQ - 1, last=True)

            @block.scalar
            def _(act):
                def hi_halves(q, m):
                    act.wait_ge(sem["t2"], NJ * q + m + 1)
                    nc.scalar.activation(hT_hi[:, :, :], pT[:, :, :], ACT.Relu).then_inc(sem["h_hi"], 1)

                def split_hi(q, m, t):
                    act.wait_ge(sem["u_mm"], QT * q + GT * m + t + 1)
                    if m == NJ and t == 0:
                        wait(act, sem["moved"], 32 * q)
                    for i, r in enumerate((slice(0, NODES), slice(NODES, P))):
                        gi = 2 * t + i
                        nc.scalar.activation(keys[r, gi, :], pU[r, 0:D], ACT.Copy).then_inc(sem["s_hi"], 1)
                        nc.scalar.activation(vals[r, GG * m + gi, :], pU[r, D:2 * D], ACT.Copy).then_inc(sem["s_hi"], 1)

                def relu(q, m, i):
                    act.wait_ge(sem["z_mm"], QG * q + GG * m + i + 1)
                    nc.scalar.activation(r_hi[i % 2][:, :, :], pZ[i % 2][:, :, :], ACT.Relu).then_inc(sem["r_hi_done"], 1)

                def exponent(q):
                    act.wait_ge(sem["soft"], 8 * q + 4)
                    nc.scalar.activation(work[:, 1, :], work[:, 0, :], ACT.Exp).then_inc(sem["exp_done"], 1)

                def group(q, m, end=2 * NJ):
                    for i in range(GG):
                        relu(q, m, i)
                        if m + 1 < end:
                            if i == 0:
                                hi_halves(q, m + 1)
                            if i % 2:
                                split_hi(q, m + 1, i // 2)
                        if m == NJ and i == 4:
                            exponent(q)

                def body(q, last=False):
                    for m in range(1, NJ if last else NJ + 1):
                        group(q, m, NJ if last else 2 * NJ)
                    if last:
                        exponent(q)
                    act.wait_ge(sem["at_mm"], q + 1)
                    wait(act, sem["wv_done"], QG * q)
                    nc.scalar.activation(attn_T[:, :, :], pT[:, 0, :].rearrange("p (c r) -> p c r", c=EC), ACT.Copy)\
                        .then_inc(sem["attn_ready"], 1)

                    def halves_of_sums(h):
                        act.wait_ge(sem["yT_mm"], NH * q + h + 1)
                        nc.scalar.activation(yT_hi[h % 2], pYT, ACT.Copy).then_inc(sem["y_hi"], 1)

                    def rows_of_sums(t):
                        act.wait_ge(sem["scattered"], QG * q + TILE_GRAPHS * (t + 1))
                        if t >= 2:
                            act.wait_ge(sem["yT_mm"], NH * q + t // 2)
                        nc.scalar.activation(y_rows[t % 2][:, :], pY[t % 2], ACT.Copy).then_inc(sem["y_rows"], 1)

                    for gi in range(QG):
                        act.wait_ge(sem["wv_done"], QG * q + gi + 1)
                        if gi >= 2:
                            act.wait_ge(sem["scattered"], QG * q + gi - 1)
                        nc.scalar.activation(wv_hi[gi % 2], wv[gi % 2], ACT.Copy).then_inc(sem["wv_hi_done"], 1)
                        if gi >= 2 and gi % 2 == 0:
                            rows_of_sums(gi // 2 - 1)
                        if gi % HG == 2 and gi > HG:
                            halves_of_sums(gi // HG - 1)
                    rows_of_sums(QT - 1)
                    halves_of_sums(NH - 1)

                hi_halves(0, 0)
                for t in range(GT):
                    split_hi(0, 0, t)
                group(0, 0)
                body(0)
                with act.Fori(1, NQ - 1) as q:
                    body(q)
                body(NQ - 1, last=True)

            @block.vector
            def _(dve):
                V = nc.vector

                def add_x(q, m):
                    G = NJ * q + m
                    dve.wait_ge(sem["t1"], G + 1)
                    V.tensor_tensor(x1_group(G), quad(pTr), quad(xt[m % 2][:, :, :]), ALU.add).then_inc(sem["x1_done"], 1)
                    dve.wait_ge(sem["x1_done"], G + 1)
                    wait(dve, sem["rstd_ready"], G)
                    V.memset(ve[:, :], EPS)
                    for t in range(GT):
                        last = V.bn_stats(st[:, t, :], x1_group(G)[:, t // KD, t % KD, :])
                    last.then_inc(sem["stats"], 1)
                    dve.wait_ge(sem["stats"], G + 1)
                    V.memset(unused[:, :], 0.0)
                    for t in range(GT):
                        last = V.bn_aggr(mv[:, t, :], st[:, t, :])
                    last.then_inc(sem["moments"], 1)
                    dve.wait_ge(sem["moments"], G + 1)
                    V.tensor_tensor(ve[:, :], ve[:, :], mv[:, :, 1], ALU.add).then_inc(sem["var_eps"], 1)

                def normalise(q, m):
                    G = NJ * q + m
                    dve.wait_ge(sem["rstd_ready"], G + 1)
                    xn = hst[m % 2][:, :, :].rearrange("p k (a d) -> p (k a) d", d=D)
                    for t in range(GT):
                        last = V.tensor_scalar(xn[:, t, :], x1_group(G)[:, t // KD, t % KD, :], mv[:, t, 0:1],
                                               rstd[:, t:t + 1], ALU.subtract, ALU.mult)
                    last.then_inc(sem["normed"], 1)

                def lo_halves(q, m):
                    dve.wait_ge(sem["h_hi"], NJ * q + m + 1)
                    V.scalar_tensor_tensor(out=hT_lo[:, :, :], in0=pT[:, :, :], scalar=0.0, in1=f32(hT_hi[:, :, :]),
                                           op0=ALU.max, op1=ALU.subtract).then_inc(sem["h_lo"], 1)

                def split_lin(q, m):
                    G, cols = NJ * q + m, slice(GG * HEADS * m, GG * HEADS * (m + 1))
                    dve.wait_ge(sem["lin_mm"], G + 1)
                    if m == NJ:
                        wait(dve, sem["moved"], 32 * q)
                    part = pT[0:NODES, 0, 0:GG * HEADS]
                    V.tensor_copy(lin[0:NODES, cols], part).then_inc(sem["lin_part"], 1)
                    dve.wait_ge(sem["lin_part"], G + 1)
                    V.tensor_tensor(lin[NODES:P, cols], part, f32(lin[0:NODES, cols]), ALU.subtract).then_inc(sem["lin_done"], 1)

                def split_lo(q, m, t):
                    halves = (slice(0, NODES), slice(NODES, P))
                    dve.wait_ge(sem["s_hi"], 4 * (QT * q + GT * m + t + 1))
                    for i in range(2):
                        gi, own, other = 2 * t + i, halves[i], halves[1 - i]
                        V.tensor_tensor(keys[other, gi, :], pU[own, 0:D], f32(keys[own, gi, :]), ALU.subtract)
                        last = V.tensor_tensor(vals[other, GG * m + gi, :], pU[own, D:2 * D],
                                               f32(vals[own, GG * m + gi, :]), ALU.subtract)
                    last.then_inc(sem["s_lo"], 1)

                def relu_lo(q, m, i):
                    dve.wait_ge(sem["r_hi_done"], QG * q + GG * m + i + 1)
                    V.scalar_tensor_tensor(out=r_lo[i % 2][:, :, :], in0=pZ[i % 2][:, :, :], scalar=0.0,
                                           in1=f32(r_hi[i % 2][:, :, :]), op0=ALU.max,
                                           op1=ALU.subtract).then_inc(sem["r_lo_done"], 1)

                def softmax_step(q, n):
                    w = [work[:, i, :] for i in range(4)]
                    cut, same = tab["cut"], tab["same"]
                    if n == 0:
                        dve.wait_ge(sem["e_mm"], q + 1)
                        wait(dve, sem["wv_lo_done"], QG * q)
                        ins = V.tensor_tensor(w[0], pE, tab["log_w"][:, :], ALU.add)
                    if n == 1:
                        ins = V.tensor_tensor_scan(w[1], cut[:, 0:EDGES], w[0], 0.0, ALU.add, ALU.max)
                    if n == 2:
                        ins = V.tensor_tensor_scan(w[2][:, ::-1], cut[:, EDGES:0:-1], w[1][:, ::-1], 0.0, ALU.add, ALU.max)
                    if n == 3:
                        ins = V.tensor_tensor(w[0], w[0], w[2], ALU.subtract)
                    if n == 4:
                        dve.wait_ge(sem["exp_done"], q + 1)
                        ins = V.tensor_tensor_scan(w[2], same[:, 0:EDGES], w[1], 0.0, ALU.mult, ALU.add)
                    if n == 5:
                        ins = V.tensor_tensor_scan(w[3][:, ::-1], same[:, EDGES:0:-1], w[2][:, ::-1], 0.0, ALU.mult, ALU.max)
                    if n == 6:
                        ins = V.reciprocal(w[2], w[3])
                    if n == 7:
                        ins = V.tensor_tensor(w[0], w[1], w[2], ALU.mult)
                    ins.then_inc(sem["soft"], 1)
                    dve.wait_ge(sem["soft"], 8 * q + n + 1)

                SOFT_AT = {0: (0,), 1: (1,), 2: (2,), 3: (3,), 5: (4,), 6: (5, 6, 7)}

                def group(q, m, end=2 * NJ):
                    for i in range(GG):
                        relu_lo(q, m, i)
                        if m + 1 < end:
                            if i == 0:
                                lo_halves(q, m + 1)
                            if i == 1:
                                split_lin(q, m + 1)
                            if i % 2:
                                split_lo(q, m + 1, i // 2)
                        if m == NJ:
                            for n in SOFT_AT.get(i, ()):
                                softmax_step(q, n)
                        if m + 2 < end:
                            if i == GG // 2:
                                add_x(q, m + 2)
                            if i == GG // 2 + 1:
                                normalise(q, m + 2)

                def weigh(q, gi):
                    dve.wait_ge(sem["vg_mm"], QG * q + gi + 1)
                    if gi == 0:
                        dve.wait_ge(sem["attn_ready"], q + 1)
                    else:
                        wait(dve, sem["wv_lo_done"], QG * q + gi - 1)
                    shape = [P, EC, HEADS, DH]
                    V.tensor_tensor(wv[gi % 2].rearrange("p c (h d) -> p c h d", h=HEADS),
                                    pZ[gi % 2][:, :, :].rearrange("p k (a h d) -> p (k a) h d", h=HEADS, d=DH),
                                    attn_T[:, :, HEADS * gi:HEADS * (gi + 1)].unsqueeze(3).to_broadcast(shape),
                                    ALU.mult).then_inc(sem["wv_done"], 1)

                def body(q, last=False):
                    for m in range(1, NJ if last else NJ + 1):
                        group(q, m, NJ if last else 2 * NJ)
                    if last:
                        for n in range(8):
                            softmax_step(q, n)

                    def lo_of_sums(h):
                        dve.wait_ge(sem["y_hi"], NH * q + h + 1)
                        V.tensor_tensor(yT_lo[h % 2], pYT, f32(yT_hi[h % 2]),
                                        ALU.subtract).then_inc(sem["y_lo"], 1)

                    def add_out(h):
                        dve.wait_ge(sem["o_mm"], NH * q + h + 1)
                        part = HTg[:, h % 2, NJ * q + h // 2, :]
                        V.tensor_tensor(part, pU[:, :], part, ALU.add).then_inc(sem["x2_done"], 1)

                    weigh(q, 0)
                    weigh(q, 1)
                    for gi in range(QG):
                        dve.wait_ge(sem["wv_hi_done"], QG * q + gi + 1)
                        V.tensor_tensor(wv_lo[gi % 2], wv[gi % 2], f32(wv_hi[gi % 2]), ALU.subtract)\
                            .then_inc(sem["wv_lo_done"], 1)
                        if gi + 2 < QG:
                            weigh(q, gi + 2)
                        if gi % HG == 2 and gi > HG:
                            lo_of_sums(gi // HG - 1)
                        if gi % HG == 0 and gi > HG:
                            add_out(gi // HG - 2)
                    add_out(NH - 2)
                    lo_of_sums(NH - 1)
                    add_out(NH - 1)

                add_x(0, 0)
                normalise(0, 0)
                lo_halves(0, 0)
                split_lin(0, 0)
                add_x(0, 1)
                normalise(0, 1)
                for t in range(GT):
                    split_lo(0, 0, t)
                group(0, 0)
                body(0)
                with dve.Fori(1, NQ - 1) as q:
                    body(q)
                body(NQ - 1, last=True)


def attention_layer(core, a, x, x2, HT):
    with ExitStack() as ctx:
        sb, _ = allocator(core.nc, ctx)
        tab = {"ident": sb("t_ident", [P, P]), "both": sb("t_both", [P, EDGES], F32R), "dst": sb("t_dst", [P, EDGES], F32R),
               "src": sb("t_src", [P, TILE_GRAPHS, EC, P], F32R), "sign": sb("t_sign", [P, KD, 2 * P - HEADS], F32R),
               "log_w": sb("t_log_w", [P, EDGES]),
               "wqv_hi": sb("t_wqv_hi", [P, KD, 2 * D], F32R), "wqv_lo": sb("t_wqv_lo", [P, KD, 2 * D], F32R),
               "wo_hi": sb("t_wo_hi", [P, KD, D], F32R), "wo_lo": sb("t_wo_lo", [P, KD, D], F32R),
               "wl_hi": sb("t_wl_hi", [P, KD, HEADS], F32R), "wl_lo": sb("t_wl_lo", [P, KD, HEADS], F32R)}
        for n in ("same", "cut"):
            tab[n] = sb("t_" + n, [P, EDGES + 1])
        edge_tables(core, a, tab)
        edge_attention(core, x, x2, tab, HT)


def conv_first(core, a, x2, H1, st1, W2):
    nc = core.nc
    NI = NG // 2
    with ExitStack() as ctx:
        sb, ps = allocator(nc, ctx)
        mhalf = sb("d_mhalf", [P, GT])
        an_t, an = sb("d_an_t", [NODES, NODES]), sb("d_an", [NODES, NODES])
        eye = sb("d_eye", [P, P])
        both, diag = sb("d_both", [NODES, NODES]), sb("d_diag", [NODES, NODES])
        ones = sb("d_ones", [NODES, P])
        deg, dinv, dcol = sb("d_deg", [P, NODES]), sb("d_dinv", [P, NODES]), sb("d_dcol", [P, 1])
        pick = sb("d_pick", [P, NODES])
        hat = sb("d_hat", [P, P])
        an_t2 = sb("d_an_t2", [P, NODES])
        eye2 = sb("d_eye2", [P, NODES])
        hat_hi, hat_lo = sb("d_hat_hi", [P, P], F32R), sb("d_hat_lo", [P, P], F32R)
        w1 = sb("d_w1", [P, KD, HID2])
        w1_hi, w1_lo = sb("d_w1_hi", [P, KD, HID2], F32R), sb("d_w1_lo", [P, KD, HID2], F32R)
        w2 = sb("d_w2", [P, KH, D])
        b1 = sb("d_b1", [P, KH])
        xt = [sb(f"d_xt{b}", [P, GT, D]) for b in range(2)]
        st, mv, ve, rstd = sb("d_st", [P, GT, 6]), sb("d_mv", [P, GT, 2]), sb("d_ve", [P, GT]), sb("d_rstd", [P, GT])
        h_hi = [sb(f"d_hhi{b}", [P, GT, D], F32R) for b in range(2)]
        h_lo = [sb(f"d_hlo{b}", [P, GT, D], F32R) for b in range(2)]
        g_hi = [sb(f"d_ghi{b}", [P, KD, GROWS], F32R) for b in range(2)]
        g_lo = [sb(f"d_glo{b}", [P, KD, GROWS], F32R) for b in range(2)]
        pA = [ps(f"d_pA{b}", [P, KD, GROWS]) for b in range(2)]
        pW = ps("d_pW", [P, KH, GROWS])
        names = ("consts half_set step deg_ready deg_mm root_ready hat_ready stats moments var_eps rstd_ready normed "
                 "h_hi_done h_lo_done agg_mm g_hi_done g_lo_done w1_mm h1_done").split()
        sem = {n: core.sem("d_" + n) for n in names}
        landed = [core.sem(f"d_landed{b}") for b in range(2)]
        loads = [(eye[:, :], a["ident"]), (an_t[:, :], a["adj_t"]), (an[:, :], a["adj"]), (w1[:, :, :], a["w1"]),
                 (w2[:, :, :], a["w2"]), (b1[:, :], a["b1"])]
        for g in range(TILE_GRAPHS):
            r = slice(g * NODES, (g + 1) * NODES)
            loads += [(an_t2[r, :], a["adj_t"]), (eye2[r, :], a["ident"][0:NODES, 0:NODES])]
        H1g = H1.rearrange("p k (g c) -> p k g c", c=GROWS)

        with nc.Block() as block:
            @block.sync
            def _(sp):
                for t, src in loads:
                    sp.dma_start(t, src).then_inc(sem["consts"], 16)

                def body(it):
                    for b in range(2):
                        wait(sp, sem["h_lo_done"], 2 * it + b - 1)
                        sp.dma_start(xt[b][:, :, :], x2[2 * it + b]).then_inc(landed[b], 16)

                peeled(sp, NI, body)

            @block.gpsimd
            def _(pool):
                nc.gpsimd.memset(mhalf[:, :], -0.5).then_inc(sem["half_set"], 1)
                pool.wait_ge(sem["half_set"], 1)
                pool.wait_ge(sem["deg_ready"], 1)
                nc.gpsimd.tensor_tensor(dinv[:, :], deg[:, :], mhalf[:, 0:1].to_broadcast([P, NODES]), ALU.pow)\
                    .then_inc(sem["root_ready"], 1)
                with pool.Fori(0, NG) as g:
                    pool.wait_ge(sem["var_eps"], g + 1)
                    nc.gpsimd.tensor_tensor(rstd[:, :], ve[:, :], mhalf[:, :], ALU.pow).then_inc(sem["rstd_ready"], 1)

            @block.tensor
            def _(pe):
                pe.wait_ge(sem["step"], 6)
                nc.tensor.matmul(pA[0][:, 0, 0:NODES], ones[:, :], both[:, :], start=True, stop=True).then_inc(sem["deg_mm"], 1)
                pe.wait_ge(sem["hat_ready"], 1)

                def aggregate(g, b):
                    pe.wait_ge(sem["h_lo_done"], g + 1)
                    pe.wait_ge(sem["h_hi_done"], g + 1)
                    for k in range(KD):
                        c = slice(k * P, (k + 1) * P)
                        for t in range(GT):
                            last = mm3(nc, pA[b][:, k, t * P:(t + 1) * P], h_hi[b][:, t, c], h_lo[b][:, t, c],
                                       hat_hi[:, :], hat_lo[:, :], True, True)
                    last.then_inc(sem["agg_mm"], 1)

                def first(g, b):
                    pe.wait_ge(sem["g_hi_done"], g + 1)
                    pe.wait_ge(sem["g_lo_done"], g + 1)
                    for m in range(KH):
                        wait(pe, sem["h1_done"], KH * (g - 1) + m + 1)
                        c = slice(m * P, (m + 1) * P)
                        for k in range(KD):
                            last = mm3(nc, pW[:, m, :], w1_hi[:, k, c], w1_lo[:, k, c], g_hi[b][:, k, :], g_lo[b][:, k, :],
                                       k == 0, k == KD - 1)
                        last.then_inc(sem["w1_mm"], 1)

                def body(it):
                    for b in range(2):
                        g = 2 * it + b
                        aggregate(g, b)
                        if not (isinstance(g, int) and g == 0):
                            first(g - 1, 1 - b)

                peeled(pe, NI, body)
                first(NG - 1, 1)

            @block.scalar
            def _(act):
                act.wait_ge(sem["consts"], 16 * len(loads))

                def keep(g):
                    for m in range(KH):
                        act.wait_ge(sem["w1_mm"], KH * g + m + 1)
                        nc.scalar.activation(H1g[:, m, g, :], pW[:, m, :], ACT.Identity, bias=b1[:, m:m + 1])\
                            .then_inc(sem["h1_done"], 1)

                def body(it):
                    for b in range(2):
                        g = 2 * it + b
                        act.wait_ge(sem["normed"], g + 1)
                        wait(act, sem["agg_mm"], g - 1)
                        nc.scalar.activation(h_hi[b][:, :, :], xt[b][:, :, :], ACT.Relu).then_inc(sem["h_hi_done"], 1)
                        act.wait_ge(sem["agg_mm"], g + 1)
                        nc.scalar.activation(g_hi[b][:, :, :], pA[b][:, :, :], ACT.Copy).then_inc(sem["g_hi_done"], 1)
                        if not (isinstance(g, int) and g == 0):
                            keep(g - 1)

                peeled(act, NI, body)
                keep(NG - 1)

            @block.vector
            def _(dve):
                V = nc.vector
                link = Chain(dve, sem["step"])
                dve.wait_ge(sem["consts"], 16 * len(loads))
                link(V.tensor_tensor(an_t[:, :], an_t[:, :], eye[0:NODES, 0:NODES], ALU.add))
                link(V.tensor_tensor(an[:, :], an[:, :], eye[0:NODES, 0:NODES], ALU.add))
                link(V.tensor_tensor(diag[:, :], an[:, :], eye[0:NODES, 0:NODES], ALU.mult))
                link(V.tensor_tensor(both[:, :], an[:, :], an_t[:, :], ALU.add))
                link(V.tensor_tensor(both[:, :], both[:, :], diag[:, :], ALU.subtract))
                link(V.memset(ones[:, :], 1.0))
                for raw, hi, lo in ((w1, w1_hi, w1_lo), (w2, W2[0], W2[1])):
                    link(V.tensor_copy(hi[:, :, :], raw[:, :, :]))
                    link(V.tensor_tensor(lo[:, :, :], raw[:, :, :], f32(hi[:, :, :]), ALU.subtract))
                dve.wait_ge(sem["deg_mm"], 1)
                V.tensor_copy(deg[:, :], pA[0][:, 0, 0:NODES]).then_inc(sem["deg_ready"], 1)
                dve.wait_ge(sem["root_ready"], 1)
                link(V.tensor_tensor(pick[:, :], dinv[:, :], eye2[:, :], ALU.mult))
                link(V.tensor_reduce(dcol[:, :], pick[:, :], AX.X, ALU.add))
                link(V.tensor_tensor(an_t2[:, :], an_t2[:, :], eye2[:, :], ALU.add))
                link(V.memset(hat[:, :], 0.0))
                for g in range(TILE_GRAPHS):
                    r = slice(g * NODES, (g + 1) * NODES)
                    link(V.scalar_tensor_tensor(out=hat[r, r], in0=an_t2[r, :], scalar=dcol[r, 0:1], in1=dinv[r, :],
                                                op0=ALU.mult, op1=ALU.mult))
                link(V.tensor_copy(hat_hi[:, :], hat[:, :]))
                V.tensor_tensor(hat_lo[:, :], hat[:, :], f32(hat_hi[:, :]), ALU.subtract).then_inc(sem["hat_ready"], 1)

                def norm(g, b):
                    dve.wait_ge(landed[b], 8 * (g - b) + 16)
                    for t in range(GT):
                        last = V.bn_stats(st[:, t, :], xt[b][:, t, :])
                    last.then_inc(sem["stats"], 1)
                    dve.wait_ge(sem["stats"], g + 1)
                    wait(dve, sem["rstd_ready"], g)
                    V.memset(ve[:, :], EPS)
                    for t in range(GT):
                        last = V.bn_aggr(mv[:, t, :], st[:, t, :])
                    last.then_inc(sem["moments"], 1)
                    dve.wait_ge(sem["moments"], g + 1)
                    V.tensor_tensor(ve[:, :], ve[:, :], mv[:, :, 1], ALU.add).then_inc(sem["var_eps"], 1)
                    dve.wait_ge(sem["rstd_ready"], g + 1)
                    for t in range(GT):
                        last = V.tensor_scalar(xt[b][:, t, :], xt[b][:, t, :], mv[:, t, 0:1], rstd[:, t:t + 1],
                                               ALU.subtract, ALU.mult)
                    last.then_inc(sem["normed"], 1)
                    dve.wait_ge(sem["h_hi_done"], g + 1)
                    V.scalar_tensor_tensor(out=h_lo[b][:, :, :], in0=xt[b][:, :, :], scalar=0.0, in1=f32(h_hi[b][:, :, :]),
                                           op0=ALU.max, op1=ALU.subtract).then_inc(sem["h_lo_done"], 1)

                def measure(g):
                    for m in range(KH):
                        dve.wait_ge(sem["h1_done"], KH * g + m + 1)
                        V.bn_stats(st1[:, m, g, :], H1g[:, m, g, :])

                norm(0, 0)

                def body(it):
                    for b in range(2):
                        g = 2 * it + b
                        end = isinstance(g, int) and g == NG - 1
                        dve.wait_ge(sem["g_hi_done"], g + 1)
                        V.tensor_tensor(g_lo[b][:, :, :], pA[b][:, :, :], f32(g_hi[b][:, :, :]), ALU.subtract)\
                            .then_inc(sem["g_lo_done"], 1)
                        if not end:
                            norm(g + 1, 1 - b)
                        if not (isinstance(g, int) and g == 0):
                            measure(g - 1)

                both_ends(dve, NI, body)
                measure(NG - 1)


def conv_second(core, a, H1, st1, st2, W2):
    nc = core.nc
    NI = NG // 2
    with ExitStack() as ctx:
        sb, ps = allocator(nc, ctx)
        mhalf = sb("f_mhalf", [P, KH])
        g1, be1, b2 = sb("f_g1", [P, KH]), sb("f_be1", [P, KH]), sb("f_b2", [P, KD])
        mv, ve, rstd = sb("f_mv", [P, KH, 2]), sb("f_ve", [P, KH]), sb("f_rstd", [P, KH])
        scale, shift, moved = sb("f_scale", [P, KH]), sb("f_shift", [P, KH]), sb("f_moved", [P, KH])
        r = [sb(f"f_r{b}", [P, KH, GROWS]) for b in range(2)]
        r_hi = [sb(f"f_rhi{b}", [P, KH, GROWS], F32R) for b in range(2)]
        r_lo = [sb(f"f_rlo{b}", [P, KH, GROWS], F32R) for b in range(2)]
        pO = [ps(f"f_pO{b}", [P, KD, GROWS]) for b in range(2)]
        names = "consts half_set step ve_ready rstd_ready affine_ready relu_done hi_done lo_done o_mm o_done".split()
        sem = {n: core.sem("f_" + n) for n in names}
        H1g = H1.rearrange("p k (g c) -> p k g c", c=GROWS)
        loads = [(g1, a["g1"]), (be1, a["be1"]), (b2, a["b2"])]
        with nc.Block() as block:
            @block.sync
            def _(sp):
                for t, src in loads:
                    sp.dma_start(t[:, :], src).then_inc(sem["consts"], 16)

            @block.gpsimd
            def _(pool):
                nc.gpsimd.memset(mhalf[:, :], -0.5).then_inc(sem["half_set"], 1)
                pool.wait_ge(sem["half_set"], 1)
                pool.wait_ge(sem["ve_ready"], 1)
                nc.gpsimd.tensor_tensor(rstd[:, :], ve[:, :], mhalf[:, :], ALU.pow).then_inc(sem["rstd_ready"], 1)

            @block.vector
            def _(dve):
                V = nc.vector
                link = Chain(dve, sem["step"])
                dve.wait_ge(sem["consts"], 16 * len(loads))
                for m in range(KH):
                    link(V.bn_aggr(mv[:, m, :], st1[:, m, :, :].rearrange("p g s -> p (g s)")))
                V.tensor_scalar(ve[:, :], mv[:, :, 1], EPS, None, ALU.add).then_inc(sem["ve_ready"], 1)
                dve.wait_ge(sem["rstd_ready"], 1)
                link(V.tensor_tensor(scale[:, :], g1[:, :], rstd[:, :], ALU.mult))
                link(V.tensor_tensor(moved[:, :], mv[:, :, 0], scale[:, :], ALU.mult))
                V.tensor_tensor(shift[:, :], be1[:, :], moved[:, :], ALU.subtract).then_inc(sem["affine_ready"], 1)

                def split(g, b):
                    dve.wait_ge(sem["relu_done"], g + 1)
                    wait(dve, sem["o_mm"], g - 1)
                    V.tensor_copy(r_hi[b][:, :, :], r[b][:, :, :]).then_inc(sem["hi_done"], 1)
                    dve.wait_ge(sem["hi_done"], g + 1)
                    V.tensor_tensor(r_lo[b][:, :, :], r[b][:, :, :], f32(r_hi[b][:, :, :]), ALU.subtract)\
                        .then_inc(sem["lo_done"], 1)

                def measure(g, b):
                    dve.wait_ge(sem["o_mm"], g + 1)
                    for m in range(KD):
                        last = V.tensor_scalar(H1g[:, m, g, :], pO[b][:, m, :], b2[:, m:m + 1], None, ALU.add)
                    last.then_inc(sem["o_done"], 1)
                    dve.wait_ge(sem["o_done"], g + 1)
                    for m in range(KD):
                        V.bn_stats(st2[:, m, g, :], H1g[:, m, g, :])

                split(0, 0)

                def body(it):
                    for b in range(2):
                        g = 2 * it + b
                        if not (isinstance(g, int) and g == NG - 1):
                            split(g + 1, 1 - b)
                        measure(g, b)

                both_ends(dve, NI, body)

            @block.scalar
            def _(act):
                act.wait_ge(sem["affine_ready"], 1)

                def relu(g, b):
                    wait(act, sem["lo_done"], g - 1)
                    for m in range(KH):
                        last = nc.scalar.activation(r[b][:, m, :], H1g[:, m, g, :], ACT.Relu, bias=shift[:, m:m + 1],
                                                    scale=scale[:, m:m + 1])
                    last.then_inc(sem["relu_done"], 1)

                relu(0, 0)

                def body(it):
                    for b in range(2):
                        g = 2 * it + b
                        if not (isinstance(g, int) and g == NG - 1):
                            relu(g + 1, 1 - b)

                both_ends(act, NI, body)

            @block.tensor
            def _(pe):
                def body(it):
                    for b in range(2):
                        g = 2 * it + b
                        pe.wait_ge(sem["lo_done"], g + 1)
                        wait(pe, sem["o_done"], g - 1)
                        for m in range(KD):
                            c = slice(m * P, (m + 1) * P)
                            for k in range(KH):
                                last = mm3(nc, pO[b][:, m, :], W2[0][:, k, c], W2[1][:, k, c], r_hi[b][:, k, :],
                                           r_lo[b][:, k, :], k == 0, k == KH - 1)
                        last.then_inc(sem["o_mm"], 1)

                peeled(pe, NI, body)


def dense_attention(core, a, x2, out, H1, st2):
    nc = core.nc
    NI = NG // 2
    WE = D + 2
    with ExitStack() as ctx:
        sb, ps = allocator(nc, ctx)
        mhalf = sb("e_mhalf", [P, GT])
        ident = sb("e_ident", [P, P])
        g2, be2 = sb("e_g2", [P, KD]), sb("e_be2", [P, KD])
        mv2, ve2, rstd2 = sb("e_mv2", [P, KD, 2]), sb("e_ve2", [P, KD]), sb("e_rstd2", [P, KD])
        scale, shift, moved = sb("e_scale", [P, KD]), sb("e_shift", [P, KD]), sb("e_moved", [P, KD])
        w_ext = sb("e_w_ext", [P, KD, WE])
        w_hi, w_lo = sb("e_w_hi", [P, KD, WE], F32R), sb("e_w_lo", [P, KD, WE], F32R)
        a_hi, a_lo = sb("e_a_hi", [P, KD, P], F32R), sb("e_a_lo", [P, KD, P], F32R)
        a_row = sb("e_a_row", [P, 2, D])
        prod = sb("e_prod", [P, KD, 2, D])
        adj2, mask = sb("e_adj2", [P, NODES]), sb("e_mask", [P, NODES])
        y = sb("e_y", [P, KD, GROWS])
        xt = [sb(f"e_xt{b}", [P, GT, D]) for b in range(2)]
        xn = sb("e_xn", [P, GT, D])
        st, mv, ve, rstd = sb("e_st", [P, GT, 6]), sb("e_mv", [P, GT, 2]), sb("e_ve", [P, GT]), sb("e_rstd", [P, GT])
        hT_hi, hT_lo = sb("e_hThi", [P, KD, GROWS], F32R), sb("e_hTlo", [P, KD, GROWS], F32R)
        v_hi, v_lo = sb("e_vhi", [P, GT, D], F32R), sb("e_vlo", [P, GT, D], F32R)
        s1 = sb("e_s1", [P, GT])
        e = sb("e_e", [P, GT, NODES])
        top, total, inv = sb("e_top", [P, GT]), sb("e_total", [P, GT]), sb("e_inv", [P, GT])
        prob = sb("e_prob", [P, GT, P])
        p_hi, p_lo = sb("e_phi", [P, GT, P], F32R), sb("e_plo", [P, GT, P], F32R)
        pT = ps("e_pT", [P, KD, GROWS])
        pW = ps("e_pW", [P, GT, GROWS])
        pS = ps("e_pS", [P, GT, P])
        pTr = pT[:, :, :].rearrange("p k (a d) -> p (k a) d", d=D)
        pO = pW[:, 0:2, :].rearrange("p k (a d) -> p (k a) d", d=D)
        names = ("consts half_set step ve2_ready rstd2_ready ready y_done t1 x3_done stats moments var_eps "
                 "rstd_ready normed t2 h_hi h_lo w_mm s_mm v_hi_done soft exp_done prob_done t3 p_hi_done "
                 "p_lo_done o_mm out_done").split()
        sem = {n: core.sem("e_" + n) for n in names}
        landed = [core.sem(f"e_landed{b}") for b in range(2)]
        stored = [core.sem(f"e_stored{b}") for b in range(2)]
        H1g = H1.rearrange("p k (g c) -> p k g c", c=GROWS)
        loads = [(ident[:, :], a["ident"]), (g2[:, :], a["g2"]), (be2[:, :], a["be2"]), (w_ext[:, :, 0:D], a["w3"]),
                 (a_row[:, :, :], a["a3"].rearrange("p (h d) -> p h d", h=2))]
        for g in range(TILE_GRAPHS):
            loads.append((adj2[g * NODES:(g + 1) * NODES, :], a["adj"]))
        SOFT = 9

        with nc.Block() as block:
            @block.sync
            def _(sp):
                for t, src in loads:
                    sp.dma_start(t, src).then_inc(sem["consts"], 16)

                for b in range(2):
                    sp.dma_start(xt[b][:, :, :], x2[b]).then_inc(landed[b], 16)

                def body(it):
                    for b in range(2):
                        g = 2 * it + b
                        sp.wait_ge(sem["out_done"], g + 1)
                        sp.dma_start(out[g], xt[b][:, :, :]).then_inc(stored[b], 16)
                        if not (isinstance(it, int) and it == NI - 1):
                            sp.wait_ge(stored[b], 16 * it + 16)
                            sp.dma_start(xt[b][:, :, :], x2[g + 2]).then_inc(landed[b], 16)

                both_ends(sp, NI, body)
                for b in range(2):
                    sp.wait_ge(stored[b], 16 * NI)

            @block.gpsimd
            def _(pool):
                nc.gpsimd.memset(mhalf[:, :], -0.5).then_inc(sem["half_set"], 1)
                pool.wait_ge(sem["half_set"], 1)
                pool.wait_ge(sem["ve2_ready"], 1)
                nc.gpsimd.tensor_tensor(rstd2[:, :], ve2[:, :], mhalf[:, 0:KD], ALU.pow).then_inc(sem["rstd2_ready"], 1)
                with pool.Fori(0, NG) as g:
                    pool.wait_ge(sem["var_eps"], g + 1)
                    nc.gpsimd.tensor_tensor(rstd[:, :], ve[:, :], mhalf[:, :], ALU.pow).then_inc(sem["rstd_ready"], 1)

            @block.tensor
            def _(pe):
                def rows(g):
                    pe.wait_ge(sem["y_done"], g + 1)
                    for t in range(GT):
                        for k in range(KD):
                            last = nc.tensor.transpose(pTr[:, t, k * P:(k + 1) * P], y[:, k, t * P:(t + 1) * P], ident[:, :])
                    last.then_inc(sem["t1"], 1)
                    pe.wait_ge(sem["normed"], g + 1)
                    for t in range(GT):
                        for k in range(KD):
                            last = nc.tensor.transpose(pT[:, k, t * P:(t + 1) * P], xn[:, t, k * P:(k + 1) * P], ident[:, :])
                    last.then_inc(sem["t2"], 1)

                def project(g):
                    pe.wait_ge(sem["h_lo"], g + 1)
                    pe.wait_ge(sem["h_hi"], g + 1)
                    wait(pe, sem["out_done"], g)
                    for t in range(GT):
                        c = slice(t * P, (t + 1) * P)
                        for k in range(KD):
                            last = mm3(nc, pW[:, t, 0:WE], hT_hi[:, k, c], hT_lo[:, k, c], w_hi[:, k, :], w_lo[:, k, :],
                                       k == 0, k == KD - 1)
                    last.then_inc(sem["w_mm"], 1)
                    for k in range(KD):
                        last = mm3(nc, pS[:, :, :].rearrange("p t r -> p (t r)"), a_hi[:, k, :], a_lo[:, k, :],
                                   hT_hi[:, k, :], hT_lo[:, k, :], k == 0, k == KD - 1)
                    last.then_inc(sem["s_mm"], 1)

                def attend(g):
                    pe.wait_ge(sem["prob_done"], g + 1)
                    for t in range(GT):
                        last = nc.tensor.transpose(pT[:, 0, t * P:(t + 1) * P], prob[:, t, :], ident[:, :])
                    last.then_inc(sem["t3"], 1)
                    pe.wait_ge(sem["p_hi_done"], g + 1)
                    pe.wait_ge(sem["p_lo_done"], g + 1)
                    for t in range(GT):
                        last = mm3(nc, pO[:, t, :], p_hi[:, t, :], p_lo[:, t, :], v_hi[:, t, :], v_lo[:, t, :], True, True)
                    last.then_inc(sem["o_mm"], 1)

                pe.wait_ge(sem["consts"], 16 * len(loads))
                rows(0)
                pe.wait_ge(sem["ready"], 1)

                def body(it):
                    for b in range(2):
                        g = 2 * it + b
                        project(g)
                        if not (isinstance(g, int) and g == NG - 1):
                            rows(g + 1)
                            pe.wait_ge(sem["h_lo"], g + 2)
                        attend(g)

                both_ends(pe, NI, body)

            @block.scalar
            def _(act):
                def second_norm(g):
                    wait(act, sem["t1"], g)
                    for k in range(KD):
                        last = nc.scalar.activation(y[:, k, :], H1g[:, k, g, :], ACT.Identity, bias=shift[:, k:k + 1],
                                                    scale=scale[:, k:k + 1])
                    last.then_inc(sem["y_done"], 1)

                def relu(g):
                    act.wait_ge(sem["t2"], g + 1)
                    nc.scalar.activation(hT_hi[:, :, :], pT[:, :, :], ACT.Relu).then_inc(sem["h_hi"], 1)

                act.wait_ge(sem["step"], KD + 3)
                second_norm(0)
                relu(0)

                def body(it):
                    for b in range(2):
                        g = 2 * it + b
                        end = isinstance(g, int) and g == NG - 1
                        act.wait_ge(sem["w_mm"], g + 1)
                        nc.scalar.activation(v_hi[:, :, :], pW[:, :, 0:D], ACT.Copy).then_inc(sem["v_hi_done"], 1)
                        if not end:
                            second_norm(g + 1)
                        act.wait_ge(sem["soft"], SOFT * g + 6)
                        nc.scalar.activation(e[:, :, :], e[:, :, :], ACT.Exp).then_inc(sem["exp_done"], 1)
                        if not end:
                            relu(g + 1)
                        act.wait_ge(sem["t3"], g + 1)
                        nc.scalar.activation(p_hi[:, :, :], pT[:, 0, :].rearrange("p (t r) -> p t r", t=GT), ACT.Copy)\
                            .then_inc(sem["p_hi_done"], 1)

                both_ends(act, NI, body)

            @block.vector
            def _(dve):
                V = nc.vector
                link = Chain(dve, sem["step"])
                dve.wait_ge(sem["consts"], 16 * len(loads))
                for m in range(KD):
                    link(V.bn_aggr(mv2[:, m, :], st2[:, m, :, :].rearrange("p g s -> p (g s)")))
                V.tensor_scalar(ve2[:, :], mv2[:, :, 1], EPS, None, ALU.add).then_inc(sem["ve2_ready"], 1)
                dve.wait_ge(sem["rstd2_ready"], 1)
                link(V.tensor_tensor(scale[:, :], g2[:, :], rstd2[:, :], ALU.mult))
                link(V.tensor_tensor(moved[:, :], mv2[:, :, 0], scale[:, :], ALU.mult))
                link(V.tensor_tensor(shift[:, :], be2[:, :], moved[:, :], ALU.subtract))
                for i in range(2):
                    link(V.tensor_tensor(prod[:, :, i, :], w_ext[:, :, 0:D],
                                         a_row[:, i, :].unsqueeze(1).to_broadcast([P, KD, D]), ALU.mult))
                    link(V.tensor_reduce(w_ext[:, :, D + i:D + i + 1], prod[:, :, i, :], AX.X, ALU.add))
                link(V.tensor_copy(w_hi[:, :, :], w_ext[:, :, :]))
                link(V.tensor_tensor(w_lo[:, :, :], w_ext[:, :, :], f32(w_hi[:, :, :]), ALU.subtract))
                link(V.tensor_copy(a_hi[:, :, :], f32(w_hi[:, :, D + 1:D + 2]).to_broadcast([P, KD, P])))
                link(V.tensor_copy(a_lo[:, :, :], f32(w_lo[:, :, D + 1:D + 2]).to_broadcast([P, KD, P])))
                link(V.tensor_scalar(mask[:, :], adj2[:, :], 0.0, -BIG, ALU.is_equal, ALU.mult))
                V.memset(prob[:, :, :], 0.0).then_inc(sem["ready"], 1)

                def norm(g, b):
                    dve.wait_ge(sem["t1"], g + 1)
                    dve.wait_ge(landed[b], 8 * (g - b) + 16)
                    V.tensor_tensor(xt[b][:, :, :], pTr, xt[b][:, :, :], ALU.add).then_inc(sem["x3_done"], 1)
                    dve.wait_ge(sem["x3_done"], g + 1)
                    for t in range(GT):
                        last = V.bn_stats(st[:, t, :], xt[b][:, t, :])
                    last.then_inc(sem["stats"], 1)
                    dve.wait_ge(sem["stats"], g + 1)
                    wait(dve, sem["rstd_ready"], g)
                    V.memset(ve[:, :], EPS)
                    for t in range(GT):
                        last = V.bn_aggr(mv[:, t, :], st[:, t, :])
                    last.then_inc(sem["moments"], 1)
                    dve.wait_ge(sem["moments"], g + 1)
                    V.tensor_tensor(ve[:, :], ve[:, :], mv[:, :, 1], ALU.add).then_inc(sem["var_eps"], 1)
                    dve.wait_ge(sem["rstd_ready"], g + 1)
                    for t in range(GT):
                        last = V.tensor_scalar(xn[:, t, :], xt[b][:, t, :], mv[:, t, 0:1], rstd[:, t:t + 1],
                                               ALU.subtract, ALU.mult)
                    last.then_inc(sem["normed"], 1)
                    dve.wait_ge(sem["h_hi"], g + 1)
                    V.scalar_tensor_tensor(out=hT_lo[:, :, :], in0=pT[:, :, :], scalar=0.0, in1=f32(hT_hi[:, :, :]),
                                           op0=ALU.max, op1=ALU.subtract).then_inc(sem["h_lo"], 1)

                def softmax(g):
                    n = [0]

                    def step(ins):
                        n[0] += 1
                        ins.then_inc(sem["soft"], 1)
                        dve.wait_ge(sem["soft"], SOFT * g + n[0])

                    def over(col):
                        return col[:, :].unsqueeze(2).to_broadcast([P, GT, NODES])

                    dve.wait_ge(sem["v_hi_done"], g + 1)
                    step(V.tensor_copy(s1[:, :], pW[:, :, D]))
                    dve.wait_ge(sem["s_mm"], g + 1)
                    for h in range(2):
                        r = slice(h * NODES, (h + 1) * NODES)
                        ins = V.tensor_tensor(e[r, :, :], pS[r, :, r], s1[r, :].unsqueeze(2).to_broadcast([NODES, GT, NODES]),
                                              ALU.add)
                    step(ins)
                    step(V.scalar_tensor_tensor(out=e[:, :, :], in0=e[:, :, :], scalar=LEAK, in1=e[:, :, :],
                                                op0=ALU.mult, op1=ALU.max))
                    step(V.tensor_tensor(e[:, :, :], e[:, :, :], mask[:, :].unsqueeze(1).to_broadcast([P, GT, NODES]), ALU.add))
                    step(V.tensor_reduce(top[:, :], e[:, :, :], AX.X, ALU.max))
                    step(V.tensor_tensor(e[:, :, :], e[:, :, :], over(top), ALU.subtract))
                    dve.wait_ge(sem["v_hi_done"], g + 1)
                    V.tensor_tensor(v_lo[:, :, :], pW[:, :, 0:D], f32(v_hi[:, :, :]), ALU.subtract)
                    dve.wait_ge(sem["exp_done"], g + 1)
                    step(V.tensor_reduce(total[:, :], e[:, :, :], AX.X, ALU.add))
                    step(V.reciprocal(inv[:, :], total[:, :]))
                    for h in range(2):
                        r = slice(h * NODES, (h + 1) * NODES)
                        ins = V.tensor_tensor(prob[r, :, r], e[r, :, :], inv[r, :].unsqueeze(2).to_broadcast([NODES, GT, NODES]),
                                              ALU.mult)
                        if h == 0:
                            step(ins)
                    ins.then_inc(sem["prob_done"], 1)

                norm(0, 0)

                def body(it):
                    for b in range(2):
                        g = 2 * it + b
                        softmax(g)
                        if not (isinstance(g, int) and g == NG - 1):
                            norm(g + 1, 1 - b)
                        dve.wait_ge(sem["p_hi_done"], g + 1)
                        V.tensor_tensor(p_lo[:, :, :], pT[:, 0, :].rearrange("p (t r) -> p t r", t=GT), f32(p_hi[:, :, :]),
                                        ALU.subtract).then_inc(sem["p_lo_done"], 1)
                        dve.wait_ge(sem["o_mm"], g + 1)
                        V.tensor_tensor(xt[b][:, :, :], pO, xt[b][:, :, :], ALU.add).then_inc(sem["out_done"], 1)

                both_ends(dve, NI, body)


def later_layers(core, a, x2, out):
    with ExitStack() as ctx:
        sb, _ = allocator(core.nc, ctx)
        H1 = sb("H1", [P, KH, ROWS])[:, :, :]
        st1, st2 = sb("st1", [P, KH, NG, 6]), sb("st2", [P, KD, NG, 6])
        with ExitStack() as inner:
            sb2, _ = allocator(core.nc, inner)
            W2 = [sb2(f"w2_{n}", [P, KH, D], F32R) for n in ("hi", "lo")]
            conv_first(core, a, x2, H1, st1, W2)
            conv_second(core, a, H1, st1, st2, W2)
        dense_attention(core, a, x2, out, H1, st2)


def build(nc, args):
    with ExitStack() as ctx:
        core = Core(nc, ctx)

        def groups(rows):
            return rows.rearrange("(g t p) d -> g p t d", t=GT, p=P)

        x = groups(args["x"].rearrange("b n d -> (b n) d"))
        out = groups(args["out"].rearrange("b n d -> (b n) d"))
        x2 = groups(nc.dram_tensor("x2_scratch", [ROWS, D], F32).ap())
        with ExitStack() as first:
            HT = first.enter_context(nc.sbuf_tensor("HT", [P, KD, ROWS], F32))[:, :, :]
            gcn_phase(core, x, args["gcn_w"], args["gcn_b"], args["adj_t"], args["ident"], HT)
            lstm_phase(core, args["wih"], args["whh"], args["bih"], args["bhh"], HT)
            attention_layer(core, args, x, x2, HT)
        later_layers(core, args, x2, out)


def layouts(inp):
    import numpy as np

    def chunks(w):
        return np.ascontiguousarray(w.reshape(-1, P, w.shape[1]).transpose(1, 0, 2))

    def alike(v):
        return np.ascontiguousarray(np.broadcast_to(v.reshape(1, -1), (P, v.size)))

    def columns(v):
        return np.ascontiguousarray(v.reshape(-1, P).T)

    def gates(b):
        return np.ascontiguousarray(b.reshape(SKIPS, -1, P).transpose(2, 0, 1))

    i = {k: np.asarray(v) for k, v in inp.items()}
    edge = np.arange(EDGES, dtype=np.float32)
    return {
        "x": i["x"], "adj": i["adj"], "adj_t": np.ascontiguousarray(i["adj"].T), "ident": np.eye(P, dtype=np.float32),
        "gcn_w": np.stack([chunks(i["L0_gnn_Wg0"]), chunks(i["L0_gnn_Wg1"])]),
        "gcn_b": np.stack([alike(i["L0_gnn_bg0"]), alike(i["L0_gnn_bg1"])]),
        "wih": np.stack([chunks(w.T) for w in i["L0_gnn_Wih"]]), "whh": np.stack([chunks(w.T) for w in i["L0_gnn_Whh"]]),
        "bih": gates(i["L0_gnn_bih"]), "bhh": gates(i["L0_gnn_bhh"]),
        "src_row": alike(i["L1_gnn_src"]), "dst_row": alike(i["L1_gnn_dst"]),
        "src_col": columns(i["L1_gnn_src"]), "dst_col": columns(i["L1_gnn_dst"]),
        "iota_row": alike(edge), "iota_col": columns(edge),
        "node_col": np.tile(np.arange(NODES, dtype=np.float32), TILE_GRAPHS).reshape(P, 1),
        "a_row": alike(i["L1_gnn_a"]), "a_col": columns(i["L1_gnn_a"]),
        "w_lin": chunks(i["L1_gnn_W_lin"].T), "w_val": chunks(i["L1_gnn_W_val"].T), "w_out": chunks(i["L1_gnn_W_out"].T),
        "w1": chunks(i["L2_gnn_W1"].T), "w2": chunks(i["L2_gnn_W2"].T),
        "b1": columns(i["L2_gnn_b1"]), "g1": columns(i["L2_gnn_g1"]), "be1": columns(i["L2_gnn_be1"]),
        "b2": columns(i["L2_gnn_b2"]), "g2": columns(i["L2_gnn_g2"]), "be2": columns(i["L2_gnn_be2"]),
        "w3": chunks(i["L3_gnn_W"]), "a3": alike(i["L3_gnn_a"]),
    }


def kernel(**inputs):
    import numpy as np
    import concourse.bacc as bacc
    from concourse.bass_utils import run_bass_kernel_spmd

    nc = bacc.Bacc("TRN2", target_bir_lowering=False, num_devices=1)
    arrays, args = {}, {}
    for name, a in layouts(inputs).items():
        arrays[f"in_{name}"] = a
        args[name] = nc.dram_tensor(f"in_{name}", a.shape, mybir.dt.from_np(a.dtype), kind="ExternalInput").ap()
    args["out"] = nc.dram_tensor("out", [BATCH, NODES, D], F32, kind="ExternalOutput").ap()
    build(nc, args)
    r = run_bass_kernel_spmd(nc, [arrays], core_ids=[0])
    return np.asarray(r.results[0]["out"])
```

```python
from contextlib import ExitStack

import concourse.bass as bass
from concourse import mybir

F32 = mybir.dt.float32
F32R = mybir.dt.float32r
I32 = mybir.dt.int32
ALU = mybir.AluOpType
ACT = mybir.ActivationFunctionType
AX = mybir.AxisListType

P = 128
BATCH, NODES, D = 128, 64, 256
ROWS = BATCH * NODES
KD = D // P
TILE_GRAPHS = P // NODES
GT = 4
GROWS = GT * P
NG = ROWS // GROWS
EDGES = 512
EC = EDGES // P
HEADS, DH = 4, 64
SKIPS = 4
HID2 = 512
KH = HID2 // P
EPS = 1e-5
LOG_EPS = 1e-8
LEAK = 0.2
BIG = 3.0e38


def wait(eng, sem, value):
    if isinstance(value, int) and value <= 0:
        return
    eng.wait_ge(sem, value)


def f32(ap):
    return ap.bitcast(F32)


def mm3(nc, out, w_hi, w_lo, x_hi, x_lo, first, last):
    nc.tensor.matmul(out, w_hi, x_hi, start=first, stop=False)
    nc.tensor.matmul(out, w_hi, x_lo, start=False, stop=False)
    return nc.tensor.matmul(out, w_lo, x_hi, start=False, stop=last)


class Core:

    def __init__(self, nc, ctx):
        self.nc, self.ctx = nc, ctx

    def sem(self, name):
        return self.ctx.enter_context(self.nc.semaphore(name))


def allocator(nc, ctx):
    def sb(name, shape, dt=F32):
        return ctx.enter_context(nc.sbuf_tensor(name, shape, dt))

    def ps(name, shape, dt=F32):
        return ctx.enter_context(nc.psum_tensor(name, shape, dt))

    return sb, ps


def both_ends(eng, n, body):
    body(0)
    with eng.Fori(1, n - 1) as i:
        body(i)
    body(n - 1)


def peeled(eng, n, body):
    body(0)
    with eng.Fori(1, n) as i:
        body(i)


class Chain:

    def __init__(self, eng, sem):
        self.eng, self.sem, self.n = eng, sem, 0

    def __call__(self, ins):
        self.n += 1
        ins.then_inc(self.sem, 1)
        self.eng.wait_ge(self.sem, self.n)


def gcn_phase(core, x, w, bg, adj_t, HT, wih, lstm_first):
    nc = core.nc
    NB = 4
    NI = NG // NB
    STAGES = 4
    with ExitStack() as ctx:
        sb, ps = allocator(nc, ctx)
        w_raw = sb("a_w_raw", [P, 2, KD, D])
        w_hi = sb("a_w_hi", [P, 2, KD, D], F32R)
        w_lo = sb("a_w_lo", [P, 2, KD, D], F32R)
        b_raw = sb("a_b_raw", [P, 2, D])
        HI0, LO0, HI1 = (slice(i * P // 4, i * P // 4 + 1) for i in range(3))
        b_first = sb("a_b_first", [P, D], F32R)
        b_second = sb("a_b_second", [NODES, D], F32R)
        sums = sb("a_sums", [P, GROWS], F32R)
        ones = sb("a_ones", [P, P], F32R)
        adj_raw = sb("a_adj_raw", [P, P])
        adj_hi = sb("a_adj_hi", [P, P], F32R)
        adj_lo = sb("a_adj_lo", [P, P], F32R)
        mhalf = sb("a_mhalf", [P, GT])
        xt = [sb(f"a_xt{b}", [P, GT, D])[:, :, :] for b in range(NB)]
        st = [sb(f"a_st{b}", [P, GT, 6]) for b in range(NB)]
        mv = [sb(f"a_mv{b}", [P, GT, 2]) for b in range(NB)]
        ve = [sb(f"a_ve{b}", [P, GT]) for b in range(NB)]
        rstd = [sb(f"a_rstd{b}", [P, GT]) for b in range(NB)]
        hT_hi = [sb(f"a_hThi{b}", [P, KD, GROWS], F32R) for b in range(NB)]
        hT_lo = [sb(f"a_hTlo{b}", [P, KD, GROWS], F32R) for b in range(NB)]
        x_hi, x_lo = ([t[:, :, :].rearrange("p k (a d) -> p (k a) d", d=D) for t in h] for h in (hT_hi, hT_lo))
        u_hi = [sb(f"a_uhi{b}", [P, GT, D], F32R) for b in range(NB)]
        u_lo = [sb(f"a_ulo{b}", [P, GT, D], F32R) for b in range(NB)]
        pV = [ps(f"a_p{b}", [P, KD, GROWS])[:, :, :] for b in range(NB)]
        pU = [p.rearrange("p k (a d) -> p (k a) d", d=D) for p in pV]
        pS = pV[NB - 1][:, 0, :]
        raw, first_hi, first_lo = lstm_first
        first_in = core.sem("a_first_in")
        consts, zeroed, w_ready = core.sem("a_consts"), core.sem("a_zeroed"), core.sem("a_w_ready")
        x_in = [core.sem(f"a_x_in{b}") for b in range(NB)]
        stats, moments = core.sem("a_stats"), core.sem("a_moments")
        var_eps, rstd_ready, normed = core.sem("a_var_eps"), core.sem("a_rstd"), core.sem("a_normed")
        mm_done, hi_done, lo_done = core.sem("a_mm"), core.sem("a_hi"), core.sem("a_lo")
        out_done = core.sem("a_out")
        HTg = HT.rearrange("p k (g c) -> p k g c", c=GROWS)
        CONSTS = 16 * (4 + TILE_GRAPHS)
        ADJ, SUMS, WEIGHTS = 2, 4, 11

        def n(it, b):
            return NB * it + b + 1

        def mm(it, s, b):
            return 1 + NB * (STAGES * it + s) + b + 1

        def half(it, s, b):
            return NB * (STAGES * it + s) + b + 1

        with nc.Block() as block:
            @block.sync
            def _(sp):
                sp.dma_start(xt[0], x[0]).then_inc(x_in[0], 16)
                sp.wait_ge(zeroed, 1)
                for g in range(TILE_GRAPHS):
                    r = slice(g * NODES, (g + 1) * NODES)
                    sp.dma_start(adj_raw[r, r], adj_t).then_inc(consts, 16)
                for l in range(2):
                    sp.dma_start(b_raw[:, l], bg[l]).then_inc(consts, 16)
                    sp.dma_start(w_raw[:, l], w[l]).then_inc(consts, 16)
                for b in range(1, NB):
                    sp.dma_start(xt[b], x[b]).then_inc(x_in[b], 16)
                sp.dma_start(raw[:, :, :], wih[0]).then_inc(first_in, 16)

                def body(it):
                    for b in range(NB):
                        sp.wait_ge(lo_done, half(it, 0, b))
                        sp.dma_start(xt[b], x[NB * it + NB + b]).then_inc(x_in[b], 16)

                peeled(sp, NI - 1, body)

            @block.gpsimd
            def _(pool):
                nc.gpsimd.memset(adj_raw[:, :], 0.0).then_inc(zeroed, 1)
                nc.gpsimd.memset(mhalf[:, :], -0.5).then_inc(zeroed, 1)
                nc.gpsimd.memset(f32(b_first[:, :]), 0.0).then_inc(zeroed, 1)
                nc.gpsimd.memset(f32(b_second[:, :]), 0.0).then_inc(zeroed, 1)
                nc.gpsimd.memset(f32(ones[:, :]), 1.0).then_inc(zeroed, 1)
                pool.wait_ge(zeroed, 5)

                def body(it):
                    for b in range(NB):
                        pool.wait_ge(var_eps, n(it, b))
                        wait(pool, normed, n(it, b) - NB)
                        nc.gpsimd.tensor_tensor(rstd[b][:, :], ve[b][:, :], mhalf[:, :], ALU.pow).then_inc(rstd_ready, 1)

                peeled(pool, NI, body)

            @block.vector
            def _(dve):
                V = nc.vector

                def measure(it, b):
                    dve.wait_ge(x_in[b], 16 * it + 16)
                    wait(dve, moments, n(it, b) - NB)
                    for j in range(GT):
                        last = V.bn_stats(st[b][:, j, :], xt[b][:, j, :])
                    last.then_inc(stats, 1)

                def moment(it, b):
                    dve.wait_ge(stats, n(it, b))
                    wait(dve, rstd_ready, n(it, b) - NB)
                    V.memset(ve[b][:, :], EPS)
                    for j in range(GT):
                        last = V.bn_aggr(mv[b][:, j, :], st[b][:, j, :])
                    last.then_inc(moments, 1)
                    dve.wait_ge(moments, n(it, b))
                    V.tensor_tensor(ve[b][:, :], ve[b][:, :], mv[b][:, :, 1], ALU.add).then_inc(var_eps, 1)

                def normalise(it, b):
                    dve.wait_ge(rstd_ready, n(it, b))
                    for j in range(GT):
                        last = V.tensor_scalar(xt[b][:, j, :], xt[b][:, j, :], mv[b][:, j, 0:1],
                                               rstd[b][:, j:j + 1], ALU.subtract, ALU.mult)
                    last.then_inc(normed, 1)

                def lo_halves(it, s, b):
                    dve.wait_ge(hi_done, half(it, s, b))
                    if s == 0:
                        V.scalar_tensor_tensor(out=x_lo[b][:, :, :], in0=xt[b], scalar=0.0, in1=f32(x_hi[b][:, :, :]),
                                               op0=ALU.max, op1=ALU.subtract).then_inc(lo_done, 1)
                    elif s == 1:
                        V.tensor_tensor(hT_lo[b][:, :, :], pV[b], f32(hT_hi[b][:, :, :]), ALU.subtract).then_inc(lo_done, 1)
                    elif s == 2:
                        V.scalar_tensor_tensor(out=hT_lo[b][:, :, :], in0=pV[b], scalar=0.0, in1=f32(hT_hi[b][:, :, :]),
                                               op0=ALU.max, op1=ALU.subtract).then_inc(lo_done, 1)
                    else:
                        V.tensor_tensor(u_lo[b][:, :, :], pU[b], f32(u_hi[b][:, :, :]), ALU.subtract).then_inc(lo_done, 1)

                def adjacency():
                    dve.wait_ge(consts, CONSTS)
                    V.tensor_copy(adj_hi[:, :], adj_raw[:, :]).then_inc(w_ready, 1)
                    dve.wait_ge(w_ready, 1)
                    V.tensor_tensor(adj_lo[:, :], adj_raw[:, :], f32(adj_hi[:, :]), ALU.subtract).then_inc(w_ready, 1)

                def row_sums():
                    lo_rows = slice(P // 4, P // 2)
                    dve.wait_ge(mm_done, 1)
                    V.tensor_copy(sums[:, :], pS).then_inc(w_ready, 1)
                    dve.wait_ge(w_ready, ADJ + 1)
                    V.tensor_tensor(sums[lo_rows, :], pS[lo_rows], f32(sums[lo_rows, :]), ALU.subtract).then_inc(w_ready, 1)

                def weights():
                    dve.wait_ge(zeroed, 5)
                    V.tensor_copy(w_hi[:, :, :, :], w_raw[:, :, :, :]).then_inc(w_ready, 1)
                    for row in (HI0, LO0, HI1):
                        V.tensor_copy(b_first[row, :], b_raw[row, 0, :]).then_inc(w_ready, 1)
                    V.tensor_copy(b_second[HI0, :], b_raw[HI0, 1, :]).then_inc(w_ready, 1)
                    dve.wait_ge(w_ready, SUMS + 5)
                    V.tensor_tensor(w_lo[:, :, :, :], w_raw[:, :, :, :], f32(w_hi[:, :, :, :]), ALU.subtract)
                    V.tensor_tensor(b_first[HI1, :], b_raw[HI1, 0, :], f32(b_first[HI1, :]), ALU.subtract).then_inc(w_ready, 1)
                    V.tensor_tensor(b_second[LO0, :], b_raw[HI0, 1, :], f32(b_second[HI0, :]), ALU.subtract).then_inc(w_ready, 1)

                measure(0, 0)
                moment(0, 0)
                adjacency()
                for b in range(NB):
                    normalise(0, b)
                    if b + 1 < NB:
                        measure(0, b + 1)
                        moment(0, b + 1)
                    if b == 0:
                        row_sums()
                    lo_halves(0, 0, b)
                weights()

                def body(it):
                    more = not (isinstance(it, int) and it == NI - 1)
                    for s in range(1, STAGES):
                        for b in range(NB):
                            lo_halves(it, s, b)
                            if more and s == 1:
                                measure(it + 1, b)
                                moment(it + 1, b)
                            if more and s == 2:
                                normalise(it + 1, b)
                            if not more and s == 2:
                                cols = slice(b * D, (b + 1) * D)
                                dve.wait_ge(first_in, 16)
                                V.tensor_copy(first_hi[:, :, cols], raw[:, :, cols]).then_inc(w_ready, 1)
                                dve.wait_ge(w_ready, WEIGHTS + b + 1)
                                V.tensor_tensor(first_lo[:, :, cols], raw[:, :, cols], f32(first_hi[:, :, cols]), ALU.subtract)
                    if more:
                        for b in range(NB):
                            lo_halves(it + 1, 0, b)

                both_ends(dve, NI, body)

            @block.scalar
            def _(act):
                def hi_of_rows(it, b):
                    act.wait_ge(normed, n(it, b))
                    wait(act, mm_done, mm(it - 1, 2, b))
                    nc.scalar.activation(x_hi[b][:, :, :], xt[b], ACT.Relu).then_inc(hi_done, 1)

                def body(it):
                    more = not (isinstance(it, int) and it == NI - 1)
                    for s in range(1, STAGES):
                        for b in range(NB):
                            act.wait_ge(mm_done, mm(it, s - 1, b))
                            if s == 1:
                                nc.scalar.activation(hT_hi[b][:, :, :], pV[b], ACT.Copy).then_inc(hi_done, 1)
                            elif s == 2:
                                nc.scalar.activation(hT_hi[b][:, :, :], pV[b], ACT.Relu).then_inc(hi_done, 1)
                            else:
                                nc.scalar.activation(u_hi[b][:, :, :], pU[b], ACT.Copy).then_inc(hi_done, 1)
                    if more:
                        for b in range(NB):
                            hi_of_rows(it + 1, b)
                    for b in range(NB):
                        act.wait_ge(mm_done, mm(it, STAGES - 1, b))
                        nc.scalar.activation(HTg[:, :, NB * it + b, :], pV[b], ACT.Relu).then_inc(out_done, 1)

                for b in range(NB):
                    hi_of_rows(0, b)
                both_ends(act, NI, body)

            @block.tensor
            def _(pe):
                pe.wait_ge(zeroed, 5)
                pe.wait_ge(w_ready, ADJ)
                for j in range(GT):
                    nc.tensor.matmul(pS[:, j * P:(j + 1) * P], ones[:, :], adj_hi[:, :], start=True, stop=False)
                    last = nc.tensor.matmul(pS[:, j * P:(j + 1) * P], ones[:, :], adj_lo[:, :], start=False, stop=True)
                last.then_inc(mm_done, 1)

                def halves_ready(it, s, b):
                    pe.wait_ge(hi_done, half(it, s, b))
                    pe.wait_ge(lo_done, half(it, s, b))

                def neighbours(it, s, b, hi, lo):
                    halves_ready(it, s, b)
                    for k in range(KD):
                        c = slice(k * P, (k + 1) * P)
                        for j in range(GT):
                            last = mm3(nc, pV[b][:, k, j * P:(j + 1) * P], hi[b][:, j, c], lo[b][:, j, c],
                                       adj_hi[:, :], adj_lo[:, :], True, True)
                    last.then_inc(mm_done, 1)

                def body(it):
                    for b in range(NB):
                        wait(pe, out_done, n(it, b) - NB)
                        if isinstance(it, int) and it == 0 and b == NB - 1:
                            pe.wait_ge(w_ready, SUMS)
                        neighbours(it, 0, b, x_hi, x_lo)
                    if isinstance(it, int) and it == 0:
                        pe.wait_ge(w_ready, WEIGHTS)
                    for b in range(NB):
                        halves_ready(it, 1, b)
                        for f in range(KD):
                            c = slice(f * P, (f + 1) * P)
                            nc.tensor.matmul(pV[b][:, f, :], b_first[:, c], sums[:, :], start=True, stop=False)
                            for k in range(KD):
                                last = mm3(nc, pV[b][:, f, :], w_hi[:, 0, k, c], w_lo[:, 0, k, c], hT_hi[b][:, k, :],
                                           hT_lo[b][:, k, :], False, k == KD - 1)
                        last.then_inc(mm_done, 1)
                    for b in range(NB):
                        halves_ready(it, 2, b)
                        for j in range(GT):
                            c = slice(j * P, (j + 1) * P)
                            nc.tensor.matmul(pU[b][:, j, :], ones[0:NODES, :], b_second[:, :], start=True, stop=False)
                            for k in range(KD):
                                last = mm3(nc, pU[b][:, j, :], hT_hi[b][:, k, c], hT_lo[b][:, k, c],
                                           w_hi[:, 1, k, :], w_lo[:, 1, k, :], False, k == KD - 1)
                        last.then_inc(mm_done, 1)
                    for b in range(NB):
                        neighbours(it, 3, b, u_hi, u_lo)

                peeled(pe, NI, body)


def lstm_first_weights(sb):
    shape = [P, KD, 4 * D]
    return sb("b_raw0", shape), sb("b_whi10", shape, F32R), sb("b_wlo10", shape, F32R)


def lstm_phase(core, wih, whh, bih, bhh, HT, first):
    nc = core.nc
    NC4 = 4 * D
    I, F, G, O = range(4)
    SIG = {I: ACT.Sigmoid, F: ACT.Sigmoid, G: ACT.Tanh, O: ACT.Sigmoid}
    with ExitStack() as ctx:
        sb, ps = allocator(nc, ctx)
        raw = [first[0], sb("b_raw1", [P, KD, NC4])]
        w_hi, w_lo = ([[first[i] if (s, m) == (1, 0) else sb(f"b_w{n}{s}{m}", [P, KD, NC4], F32R) for m in range(2)]
                       for s in range(2)] for i, n in ((1, "hi"), (2, "lo")))
        bias = sb("b_bias", [P, SKIPS, 8])
        bias2 = sb("b_bias2", [P, SKIPS, 8])
        xs_hi = [sb(f"b_xshi{b}", [P, KD, GROWS], F32R) for b in range(2)]
        xs_lo = [sb(f"b_xslo{b}", [P, KD, GROWS], F32R) for b in range(2)]
        hs_hi = [sb(f"b_hshi{b}", [P, KD, GROWS], F32R) for b in range(2)]
        hs_lo = [sb(f"b_hslo{b}", [P, KD, GROWS], F32R) for b in range(2)]
        cell = [sb(f"b_cell{b}", [P, KD, GROWS]) for b in range(2)]
        gate = [sb(f"b_gate{s}", [P, 4, GROWS]) for s in range(2)]
        tc = [sb(f"b_tc{s}", [P, GROWS]) for s in range(2)]
        pG = [ps(f"b_pG{s}", [P, 4, GROWS]) for s in range(2)]
        bias_in, raw_in = core.sem("b_bias_in"), core.sem("b_raw_in")
        bias_ready, w_part, w_ready = core.sem("b_bias_ready"), core.sem("b_w_part"), core.sem("b_w_ready")
        gate_mm, gate_act = core.sem("b_gate_mm"), core.sem("b_gate_act")
        xs_part, xs_ready = core.sem("b_xs_part"), core.sem("b_xs_ready")
        hs_part, hs_ready = core.sem("b_hs_part"), core.sem("b_hs_ready")
        ig_ready, fc_ready, cell_ready = core.sem("b_ig"), core.sem("b_fc"), core.sem("b_cell_ready")
        tanh_ready, h_ready = core.sem("b_tanh"), core.sem("b_h_ready")

        class Plan:

            def __init__(self, p, before):
                self.p = p
                self.nw = NODES // p
                self.graphs = GROWS // NODES if p == 1 else 2 * GROWS // NODES
                self.n = self.graphs * self.nw
                self.its = BATCH // (2 * self.graphs)
                self.units = 4 * p
                self.gates = 12 + 16 * (p - 1)
                if before is None:
                    self.u0 = self.g0 = self.x0 = self.h0 = self.i0 = 0
                else:
                    q = before
                    self.u0 = q.u0 + q.its * q.units
                    self.g0 = q.g0 + q.its * q.gates
                    self.x0 = q.x0 + q.its * 2 * q.p
                    self.h0 = q.h0 + q.its * 2 * (q.p - 1)
                    self.i0 = q.i0 + q.its * 4 * (q.p - 1)

            def unit(self, it, t, b, s):
                return self.u0 + it * self.units + (2 * t + b) * 2 + s

            def gate(self, it, t, b, s):
                before = (2 * b + s) * 3 if t == 0 else 12 + 16 * (t - 1) + (2 * b + s) * 4
                return self.g0 + it * self.gates + before

            def later(self, it, t, b, s):
                return self.i0 + it * 4 * (self.p - 1) + (t - 1) * 4 + 2 * b + s

            def x(self, it, t, b):
                return self.x0 + it * 2 * self.p + 2 * t + b

            def h(self, it, t, b):
                return self.h0 + it * 2 * (self.p - 1) + 2 * t + b

            def order(self, t):
                return (I, G, O) if t == 0 else (I, G, F, O)

            def windows(self, it, b, k, t):
                v = HT.rearrange("p k (i g c) -> p k i g c", g=self.graphs, c=NODES)[:, k, 2 * it + b, :, :]
                return v[:, :, t:t + (self.nw - 1) * self.p + 1:self.p]

            def flat(self, ap):
                return ap[:, 0:self.n].rearrange("p (g w) -> p g w", w=self.nw)

        plans = []
        for p in range(1, SKIPS + 1):
            plans.append(Plan(p, plans[-1] if plans else None))
        w_count = [0]
        for q in plans[:-1]:
            w_count.append(w_count[-1] + q.its)

        def loop(eng, plan, body):
            if plan.p == 1:
                peeled(eng, plan.its, body)
            else:
                with eng.Fori(0, plan.its) as it:
                    body(it)

        with nc.Block() as block:
            @block.sync
            def _(sp):
                sp.dma_start(bias[:, :, :], bih).then_inc(bias_in, 16)
                sp.dma_start(bias2[:, :, :], bhh).then_inc(bias_in, 16)
                for p in range(1, SKIPS):
                    wait(sp, w_ready, w_count[p - 1])
                    for m, src in enumerate((wih, whh)):
                        sp.dma_start(raw[m][:, :, :], src[p]).then_inc(raw_in, 16)

            @block.tensor
            def _(pe):
                for plan in plans:
                    slot = plan.p % 2
                    wait(pe, w_ready, w_count[plan.p - 1])

                    def body(it, plan=plan, slot=slot):
                        for t in range(plan.p):
                            for b in range(2):
                                for s in range(2):
                                    if s == 0:
                                        pe.wait_ge(xs_ready, plan.x(it, t, b) + 1)
                                        if t:
                                            pe.wait_ge(hs_ready, plan.h(it, t - 1, b) + 1)
                                    ahead = 3 if t == 0 and (b or s) else 4
                                    if t == 0 and b == 0 and s == 0 and plan.p <= 2:
                                        ahead = 3
                                    if t == 1 and b == 0 and s == 0:
                                        ahead = 3
                                    wait(pe, gate_act, plan.gate(it, t, b, s) - ahead)
                                    for g in plan.order(t):
                                        c = slice(g * D + s * P, g * D + s * P + P)
                                        out = pG[s][:, g, 0:plan.n]
                                        pairs = [(0, xs_hi[b], xs_lo[b], k) for k in range(KD)]
                                        if t:
                                            pairs += [(1, hs_hi[b], hs_lo[b], k) for k in range(KD)]
                                        for i, (m, hi, lo, k) in enumerate(pairs):
                                            last = mm3(nc, out, w_hi[slot][m][:, k, c], w_lo[slot][m][:, k, c],
                                                       hi[:, k, 0:plan.n], lo[:, k, 0:plan.n],
                                                       i == 0, i == len(pairs) - 1)
                                        last.then_inc(gate_mm, 1)

                    loop(pe, plan, body)

            @block.scalar
            def _(act):
                act.wait_ge(bias_ready, 1)
                for plan in plans:
                    def body(it, plan=plan):
                        for t in range(plan.p):
                            for b in range(2):
                                for s in range(2):
                                    wait(act, h_ready, plan.unit(it, t, b, s) - 1)
                                    for i, g in enumerate(plan.order(t)):
                                        act.wait_ge(gate_mm, plan.gate(it, t, b, s) + i + 1)
                                        nc.scalar.activation(gate[s][:, g, 0:plan.n], pG[s][:, g, 0:plan.n], SIG[g],
                                                             bias=bias[:, plan.p - 1, 2 * g + s:2 * g + s + 1])\
                                            .then_inc(gate_act, 1)
                                    act.wait_ge(cell_ready, plan.unit(it, t, b, s) + 1)
                                    pt, pb = (t, 0) if b else (t - 1, 1)
                                    if 0 <= pt < plan.p - 1:
                                        act.wait_ge(hs_ready, plan.h(it, pt, pb) + 1)
                                    nc.scalar.activation(tc[s][:, 0:plan.n], cell[b][:, s, 0:plan.n],
                                                         ACT.Tanh).then_inc(tanh_ready, 1)

                    loop(act, plan, body)

            @block.gpsimd
            def _(pool):
                for plan in plans[1:]:
                    def body(it, plan=plan):
                        for t in range(1, plan.p):
                            for b in range(2):
                                for s in range(2):
                                    pool.wait_ge(gate_act, plan.gate(it, t, b, s) + 2)
                                    nc.gpsimd.tensor_tensor(gate[s][:, I, 0:plan.n], gate[s][:, I, 0:plan.n],
                                                            gate[s][:, G, 0:plan.n], ALU.mult).then_inc(ig_ready, 1)

                    loop(pool, plan, body)

            @block.vector
            def _(dve):
                dve.wait_ge(bias_in, 32)
                nc.vector.tensor_tensor(bias[:, :, :], bias[:, :, :], bias2[:, :, :], ALU.add).then_inc(bias_ready, 1)

                def split_w(slot, cols):
                    for m in range(2):
                        nc.vector.tensor_copy(w_hi[slot][m][:, :, cols], raw[m][:, :, cols]).then_inc(w_part, 1)

                def split_w_lo(slot, cols):
                    for m in range(2):
                        last = nc.vector.tensor_tensor(w_lo[slot][m][:, :, cols], raw[m][:, :, cols],
                                                       f32(w_hi[slot][m][:, :, cols]), ALU.subtract)
                    last.then_inc(w_ready, 1)

                def split_x(plan, it, t, b, count):
                    for k in range(KD):
                        nc.vector.tensor_copy(plan.flat(xs_hi[b][:, k, :]), plan.windows(it, b, k, t))\
                            .then_inc(xs_part, 1)
                    dve.wait_ge(xs_part, KD * (count + 1))
                    for k in range(KD):
                        last = nc.vector.tensor_tensor(plan.flat(xs_lo[b][:, k, :]), plan.windows(it, b, k, t),
                                                       plan.flat(f32(xs_hi[b][:, k, :])), ALU.subtract)
                    last.then_inc(xs_ready, 1)

                for b in range(2):
                    split_x(plans[0], 0, 0, b, b)

                for plan in plans:
                    n, T = plan.n, plan.p
                    after = plans[plan.p] if plan.p < SKIPS else None

                    def body(it, end=False, plan=plan, after=after, n=n, T=T):
                        for t in range(T):
                            for b in range(2):
                                for s in range(2):
                                    un, g0, ng = plan.unit(it, t, b, s), plan.gate(it, t, b, s), len(plan.order(t))
                                    c = cell[b][:, s, 0:n]
                                    if s == 1:
                                        dve.wait_ge(gate_mm, g0 + ng)
                                        if t < T - 1:
                                            split_x(plan, it, t + 1, b, plan.x(it, t + 1, b))
                                        elif not end:
                                            split_x(plan, it + 1, 0, b, plan.x(it, T, b))
                                        elif after:
                                            wait(dve, h_ready, plan.u0 + it * plan.units)
                                            split_x(after, 0, 0, b, after.x(0, 0, b))
                                    if t == 0:
                                        dve.wait_ge(gate_act, g0 + 2)
                                        nc.vector.tensor_tensor(c, gate[s][:, I, 0:n], gate[s][:, G, 0:n],
                                                                ALU.mult).then_inc(cell_ready, 1)
                                    else:
                                        dve.wait_ge(gate_act, g0 + 3)
                                        nc.vector.tensor_tensor(c, gate[s][:, F, 0:n], c, ALU.mult).then_inc(fc_ready, 1)
                                        dve.wait_ge(fc_ready, plan.later(it, t, b, s) + 1)
                                        dve.wait_ge(ig_ready, plan.later(it, t, b, s) + 1)
                                        nc.vector.tensor_tensor(c, c, gate[s][:, I, 0:n], ALU.add).then_inc(cell_ready, 1)
                                    dve.wait_ge(gate_act, g0 + ng)
                                    dve.wait_ge(tanh_ready, un + 1)
                                    if t == T - 1:
                                        nc.vector.tensor_tensor(plan.windows(it, b, s, t), plan.flat(gate[s][:, O, :]),
                                                                plan.flat(tc[s][:, :]), ALU.mult).then_inc(h_ready, 1)
                                    else:
                                        nc.vector.tensor_tensor(tc[s][:, 0:n], gate[s][:, O, 0:n], tc[s][:, 0:n],
                                                                ALU.mult).then_inc(h_ready, 1)
                                if t < T - 1:
                                    for s in range(2):
                                        dve.wait_ge(h_ready, plan.unit(it, t, b, s) + 1)
                                        nc.vector.tensor_copy(hs_hi[b][:, s, 0:n], tc[s][:, 0:n]).then_inc(hs_part, 1)
                                    dve.wait_ge(hs_part, 2 * (plan.h(it, t, b) + 1))
                                    for s in range(2):
                                        last = nc.vector.tensor_tensor(hs_lo[b][:, s, 0:n], tc[s][:, 0:n],
                                                                       f32(hs_hi[b][:, s, 0:n]), ALU.subtract)
                                    last.then_inc(hs_ready, 1)
                                if after and t == T - 1 and b == 0:
                                    wc = NC4 // plan.its
                                    cols = bass.ds(it * wc, wc)
                                    dve.wait_ge(raw_in, 32 * plan.p)
                                    split_w(1 - plan.p % 2, cols)
                                    done = w_count[plan.p - 1] + it
                                    dve.wait_ge(w_part, 2 * (done + 1))
                                    split_w_lo(1 - plan.p % 2, cols)

                    start = 1 if plan.p == 1 else 0
                    if start:
                        body(0)
                    with dve.Fori(start, plan.its - 1) as it:
                        body(it)
                    body(plan.its - 1, end=True)



def edge_tables(core, a, tab, x, HT, rows_ahead):
    nc = core.nc
    HTg = HT.rearrange("p k (g c) -> p k g c", c=GROWS)
    with ExitStack() as ctx:
        sb, ps = allocator(nc, ctx)
        ints = {n: sb(f"s_{n}_i", [P, w], I32) for n, w in (("src_row", EDGES), ("dst_row", EDGES), ("src_col", EC), ("dst_col", EC))}
        flt = {n: sb(f"s_{n}_f", list(t.shape)) for n, t in ints.items()}
        iota_row, iota_col = sb("s_iota_row", [P, EDGES]), sb("s_iota_col", [P, EC])
        node_col = sb("s_node_col", [P, 1])
        adj = sb("s_adj", [NODES, NODES])
        a_row, a_col = sb("s_a_row", [P, D]), sb("s_a_col", [P, KD])
        w_raw = sb("s_w_raw", [P, 3, KD, D])
        key_row, key_col = sb("s_key_row", [P, EDGES]), sb("s_key_col", [P, EC])
        less, rank = sb("s_less", [P, EC, EDGES]), sb("s_rank", [P, EC])
        perm = sb("s_perm", [P, EC, EDGES], F32R)
        spread = sb("s_spread", [P, 2, EC, P], F32R)
        s_row, d_row = sb("s_s_row", [P, EDGES]), sb("s_d_row", [P, EDGES])
        oh_s, oh_d = sb("s_oh_s", [P, EDGES]), sb("s_oh_d", [P, EDGES])
        s_col = sb("s_s_col", [P, EC])
        picked = sb("s_picked", [NODES, EDGES])
        ones = sb("s_ones", [NODES, P])
        weight = sb("s_weight", [P, EDGES])
        a_abs = sb("s_a_abs", [P, D])
        prod = sb("s_prod", [P, KD, D])
        wq = sb("s_wq", [P, KD, D])
        wl = sb("s_wl", [P, KD, HEADS])
        pos, neg, sgn = sb("s_pos", [P, KD]), sb("s_neg", [P, KD]), sb("s_sgn", [P, KD])
        pA, pB = ps("s_pA", [P, EDGES]), ps("s_pB", [P, EDGES])
        pC, pD = ps("s_pC", [P, EC, P]), ps("s_pD", [P, EDGES])
        pW = ps("s_pW", [P, EDGES])
        landed, step = core.sem("s_landed"), core.sem("s_step")
        ranked, sorted_mm = core.sem("s_ranked"), core.sem("s_sorted_mm")
        onehot, turned = core.sem("s_onehot"), core.sem("s_turned")
        picked_ready, weight_mm = core.sem("s_picked_ready"), core.sem("s_weight_mm")
        weight_ready = core.sem("s_weight_ready")
        folded, rounded, zeroed, w_landed = (core.sem("s_" + n) for n in ("folded", "rounded", "zeroed", "w_landed"))
        loads = [(ints["src_row"], a["src_row"]), (ints["dst_row"], a["dst_row"]), (ints["src_col"], a["src_col"]),
                 (ints["dst_col"], a["dst_col"]), (iota_row, a["iota_row"]), (iota_col, a["iota_col"]),
                 (node_col, a["node_col"]), (adj, a["adj"]), (a_row, a["a_row"]), (a_col, a["a_col"]),
                 (tab["ident"], a["ident"])]
        with nc.Block() as block:
            @block.sync
            def _(sp):
                for t, src in loads:
                    sp.dma_start(t[:, :], src).then_inc(landed, 16)
                for i, src in enumerate((a["w_lin"], a["w_val"], a["w_out"])):
                    sp.dma_start(w_raw[:, i], src).then_inc(w_landed, 16)
                for b in range(2):
                    sp.dma_start(rows_ahead[0][b][:, :, :], x[b]).then_inc(rows_ahead[2][b], 16)
                    sp.dma_start(rows_ahead[1][b][:, :, :], HTg[:, :, b, :]).then_inc(rows_ahead[2][b], 16)

            splits = [(tab["wqv_hi"][:, :, D:2 * D], tab["wqv_lo"][:, :, D:2 * D], w_raw[:, 1]),
                      (tab["wo_hi"][:, :, :], tab["wo_lo"][:, :, :], w_raw[:, 2]),
                      (tab["wqv_hi"][:, :, 0:D], tab["wqv_lo"][:, :, 0:D], wq[:, :, :]),
                      (tab["wl_hi"][:, :, :], tab["wl_lo"][:, :, :], wl[:, :, :])]

            @block.gpsimd
            def _(pool):
                nc.gpsimd.memset(f32(tab["sign"][:, :, :]), 0.0).then_inc(zeroed, 1)
                nc.gpsimd.memset(f32(tab["src"][:, :, :, :]), 0.0).then_inc(zeroed, 1)
                for i, (hi, lo, full) in enumerate(splits):
                    pool.wait_ge(rounded, i + 1)
                    nc.gpsimd.tensor_tensor(lo, full, f32(hi), ALU.subtract)

            @block.vector
            def _(dve):
                link = Chain(dve, step)
                V = nc.vector
                dve.wait_ge(landed, 16 * len(loads))
                for n in ints:
                    link(V.tensor_copy(flt[n][:, :], ints[n][:, :]))
                link(V.scalar_tensor_tensor(out=key_row[:, :], in0=flt["src_row"][:, :], scalar=float(EDGES),
                                            in1=iota_row[:, :], op0=ALU.mult, op1=ALU.add))
                link(V.scalar_tensor_tensor(out=key_col[:, :], in0=flt["src_col"][:, :], scalar=float(EDGES),
                                            in1=iota_col[:, :], op0=ALU.mult, op1=ALU.add))
                for c in range(EC):
                    link(V.tensor_scalar(less[:, c, :], key_row[:, :], key_col[:, c:c + 1], None, ALU.is_lt))
                link(V.tensor_reduce(rank[:, :], less[:, :, :], AX.X, ALU.add))
                for c in range(EC):
                    link(V.tensor_scalar(perm[:, c, :], iota_row[:, :], rank[:, c:c + 1], None, ALU.is_equal))
                link(V.tensor_copy(spread[:, 0], flt["src_col"][:, :].unsqueeze(2).to_broadcast([P, EC, P])))
                V.tensor_copy(spread[:, 1], flt["dst_col"][:, :].unsqueeze(2).to_broadcast([P, EC, P])).then_inc(ranked, 1)

                dve.wait_ge(w_landed, 16 * 3)
                link(V.scalar_tensor_tensor(out=a_abs[:, :], in0=a_row[:, :], scalar=-1.0, in1=a_row[:, :],
                                            op0=ALU.mult, op1=ALU.max))
                for k in range(KD):
                    link(V.scalar_tensor_tensor(out=wq[:, k, :], in0=w_raw[:, 0, k, :], scalar=1.0 - LEAK,
                                                in1=a_abs[:, :], op0=ALU.mult, op1=ALU.mult))
                    link(V.scalar_tensor_tensor(out=prod[:, k, :], in0=w_raw[:, 0, k, :], scalar=LEAK,
                                                in1=a_row[:, :], op0=ALU.mult, op1=ALU.mult))
                link(V.tensor_reduce(wl[:, :, :], prod[:, :, :].rearrange("p k (h d) -> p k h d", h=HEADS), AX.X, ALU.add))
                V.memset(a_abs[:, :], 0.0).then_inc(folded, 1)
                link(V.tensor_scalar(pos[:, :], a_col[:, :], 0.0, None, ALU.is_gt))
                link(V.tensor_scalar(neg[:, :], a_col[:, :], 0.0, None, ALU.is_lt))
                link(V.tensor_tensor(sgn[:, :], pos[:, :], neg[:, :], ALU.subtract))
                dve.wait_ge(zeroed, 2)
                for k in range(KD):
                    for h in range(2):
                        r, col = slice(h * DH, (h + 1) * DH), P - HEADS + 2 * k + h
                        link(V.tensor_copy(tab["sign"][r, k, col:col + 1], sgn[r, k:k + 1]))

                dve.wait_ge(sorted_mm, 1)
                link(V.tensor_copy(s_row[:, :], pA[:, :]))
                link(V.tensor_copy(d_row[:, :], pB[:, :]))
                link(V.tensor_scalar(oh_s[:, :], s_row[:, :], node_col[:, 0:1], None, ALU.is_equal))
                link(V.tensor_scalar(oh_d[:, :], d_row[:, :], node_col[:, 0:1], None, ALU.is_equal))
                link(V.memset(ones[:, :], 1.0))
                V.tensor_tensor(tab["both"][:, :], oh_s[:, :], oh_d[:, :], ALU.add).then_inc(onehot, 1)
                link(V.tensor_copy(tab["dst"][:, :], oh_d[:, :]))
                link(V.memset(tab["same"][:, 0:1], 0.0))
                link(V.memset(tab["same"][:, EDGES:], 0.0))
                link(V.tensor_tensor(tab["same"][:, 1:EDGES], s_row[:, 1:], s_row[:, 0:EDGES - 1], ALU.is_equal))
                link(V.tensor_scalar(tab["cut"][:, :], tab["same"][:, :], 1.0, BIG, ALU.subtract, ALU.mult))
                dve.wait_ge(turned, 1)
                V.tensor_tensor(picked[:, :], pD[0:NODES, :], oh_d[0:NODES, :], ALU.mult).then_inc(picked_ready, 1)
                link(V.tensor_copy(s_col[:, :], pC[:, :, 0]))
                for g in range(TILE_GRAPHS):
                    for c in range(EC):
                        link(V.tensor_scalar(tab["src"][:, g, c, g * NODES:(g + 1) * NODES], iota_row[:, 0:NODES],
                                             s_col[:, c:c + 1], None, ALU.is_equal))
                dve.wait_ge(weight_mm, 1)
                V.tensor_scalar(weight[:, :], pW[:, :], LOG_EPS, None, ALU.add).then_inc(weight_ready, 1)

            @block.scalar
            def _(act):
                act.wait_ge(w_landed, 16 * 3)
                for i, (hi, lo, full) in enumerate(splits):
                    if i == 2:
                        act.wait_ge(folded, 1)
                    nc.scalar.activation(hi, full, ACT.Copy).then_inc(rounded, 1)
                act.wait_ge(weight_ready, 1)
                nc.scalar.activation(tab["log_w"][:, :], weight[:, :], ACT.Ln)

            @block.tensor
            def _(pe):
                pe.wait_ge(ranked, 1)
                for i, out in enumerate((pA, pB)):
                    for c in range(EC):
                        last = nc.tensor.matmul(out[:, :], spread[:, i, c, :], perm[:, c, :], start=c == 0, stop=c == EC - 1)
                last.then_inc(sorted_mm, 1)
                pe.wait_ge(onehot, 1)
                for c in range(EC):
                    nc.tensor.transpose(pC[:, c, :], s_row[:, c * P:(c + 1) * P], tab["ident"][:, :])
                nc.tensor.matmul(pD[0:NODES, :], adj[:, :], oh_s[0:NODES, :], start=True, stop=True).then_inc(turned, 1)
                pe.wait_ge(picked_ready, 1)
                nc.tensor.matmul(pW[:, :], ones[:, :], picked[:, :], start=True, stop=True).then_inc(weight_mm, 1)


def edge_attention(core, x, x2, tab, HT, rows_ahead):
    nc = core.nc
    NQ, QG, QT = 4, 32, 16
    GG = GT * TILE_GRAPHS
    NJ = QT // GT
    AHEAD = 2
    HG = GG // 2
    NH = QG // HG
    NT = 2
    NV = 2
    with ExitStack() as ctx:
        sb, ps = allocator(nc, ctx)
        mhalf, unused = sb("c_mhalf", [P, GT]), sb("c_unused", [P, 1])
        xt, hst, landed = rows_ahead
        st, mv, ve, rstd = sb("c_st", [P, GT, 6]), sb("c_mv", [P, GT, 2]), sb("c_ve", [P, GT]), sb("c_rstd", [P, GT])
        hT_hi, hT_lo = sb("c_hThi", [P, KD, GROWS], F32R), sb("c_hTlo", [P, KD, GROWS], F32R)
        keys_vals = sb("c_keys_vals", [P, GG + QG + AHEAD * GG, D], F32R)
        keys, vals = keys_vals[:, 0:GG, :], keys_vals[:, GG:, :]
        lin_hi, lin_lo = (sb("c_lin_" + n, [P, (NJ + AHEAD) * GG * HEADS], F32R) for n in ("hi", "lo"))
        r_hi = [sb(f"c_rhi{b}", [P, KD, EDGES], F32R) for b in range(2)]
        r_lo = [sb(f"c_rlo{b}", [P, KD, EDGES], F32R) for b in range(2)]
        work = sb("c_work", [P, 4, EDGES])
        wv = [work[:, 2 * b:2 * b + 2, :].rearrange("p a (c f) -> p (a c) f", f=D) for b in range(2)]
        wv.append(sb("c_wv", [P, EC, D])[:, :, :])
        WB = len(wv)
        wv_hi = [t[:, :, :].rearrange("p k (a d) -> p (k a) d", d=D) for t in r_hi]
        wv_lo = [t[:, :, :].rearrange("p k (a d) -> p (k a) d", d=D) for t in r_lo]
        attn_T = sb("c_attnT", [P, EC, P])
        y_rows = sb("c_yrows", [P, 2, D])
        lin_row = y_rows[0:HEADS, :, :].rearrange("p a d -> p (a d)")
        yT_hi, yT_lo = ([t[:, :, b * HG * NODES:(b + 1) * HG * NODES] for b in range(2)] for t in (hT_hi, hT_lo))
        pT = ps("c_pT", [P, KD, GROWS])
        pZ = [ps(f"c_pZ{b}", [P, KD, EDGES]) for b in range(2)]
        pU, pE = (ps("c_" + n, [P, EDGES])[:, :] for n in ("pU", "pE"))
        pTr = pT[:, :, :].rearrange("p k (a d) -> p (k a) d", d=D)
        pY = [pT[:, b, 0:D] for b in range(2)]
        pYT = pU.rearrange("p (k c) -> p k c", k=KD)
        pO = pU[:, :].rearrange("p (a d) -> p a d", d=D)
        names = ("half_set t1 x1_done stats moments var_eps rstd_ready normed t2 h_hi h_lo u_mm s_hi  s_lo "
                 "lin_mm lin_row lin_t lin_part lin_done z_mm r_hi_done r_lo_done e_mm soft exp_done at_mm attn_ready "
                 "vg_mm wv_done wv_hi_done wv_lo_done wv_lo_rest scattered y_rows yT_mm y_hi y_lo o_mm x2_done moved stored").split()
        sem = {n: core.sem("c_" + n) for n in names}
        HTg = HT.rearrange("p k (g c) -> p k g c", c=GROWS)

        halves = (slice(0, NODES), slice(NODES, P))

        def bank(m, t):
            return pE if m == 0 and t % 2 else pU

        def parts(r, m, gi):
            apart = GG + GG * m
            return keys_vals[r, gi:gi + apart + 1:apart, :]

        def x1_group(G):
            return HTg[:, :, G, :].rearrange("p k (a d) -> p k a d", d=D)

        def quad(ap):
            return ap.rearrange("p (k a) d -> p k a d", k=KD)

        with nc.Block() as block:
            @block.sync
            def _(sp):
                def load(G, m):
                    b = m % 2
                    wait(sp, sem["t2"], G - 1)
                    wait(sp, sem["x1_done"], G - 1)
                    sp.dma_start(xt[b][:, :, :], x[G]).then_inc(landed[b], 16)
                    sp.dma_start(hst[b][:, :, :], HTg[:, :, G, :]).then_inc(landed[b], 16)

                def body(q, last=False):
                    if not last:
                        for m in range(NJ):
                            load(NJ * q + NJ + m, m)
                    for h in range(NH):
                        G, k = NJ * q + h // KD, h % KD
                        sp.wait_ge(sem["x2_done"], NH * q + h + 1)
                        sp.dma_start(x2[G][:, KD * k:KD * (k + 1), :], x1_group(G)[:, k]).then_inc(sem["stored"], 16)
                        if not last and h == NH // 2:
                            w, lw = AHEAD * GG, AHEAD * GG * HEADS
                            for v in (lin_hi, lin_lo):
                                sp.dma_start(f32(v[:, 0:lw]), f32(v[:, QG * HEADS:QG * HEADS + lw])).then_inc(sem["moved"], 16)
                            sp.dma_start(f32(vals[:, 0:w, :]), f32(vals[:, QG:QG + w, :])).then_inc(sem["moved"], 16)

                for m in range(2, NJ):
                    load(m, m)
                body(0)
                with sp.Fori(1, NQ - 1) as q:
                    body(q)
                body(NQ - 1, last=True)
                sp.wait_ge(sem["stored"], 16 * NQ * NH)

            @block.gpsimd
            def _(pool):
                nc.gpsimd.memset(mhalf[:, :], -0.5).then_inc(sem["half_set"], 1)
                for v in (lin_hi, lin_lo):
                    nc.gpsimd.memset(f32(v[:, :]), 0.0).then_inc(sem["half_set"], 1)
                pool.wait_ge(sem["half_set"], 3)

                def normalise(q, m):
                    G = NJ * q + m
                    pool.wait_ge(sem["var_eps"], G + 1)
                    nc.gpsimd.tensor_tensor(rstd[:, :], ve[:, :], mhalf[:, :], ALU.pow).then_inc(sem["rstd_ready"], 1)
                    pool.wait_ge(sem["rstd_ready"], 2 * G + 1)
                    xn = hst[m % 2][:, :, :].rearrange("p k (a d) -> p (k a) d", d=D)
                    shape = [P, GT - NT, D]
                    nc.gpsimd.tensor_tensor(xn[:, NT:, :], x1_group(G)[:, NT // KD, NT % KD:, :],
                                            mv[:, NT:, 0:1].to_broadcast(shape), ALU.subtract).then_inc(sem["rstd_ready"], 1)
                    pool.wait_ge(sem["rstd_ready"], 2 * G + 2)
                    nc.gpsimd.tensor_tensor(xn[:, NT:, :], xn[:, NT:, :], rstd[:, NT:].unsqueeze(2).to_broadcast(shape),
                                            ALU.mult).then_inc(sem["normed"], 1)

                def body(q, last=False):
                    for m in range(3, NJ if last else NJ + 3):
                        normalise(q, m)
                    for gi in range(QG):
                        pool.wait_ge(sem["wv_hi_done"], QG * q + gi + 1)
                        nc.gpsimd.tensor_tensor(wv_lo[gi % 2][:, NV:, :], wv[gi % WB][:, NV:, :], f32(wv_hi[gi % 2][:, NV:, :]),
                                                ALU.subtract).then_inc(sem["wv_lo_rest"], 1)

                for m in range(3):
                    normalise(0, m)
                body(0)
                with pool.Fori(1, NQ - 1) as q:
                    body(q)
                body(NQ - 1, last=True)

            @block.tensor
            def _(pe):
                def turn_back(q, m):
                    pe.wait_ge(landed[m % 2], 32 * (NJ // 2 * q + m // 2 + 1))
                    wait(pe, sem["lin_done"], NJ * q + m)
                    for t in range(GT):
                        for k in range(KD):
                            last = nc.tensor.transpose(pTr[:, t, k * P:(k + 1) * P],
                                                       hst[m % 2][:, k, t * P:(t + 1) * P], tab["ident"][:, :])
                    last.then_inc(sem["t1"], 1)

                def turn(q, m):
                    pe.wait_ge(sem["normed"], 2 * (NJ * q + m + 1))
                    if m == 2:
                        wait(pe, sem["y_rows"], QT * q)
                    xn = hst[m % 2][:, :, :].rearrange("p k (a d) -> p (k a) d", d=D)
                    for t in range(GT):
                        for k in range(KD):
                            last = nc.tensor.transpose(pT[:, k, t * P:(t + 1) * P], xn[:, t, k * P:(k + 1) * P],
                                                       tab["ident"][:, :])
                    last.then_inc(sem["t2"], 1)

                def linear(q, m):
                    G = NJ * q + m
                    pe.wait_ge(sem["h_hi"], G + 1)
                    pe.wait_ge(sem["h_lo"], G + 1)
                    for k in range(KD):
                        last = mm3(nc, pT[0:HEADS, 0, :], tab["wl_hi"][:, k, :], tab["wl_lo"][:, k, :], hT_hi[:, k, :],
                                   hT_lo[:, k, :], k == 0, k == KD - 1)
                    last.then_inc(sem["lin_mm"], 1)

                def turn_linear(q, m):
                    for t in range(GT):
                        last = nc.tensor.transpose(pT[:, 1, HEADS * t:HEADS * (t + 1)], lin_row[:, t * P:(t + 1) * P],
                                                   tab["ident"][0:HEADS, 0:HEADS])
                    last.then_inc(sem["lin_t"], 1)

                def project(q, m, t):
                    if m == 2 and t == 0:
                        wait(pe, sem["x2_done"], NH * q)
                    wait(pe, sem["s_lo"], QT * q + GT * m + (t if m else t - 1))
                    c = slice(t * P, (t + 1) * P)
                    for k in range(KD):
                        last = mm3(nc, bank(m, t), hT_hi[:, k, c], hT_lo[:, k, c], tab["wqv_hi"][:, k, :],
                                   tab["wqv_lo"][:, k, :], k == 0, k == KD - 1)
                    last.then_inc(sem["u_mm"], 1)

                def gather(q, m, i):
                    gi = QG * q + GG * m + i
                    pe.wait_ge(sem["s_lo"], QT * q + GT * m + i // 2 + 1)
                    if m == 1 and i < 2:
                        wait(pe, sem["wv_done"], QG * q)
                    for k in range(KD):
                        wait(pe, sem["r_lo_done"], KD * (gi - 2) + k + 1)
                        nc.tensor.matmul(pZ[i % 2][:, k, :], keys[:, i, k * P:(k + 1) * P], tab["both"][:, :],
                                         start=True, stop=True).then_inc(sem["z_mm"], 1)

                def score(q, m, i):
                    gi, first = GG * m + i, m % NJ == 0 and i == 0
                    if first and not m:
                        pe.wait_ge(sem["s_lo"], GT)
                    if first and m:
                        pe.wait_ge(sem["soft"], 8 * q + 1)
                    at = P - HEADS - HEADS * (gi % QG)
                    for k in range(KD):
                        pe.wait_ge(sem["r_hi_done"], KD * (QG * q + gi) + k + 1)
                        pe.wait_ge(sem["r_lo_done"], KD * (QG * q + gi) + k + 1)
                        for n, r in enumerate((r_hi, r_lo)):
                            nc.tensor.matmul(pE, tab["sign"][:, k, at:at + P], r[i % 2][:, k, :],
                                             start=first and k == 0 and n == 0, stop=False)

                def add_linear(q):
                    pe.wait_ge(sem["lin_done"], NJ * q + NJ)
                    wait(pe, sem["moved"], 48 * q)
                    nc.tensor.matmul(pE, lin_hi[:, 0:P], tab["both"][:, :], start=False, stop=False)
                    nc.tensor.matmul(pE, lin_lo[:, 0:P], tab["both"][:, :], start=False, stop=True).then_inc(sem["e_mm"], 1)

                def turn_attention(q):
                    pe.wait_ge(sem["soft"], 8 * q + 8)
                    for c in range(EC):
                        last = nc.tensor.transpose(pT[:, 0, c * P:(c + 1) * P], work[:, 0, c * P:(c + 1) * P], tab["ident"][:, :])
                    last.then_inc(sem["at_mm"], 1)

                def values(q, gi):
                    if gi >= 2:
                        pe.wait_ge(sem["wv_done"], QG * q + gi - 1)
                    elif gi == 0:
                        pe.wait_ge(sem["s_lo"], QT * q + QT)
                        wait(pe, sem["moved"], 48 * q)
                    vg = pZ[gi % 2][:, :, :].rearrange("p k (a d) -> p (k a) d", d=D)
                    for c in range(EC):
                        last = nc.tensor.matmul(vg[:, c, :], tab["dst"][:, c * P:(c + 1) * P], vals[:, gi, :],
                                                start=True, stop=True)
                    last.then_inc(sem["vg_mm"], 1)

                def scatter(q, gi):
                    t, g = gi // TILE_GRAPHS, gi % TILE_GRAPHS
                    pe.wait_ge(sem["wv_hi_done"], QG * q + gi + 1)
                    pe.wait_ge(sem["wv_lo_done"], QG * q + gi + 1)
                    pe.wait_ge(sem["wv_lo_rest"], QG * q + gi + 1)
                    if g == 0 and t >= 2:
                        pe.wait_ge(sem["y_rows"], QT * q + t - 1)
                    for n, v in enumerate((wv_hi, wv_lo)):
                        for c in range(EC):
                            last = nc.tensor.matmul(pY[t % 2], tab["src"][:, g, c, :], v[gi % 2][:, c, :],
                                                    start=g == 0 and c == 0 and n == 0,
                                                    stop=g == TILE_GRAPHS - 1 and c == EC - 1 and n == 1)
                    last.then_inc(sem["scattered"], 1)

                def turn_sums(q, h, projected):
                    pe.wait_ge(sem["y_rows"], QT * q + 2 * h + 2)
                    if h == 0:
                        pe.wait_ge(sem["s_lo"], QT * q + projected)
                    else:
                        pe.wait_ge(sem["x2_done"], NH * q + h)
                    for t in range(2):
                        for k in range(KD):
                            last = nc.tensor.transpose(pYT[:, k, t * P:(t + 1) * P],
                                                       y_rows[:, t, k * P:(k + 1) * P], tab["ident"][:, :])
                    last.then_inc(sem["yT_mm"], 1)

                def project_out(q, h):
                    b, n = h % 2, NH * q + h
                    pe.wait_ge(sem["y_hi"], n + 1)
                    pe.wait_ge(sem["y_lo"], n + 1)
                    for t in range(GT // 2):
                        c = slice(t * P, (t + 1) * P)
                        for k in range(KD):
                            last = mm3(nc, pO[:, t, :], yT_hi[b][:, k, c], yT_lo[b][:, k, c], tab["wo_hi"][:, k, :],
                                       tab["wo_lo"][:, k, :], k == 0, k == KD - 1)
                    last.then_inc(sem["o_mm"], 1)

                def group(q, m, end=2 * NJ):
                    for i in range(GG):
                        gather(q, m, i)
                        if m + 1 < end:
                            if i == 0 and m < 2:
                                turn(q, m + 1)
                            if i == 1:
                                linear(q, m + 1)
                            if i % 2:
                                project(q, m + 1, i // 2)
                        if m + 2 < end:
                            if i == 3:
                                turn_back(q, m + 2)
                            if i == GG - 1 and 0 < m < NJ:
                                turn(q, m + 2)
                        if i == 2 and m + 1 < end:
                            pe.wait_ge(sem["lin_row"], NJ * q + m + 2)
                        if i:
                            score(q, m, i - 1)
                            if i == 2 and m + 1 < end:
                                turn_linear(q, m + 1)
                        elif m > 1:
                            score(q, m - 1, GG - 1)
                            if m == NJ:
                                add_linear(q)

                def body(q, last=False):
                    top = NJ - 1 if last else NJ
                    projected = QT if last else QT + AHEAD * GT
                    for m in range(1, top + 1):
                        group(q, m, NJ if last else 2 * NJ)
                    if last:
                        score(q, top, GG - 1)
                        add_linear(q)
                    turn_attention(q)
                    values(q, 0)
                    if not last:
                        score(q, top, GG - 1)
                    values(q, 1)
                    values(q, 2)
                    for gi in range(QG):
                        if gi % HG == 1 and gi > HG:
                            turn_sums(q, gi // HG - 1, projected)
                        if gi + 3 < QG:
                            values(q, gi + 3)
                        scatter(q, gi)
                        if gi % HG == 3 and gi > HG:
                            project_out(q, gi // HG - 1)
                    turn_sums(q, NH - 1, projected)
                    project_out(q, NH - 1)

                turn_back(0, 0)
                turn(0, 0)
                linear(0, 0)
                project(0, 0, 0)
                pe.wait_ge(sem["lin_row"], 1)
                turn_linear(0, 0)
                project(0, 0, 1)
                turn_back(0, 1)
                project(0, 0, 2)
                project(0, 0, 3)
                group(0, 0)
                score(0, 0, GG - 1)
                body(0)
                with pe.Fori(1, NQ - 1) as q:
                    body(q)
                body(NQ - 1, last=True)

            @block.scalar
            def _(act):
                def hi_halves(q, m):
                    act.wait_ge(sem["t2"], NJ * q + m + 1)
                    nc.scalar.activation(hT_hi[:, :, :], pT[:, :, :], ACT.Relu).then_inc(sem["h_hi"], 1)

                def copy_linear(q, m):
                    act.wait_ge(sem["lin_mm"], NJ * q + m + 1)
                    nc.scalar.activation(lin_row, pT[0:HEADS, 0, :], ACT.Copy).then_inc(sem["lin_row"], 1)

                def split_hi(q, m, t):
                    act.wait_ge(sem["u_mm"], QT * q + GT * m + t + 1)
                    if m == NJ and t == 0:
                        wait(act, sem["moved"], 48 * q)
                    made = bank(m, t).rearrange("p (a d) -> p a d", d=D)
                    for i, r in enumerate(halves):
                        gi = 2 * t + i
                        nc.scalar.activation(parts(r, m, gi), made[r], ACT.Copy).then_inc(sem["s_hi"], 1)

                def relu(q, m, i):
                    for k in range(KD):
                        act.wait_ge(sem["z_mm"], KD * (QG * q + GG * m + i) + k + 1)
                        nc.scalar.activation(r_hi[i % 2][:, k, :], pZ[i % 2][:, k, :], ACT.Relu).then_inc(sem["r_hi_done"], 1)

                def exponent(q):
                    act.wait_ge(sem["soft"], 8 * q + 4)
                    nc.scalar.activation(work[:, 1, :], work[:, 0, :], ACT.Exp).then_inc(sem["exp_done"], 1)

                def group(q, m, end=2 * NJ):
                    for i in range(GG):
                        relu(q, m, i)
                        if m + 1 < end:
                            if i == 0 and m < 2:
                                hi_halves(q, m + 1)
                            if i == 1:
                                copy_linear(q, m + 1)
                            if i % 2:
                                split_hi(q, m + 1, i // 2)
                        if m + 2 < end and i == GG - 1 and 0 < m < NJ:
                            hi_halves(q, m + 2)
                        if m == NJ and i == 4:
                            exponent(q)

                def body(q, last=False):
                    for m in range(1, NJ if last else NJ + 1):
                        group(q, m, NJ if last else 2 * NJ)
                    if last:
                        exponent(q)
                    act.wait_ge(sem["at_mm"], q + 1)
                    wait(act, sem["wv_done"], QG * q)
                    nc.scalar.activation(attn_T[:, :, :], pT[:, 0, :].rearrange("p (c r) -> p c r", c=EC), ACT.Copy)\
                        .then_inc(sem["attn_ready"], 1)

                    def halves_of_sums(h):
                        act.wait_ge(sem["yT_mm"], NH * q + h + 1)
                        nc.scalar.activation(yT_hi[h % 2], pYT, ACT.Copy).then_inc(sem["y_hi"], 1)

                    def rows_of_sums(t):
                        act.wait_ge(sem["scattered"], QG * q + TILE_GRAPHS * (t + 1))
                        if t >= 2:
                            act.wait_ge(sem["yT_mm"], NH * q + t // 2)
                        nc.scalar.activation(y_rows[:, t % 2, :], pY[t % 2], ACT.Copy).then_inc(sem["y_rows"], 1)

                    for gi in range(QG):
                        act.wait_ge(sem["wv_done"], QG * q + gi + 1)
                        if gi >= 2:
                            act.wait_ge(sem["scattered"], QG * q + gi - 1)
                        nc.scalar.activation(wv_hi[gi % 2], wv[gi % WB], ACT.Copy).then_inc(sem["wv_hi_done"], 1)
                        if gi >= 2 and gi % 2 == 0:
                            rows_of_sums(gi // 2 - 1)
                        if gi % HG == 2 and gi > HG:
                            halves_of_sums(gi // HG - 1)
                    rows_of_sums(QT - 1)
                    halves_of_sums(NH - 1)

                hi_halves(0, 0)
                copy_linear(0, 0)
                for t in range(GT):
                    split_hi(0, 0, t)
                group(0, 0)
                body(0)
                with act.Fori(1, NQ - 1) as q:
                    body(q)
                body(NQ - 1, last=True)

            @block.vector
            def _(dve):
                V = nc.vector

                def add_x(q, m):
                    G = NJ * q + m
                    dve.wait_ge(sem["t1"], G + 1)
                    V.tensor_tensor(x1_group(G), quad(pTr), quad(xt[m % 2][:, :, :]), ALU.add).then_inc(sem["x1_done"], 1)

                def measure(q, m):
                    G = NJ * q + m
                    dve.wait_ge(sem["x1_done"], G + 1)
                    wait(dve, sem["rstd_ready"], 2 * G)
                    V.memset(ve[:, :], EPS)
                    for t in range(GT):
                        last = V.bn_stats(st[:, t, :], x1_group(G)[:, t // KD, t % KD, :])
                    last.then_inc(sem["stats"], 1)

                def moments(q, m):
                    G = NJ * q + m
                    dve.wait_ge(sem["stats"], G + 1)
                    wait(dve, sem["normed"], 2 * G)
                    V.memset(unused[:, :], 0.0)
                    for t in range(GT):
                        last = V.bn_aggr(mv[:, t, :], st[:, t, :])
                    last.then_inc(sem["moments"], 1)
                    dve.wait_ge(sem["moments"], G + 1)
                    V.tensor_tensor(ve[:, :], ve[:, :], mv[:, :, 1], ALU.add).then_inc(sem["var_eps"], 1)

                def normalise(q, m):
                    G = NJ * q + m
                    dve.wait_ge(sem["rstd_ready"], 2 * G + 1)
                    xn = hst[m % 2][:, :, :].rearrange("p k (a d) -> p (k a) d", d=D)
                    for t in range(NT):
                        last = V.tensor_scalar(xn[:, t, :], x1_group(G)[:, t // KD, t % KD, :], mv[:, t, 0:1],
                                               rstd[:, t:t + 1], ALU.subtract, ALU.mult)
                    last.then_inc(sem["normed"], 1)

                def lo_halves(q, m):
                    dve.wait_ge(sem["h_hi"], NJ * q + m + 1)
                    V.scalar_tensor_tensor(out=hT_lo[:, :, :], in0=pT[:, :, :], scalar=0.0, in1=f32(hT_hi[:, :, :]),
                                           op0=ALU.max, op1=ALU.subtract).then_inc(sem["h_lo"], 1)

                def split_lin(q, m):
                    G, cols = NJ * q + m, slice(GG * HEADS * m, GG * HEADS * (m + 1))
                    dve.wait_ge(sem["lin_t"], G + 1)
                    if isinstance(G, int) and G == 0:
                        dve.wait_ge(sem["half_set"], 3)
                    if m == NJ:
                        wait(dve, sem["moved"], 48 * q)
                    part = pT[:, 1, 0:GT * HEADS].rearrange("p (t h) -> p t h", t=GT)
                    hi, lo = (v[:, cols].rearrange("p (t a h) -> p t a h", t=GT, h=HEADS) for v in (lin_hi, lin_lo))
                    for i, r in enumerate(halves):
                        V.tensor_copy(hi[r, :, i, :], part[r]).then_inc(sem["lin_part"], 1)
                    dve.wait_ge(sem["lin_part"], 2 * (G + 1))
                    for i, r in enumerate(halves):
                        last = V.tensor_tensor(lo[r, :, i, :], part[r], f32(hi[r, :, i, :]), ALU.subtract)
                    last.then_inc(sem["lin_done"], 1)

                def split_lo(q, m, t):
                    dve.wait_ge(sem["s_hi"], TILE_GRAPHS * (QT * q + GT * m + t + 1))
                    made = bank(m, t).rearrange("p (a d) -> p a d", d=D)
                    for i in range(2):
                        gi, own, other = 2 * t + i, halves[i], halves[1 - i]
                        last = V.tensor_tensor(parts(other, m, gi), made[own], f32(parts(own, m, gi)), ALU.subtract)
                    last.then_inc(sem["s_lo"], 1)

                def relu_lo(q, m, i):
                    for k in range(KD):
                        dve.wait_ge(sem["r_hi_done"], KD * (QG * q + GG * m + i) + k + 1)
                        V.scalar_tensor_tensor(out=r_lo[i % 2][:, k, :], in0=pZ[i % 2][:, k, :], scalar=0.0,
                                               in1=f32(r_hi[i % 2][:, k, :]), op0=ALU.max,
                                               op1=ALU.subtract).then_inc(sem["r_lo_done"], 1)

                def softmax_step(q, n):
                    w = [work[:, i, :] for i in range(4)]
                    cut, same = tab["cut"], tab["same"]
                    if n == 0:
                        dve.wait_ge(sem["e_mm"], q + 1)
                        wait(dve, sem["wv_lo_done"], QG * q)
                        wait(dve, sem["wv_lo_rest"], QG * q)
                        ins = V.tensor_tensor(w[0], pE, tab["log_w"][:, :], ALU.add)
                    if n == 1:
                        ins = V.tensor_tensor_scan(w[1], cut[:, 0:EDGES], w[0], 0.0, ALU.add, ALU.max)
                    if n == 2:
                        ins = V.tensor_tensor_scan(w[2][:, ::-1], cut[:, EDGES:0:-1], w[1][:, ::-1], 0.0, ALU.add, ALU.max)
                    if n == 3:
                        ins = V.tensor_tensor(w[0], w[0], w[2], ALU.subtract)
                    if n == 4:
                        dve.wait_ge(sem["exp_done"], q + 1)
                        ins = V.tensor_tensor_scan(w[2], same[:, 0:EDGES], w[1], 0.0, ALU.mult, ALU.add)
                    if n == 5:
                        ins = V.tensor_tensor_scan(w[3][:, ::-1], same[:, EDGES:0:-1], w[2][:, ::-1], 0.0, ALU.mult, ALU.max)
                    if n == 6:
                        ins = V.reciprocal(w[2], w[3])
                    if n == 7:
                        ins = V.tensor_tensor(w[0], w[1], w[2], ALU.mult)
                    ins.then_inc(sem["soft"], 1)
                    dve.wait_ge(sem["soft"], 8 * q + n + 1)

                SOFT_AT = {0: (0,), 1: (1,), 2: (2,), 3: (3,), 5: (4,), 6: (5, 6, 7)}

                def group(q, m, end=2 * NJ):
                    for i in range(GG):
                        relu_lo(q, m, i)
                        if m + 1 < end:
                            if i == 0 and m < 2:
                                lo_halves(q, m + 1)
                            if i == 2:
                                split_lin(q, m + 1)
                            if i % 2:
                                split_lo(q, m + 1, i // 2)
                        if m == NJ:
                            for n in SOFT_AT.get(i, ()):
                                softmax_step(q, n)
                        if m + 2 < end:
                            for at, part in ((3, add_x), (4, measure), (4, moments), (6, normalise)):
                                if i == at:
                                    part(q, m + 2)
                            if i == GG - 1 and 0 < m < NJ:
                                lo_halves(q, m + 2)

                def weigh(q, gi):
                    dve.wait_ge(sem["vg_mm"], QG * q + gi + 1)
                    if gi == 0:
                        dve.wait_ge(sem["attn_ready"], q + 1)
                    elif gi >= WB:
                        dve.wait_ge(sem["wv_lo_done"], QG * q + gi - WB + 1)
                        dve.wait_ge(sem["wv_lo_rest"], QG * q + gi - WB + 1)
                    shape = [P, EC, HEADS, DH]
                    V.tensor_tensor(wv[gi % WB].rearrange("p c (h d) -> p c h d", h=HEADS),
                                    pZ[gi % 2][:, :, :].rearrange("p k (a h d) -> p (k a) h d", h=HEADS, d=DH),
                                    attn_T[:, :, HEADS * gi:HEADS * (gi + 1)].unsqueeze(3).to_broadcast(shape),
                                    ALU.mult).then_inc(sem["wv_done"], 1)

                def body(q, last=False):
                    for m in range(1, NJ if last else NJ + 1):
                        group(q, m, NJ if last else 2 * NJ)
                    if last:
                        for n in range(8):
                            softmax_step(q, n)

                    def lo_of_sums(h):
                        dve.wait_ge(sem["y_hi"], NH * q + h + 1)
                        V.tensor_tensor(yT_lo[h % 2], pYT, f32(yT_hi[h % 2]),
                                        ALU.subtract).then_inc(sem["y_lo"], 1)

                    def add_out(h):
                        dve.wait_ge(sem["o_mm"], NH * q + h + 1)
                        part = HTg[:, h % 2, NJ * q + h // 2, :]
                        V.tensor_tensor(part, pU[:, :], part, ALU.add).then_inc(sem["x2_done"], 1)

                    weigh(q, 0)
                    weigh(q, 1)
                    for gi in range(QG):
                        dve.wait_ge(sem["wv_hi_done"], QG * q + gi + 1)
                        V.tensor_tensor(wv_lo[gi % 2][:, 0:NV, :], wv[gi % WB][:, 0:NV, :], f32(wv_hi[gi % 2][:, 0:NV, :]), ALU.subtract)\
                            .then_inc(sem["wv_lo_done"], 1)
                        if gi + 2 < QG:
                            weigh(q, gi + 2)
                        if gi % HG == 2 and gi > HG:
                            lo_of_sums(gi // HG - 1)
                        if gi % HG == 0 and gi > HG:
                            add_out(gi // HG - 2)
                    add_out(NH - 2)
                    lo_of_sums(NH - 1)
                    add_out(NH - 1)

                for part in (add_x, measure, moments, normalise, lo_halves):
                    part(0, 0)
                split_lo(0, 0, 0)
                split_lin(0, 0)
                split_lo(0, 0, 1)
                add_x(0, 1)
                split_lo(0, 0, 2)
                measure(0, 1)
                moments(0, 1)
                split_lo(0, 0, 3)
                normalise(0, 1)
                group(0, 0)
                body(0)
                with dve.Fori(1, NQ - 1) as q:
                    body(q)
                body(NQ - 1, last=True)


def attention_layer(core, a, x, x2, HT):
    with ExitStack() as ctx:
        sb, _ = allocator(core.nc, ctx)
        tab = {"ident": sb("t_ident", [P, P]), "both": sb("t_both", [P, EDGES], F32R), "dst": sb("t_dst", [P, EDGES], F32R),
               "src": sb("t_src", [P, TILE_GRAPHS, EC, P], F32R), "sign": sb("t_sign", [P, KD, 2 * P - HEADS], F32R),
               "log_w": sb("t_log_w", [P, EDGES]),
               "wqv_hi": sb("t_wqv_hi", [P, KD, 2 * D], F32R), "wqv_lo": sb("t_wqv_lo", [P, KD, 2 * D], F32R),
               "wo_hi": sb("t_wo_hi", [P, KD, D], F32R), "wo_lo": sb("t_wo_lo", [P, KD, D], F32R),
               "wl_hi": sb("t_wl_hi", [P, KD, HEADS], F32R), "wl_lo": sb("t_wl_lo", [P, KD, HEADS], F32R)}
        for n in ("same", "cut"):
            tab[n] = sb("t_" + n, [P, EDGES + 1])
        rows_ahead = ([sb(f"c_xt{b}", [P, GT, D]) for b in range(2)], [sb(f"c_hst{b}", [P, KD, GROWS]) for b in range(2)],
                      [core.sem(f"c_landed{b}") for b in range(2)])
        edge_tables(core, a, tab, x, HT, rows_ahead)
        edge_attention(core, x, x2, tab, HT, rows_ahead)


def conv_first(core, a, x2, H1, st1, W2, mhalf):
    nc = core.nc
    NI = NG // 2
    with ExitStack() as ctx:
        sb, ps = allocator(nc, ctx)
        an_t, an = sb("d_an_t", [NODES, NODES]), sb("d_an", [NODES, NODES])
        eye = sb("d_eye", [P, P])
        both, diag = sb("d_both", [NODES, NODES]), sb("d_diag", [NODES, NODES])
        ones = sb("d_ones", [NODES, P])
        deg, dcol = sb("d_deg", [P, 1]), sb("d_dcol", [P, 1])
        pick = sb("d_pick", [P, NODES])
        hat = sb("d_hat", [P, P])
        an_t2 = sb("d_an_t2", [P, NODES])
        eye2 = sb("d_eye2", [P, NODES])
        hat_hi, hat_lo = sb("d_hat_hi", [P, P], F32R), sb("d_hat_lo", [P, P], F32R)
        w1 = sb("d_w1", [P, KD, HID2])
        w1_hi, w1_lo = sb("d_w1_hi", [P, KD, HID2], F32R), sb("d_w1_lo", [P, KD, HID2], F32R)
        w2 = sb("d_w2", [P, KH, D])
        b1 = sb("d_b1", [P, KH])
        xt = [sb(f"d_xt{b}", [P, GT, D]) for b in range(2)]
        xn = [sb(f"d_xn{b}", [P, GT, D]) for b in range(2)]
        st, mv, ve, rstd = sb("d_st", [P, GT, 6]), sb("d_mv", [P, GT, 2]), sb("d_ve", [P, GT]), sb("d_rstd", [P, GT])
        h_hi = [sb(f"d_hhi{b}", [P, GT, D], F32R) for b in range(2)]
        h_lo = [sb(f"d_hlo{b}", [P, GT, D], F32R) for b in range(2)]
        g_hi = [sb(f"d_ghi{b}", [P, KD, GROWS], F32R) for b in range(2)]
        g_lo = [sb(f"d_glo{b}", [P, KD, GROWS], F32R) for b in range(2)]
        pA = [ps(f"d_pA{b}", [P, KD, GROWS]) for b in range(2)]
        pW = ps("d_pW", [P, KH, GROWS])
        names = ("consts w_in w1_ready half_set step deg_ready deg_mm root_ready diag_ready dinv_mm hat_ready stats moments var_eps rstd_ready normed "
                 "h_hi_done h_lo_done agg_mm g_hi_done g_lo_done w1_mm h1_done").split()
        sem = {n: core.sem("d_" + n) for n in names}
        landed = [core.sem(f"d_landed{b}") for b in range(2)]
        loads = [(eye[:, :], a["ident"]), (an_t[:, :], a["adj_t"]), (an[:, :], a["adj"]), (b1[:, :], a["b1"])]
        for g in range(TILE_GRAPHS):
            r = slice(g * NODES, (g + 1) * NODES)
            loads += [(an_t2[r, :], a["adj_t"]), (eye2[r, :], a["ident"][0:NODES, 0:NODES])]
        H1g = H1.rearrange("p k (g c) -> p k g c", c=GROWS)

        with nc.Block() as block:
            @block.sync
            def _(sp):
                for t, src in loads:
                    sp.dma_start(t, src).then_inc(sem["consts"], 16)
                for b in range(2):
                    sp.dma_start(xt[b][:, :, :], x2[b]).then_inc(landed[b], 16)
                sp.dma_start(w1[:, :, :], a["w1"]).then_inc(sem["w_in"], 16)
                sp.dma_start(w2[:, :, :], a["w2"]).then_inc(sem["w_in"], 16)

                def body(it):
                    for b in range(2):
                        sp.wait_ge(sem["normed"], 2 * it + b + 1)
                        sp.dma_start(xt[b][:, :, :], x2[2 * it + b + 2]).then_inc(landed[b], 16)

                peeled(sp, NI - 1, body)

            @block.gpsimd
            def _(pool):
                nc.gpsimd.memset(mhalf[:, :], -0.5).then_inc(sem["half_set"], 1)
                pool.wait_ge(sem["half_set"], 1)

                def root(g):
                    pool.wait_ge(sem["var_eps"], g + 1)
                    nc.gpsimd.tensor_tensor(rstd[:, :], ve[:, :], mhalf[:, :], ALU.pow).then_inc(sem["rstd_ready"], 1)

                pool.wait_ge(sem["deg_ready"], 1)
                nc.gpsimd.tensor_tensor(dcol[:, :], deg[:, :], mhalf[:, 0:1], ALU.pow).then_inc(sem["root_ready"], 1)
                with pool.Fori(0, NG) as g:
                    root(g)

            @block.tensor
            def _(pe):
                pe.wait_ge(sem["step"], 6)
                nc.tensor.matmul(pA[0][:, 0, 0:NODES], ones[:, :], both[:, :], start=True, stop=True).then_inc(sem["deg_mm"], 1)
                pe.wait_ge(sem["diag_ready"], 1)
                nc.tensor.matmul(pA[0][:, 1, 0:NODES], ones[:, :], diag[:, :], start=True, stop=True).then_inc(sem["dinv_mm"], 1)
                pe.wait_ge(sem["hat_ready"], 1)

                def body(it):
                    for b in range(2):
                        g = 2 * it + b
                        aggregate(g, b)
                        if isinstance(g, int) and g == 1:
                            pe.wait_ge(sem["w1_ready"], 1)
                        if not (isinstance(g, int) and g == 0):
                            first(g - 1, 1 - b)

                def aggregate(g, b):
                    pe.wait_ge(sem["h_lo_done"], g + 1)
                    pe.wait_ge(sem["h_hi_done"], g + 1)
                    for k in range(KD):
                        c = slice(k * P, (k + 1) * P)
                        for t in range(GT):
                            last = mm3(nc, pA[b][:, k, t * P:(t + 1) * P], h_hi[b][:, t, c], h_lo[b][:, t, c],
                                       hat_hi[:, :], hat_lo[:, :], True, True)
                    last.then_inc(sem["agg_mm"], 1)

                def first(g, b):
                    pe.wait_ge(sem["g_hi_done"], g + 1)
                    pe.wait_ge(sem["g_lo_done"], g + 1)
                    for m in range(KH):
                        wait(pe, sem["h1_done"], KH * (g - 1) + m + 1)
                        c = slice(m * P, (m + 1) * P)
                        for k in range(KD):
                            last = mm3(nc, pW[:, m, :], w1_hi[:, k, c], w1_lo[:, k, c], g_hi[b][:, k, :], g_lo[b][:, k, :],
                                       k == 0, k == KD - 1)
                        last.then_inc(sem["w1_mm"], 1)

                peeled(pe, NI, body)
                first(NG - 1, 1)

            @block.scalar
            def _(act):
                act.wait_ge(sem["consts"], 16 * len(loads))

                def keep(g):
                    for m in range(KH):
                        act.wait_ge(sem["w1_mm"], KH * g + m + 1)
                        nc.scalar.activation(H1g[:, m, g, :], pW[:, m, :], ACT.Identity, bias=b1[:, m:m + 1])\
                            .then_inc(sem["h1_done"], 1)

                def relu(g, b):
                    act.wait_ge(sem["normed"], g + 1)
                    wait(act, sem["agg_mm"], g - 1)
                    nc.scalar.activation(h_hi[b][:, :, :], xn[b][:, :, :], ACT.Relu).then_inc(sem["h_hi_done"], 1)

                relu(0, 0)

                def body(it):
                    for b in range(2):
                        g = 2 * it + b
                        if not (isinstance(g, int) and g == NG - 1):
                            relu(g + 1, 1 - b)
                        act.wait_ge(sem["agg_mm"], g + 1)
                        nc.scalar.activation(g_hi[b][:, :, :], pA[b][:, :, :], ACT.Copy).then_inc(sem["g_hi_done"], 1)
                        if not (isinstance(g, int) and g == 0):
                            keep(g - 1)

                both_ends(act, NI, body)
                keep(NG - 1)

            @block.vector
            def _(dve):
                V = nc.vector
                link = Chain(dve, sem["step"])
                def moments(g, b):
                    dve.wait_ge(landed[b], 8 * (g - b) + 16)
                    for t in range(GT):
                        last = V.bn_stats(st[:, t, :], xt[b][:, t, :])
                    last.then_inc(sem["stats"], 1)
                    dve.wait_ge(sem["stats"], g + 1)
                    wait(dve, sem["rstd_ready"], g)
                    V.memset(ve[:, :], EPS)
                    for t in range(GT):
                        last = V.bn_aggr(mv[:, t, :], st[:, t, :])
                    last.then_inc(sem["moments"], 1)
                    dve.wait_ge(sem["moments"], g + 1)
                    V.tensor_tensor(ve[:, :], ve[:, :], mv[:, :, 1], ALU.add).then_inc(sem["var_eps"], 1)

                def normalise(g, b):
                    dve.wait_ge(sem["rstd_ready"], g + 1)
                    if not (isinstance(g, int) and g < 2):
                        dve.wait_ge(sem["h_lo_done"], g - 1)
                    for t in range(GT):
                        last = V.tensor_scalar(xn[b][:, t, :], xt[b][:, t, :], mv[:, t, 0:1], rstd[:, t:t + 1],
                                               ALU.subtract, ALU.mult)
                    last.then_inc(sem["normed"], 1)

                def lo_halves(g, b):
                    dve.wait_ge(sem["h_hi_done"], g + 1)
                    V.scalar_tensor_tensor(out=h_lo[b][:, :, :], in0=xn[b][:, :, :], scalar=0.0, in1=f32(h_hi[b][:, :, :]),
                                           op0=ALU.max, op1=ALU.subtract).then_inc(sem["h_lo_done"], 1)

                def measure(g, m):
                    dve.wait_ge(sem["h1_done"], KH * g + m + 1)
                    V.bn_stats(st1[:, m, g, :], H1g[:, m, g, :])

                link = Chain(dve, sem["step"])

                def split(raw, hi, lo):
                    link(V.tensor_copy(hi[:, :, :], raw[:, :, :]))
                    link(V.tensor_tensor(lo[:, :, :], raw[:, :, :], f32(hi[:, :, :]), ALU.subtract))

                dve.wait_ge(sem["consts"], 16 * len(loads))
                link(V.tensor_tensor(an_t[:, :], an_t[:, :], eye[0:NODES, 0:NODES], ALU.add))
                link(V.tensor_tensor(an[:, :], an[:, :], eye[0:NODES, 0:NODES], ALU.add))
                link(V.tensor_tensor(diag[:, :], an[:, :], eye[0:NODES, 0:NODES], ALU.mult))
                link(V.tensor_tensor(both[:, :], an[:, :], an_t[:, :], ALU.add))
                link(V.tensor_tensor(both[:, :], both[:, :], diag[:, :], ALU.subtract))
                link(V.memset(ones[:, :], 1.0))
                dve.wait_ge(sem["deg_mm"], 1)
                link(V.tensor_tensor(pick[:, :], pA[0][:, 0, 0:NODES], eye2[:, :], ALU.mult))
                V.tensor_reduce(deg[:, :], pick[:, :], AX.X, ALU.add).then_inc(sem["deg_ready"], 1)
                moments(0, 0)
                normalise(0, 0)
                moments(1, 1)
                dve.wait_ge(sem["root_ready"], 1)
                V.tensor_scalar(diag[:, :], eye2[0:NODES, :], dcol[0:NODES, 0:1], None, ALU.mult).then_inc(sem["diag_ready"], 1)
                link(V.tensor_tensor(an_t2[:, :], an_t2[:, :], eye2[:, :], ALU.add))
                link(V.memset(hat[:, :], 0.0))
                dve.wait_ge(sem["dinv_mm"], 1)
                for g in range(TILE_GRAPHS):
                    r = slice(g * NODES, (g + 1) * NODES)
                    link(V.scalar_tensor_tensor(out=hat[r, r], in0=an_t2[r, :], scalar=dcol[r, 0:1], in1=pA[0][r, 1, 0:NODES],
                                                op0=ALU.mult, op1=ALU.mult))
                link(V.tensor_copy(hat_hi[:, :], hat[:, :]))
                V.tensor_tensor(hat_lo[:, :], hat[:, :], f32(hat_hi[:, :]), ALU.subtract).then_inc(sem["hat_ready"], 1)
                lo_halves(0, 0)
                normalise(1, 1)
                dve.wait_ge(sem["w_in"], 32)
                split(w1, w1_hi, w1_lo)
                V.memset(deg[:, :], 0.0).then_inc(sem["w1_ready"], 1)

                def body(it):
                    for b in range(2):
                        g = 2 * it + b
                        dve.wait_ge(sem["g_hi_done"], g + 1)
                        V.tensor_tensor(g_lo[b][:, :, :], pA[b][:, :, :], f32(g_hi[b][:, :, :]), ALU.subtract)\
                            .then_inc(sem["g_lo_done"], 1)
                        if not (isinstance(g, int) and g >= NG - 2):
                            moments(g + 2, b)
                        if not (isinstance(g, int) and g == NG - 1):
                            lo_halves(g + 1, 1 - b)
                        if not (isinstance(g, int) and g == 0):
                            for m in range(KH):
                                measure(g - 1, m)
                        if not (isinstance(g, int) and g >= NG - 2):
                            normalise(g + 2, b)

                both_ends(dve, NI, body)
                for m in range(KH):
                    measure(NG - 1, m)
                split(w2, *W2)


def conv_second(core, a, H1, st1, st2, W2, mhalf):
    nc = core.nc
    NI = NG // 2
    with ExitStack() as ctx:
        sb, ps = allocator(nc, ctx)
        unused = sb("f_unused", [P, 1])
        g1, be1, b2 = sb("f_g1", [P, KH]), sb("f_be1", [P, KH]), sb("f_b2", [P, KD])
        mv, ve, rstd = sb("f_mv", [P, KH, 2]), sb("f_ve", [P, KH]), sb("f_rstd", [P, KH])
        scale, shift, moved = sb("f_scale", [P, KH]), sb("f_shift", [P, KH]), sb("f_moved", [P, KH])
        r = [sb(f"f_r{b}", [P, KH, GROWS]) for b in range(2)]
        r_hi = [sb(f"f_rhi{b}", [P, KH, GROWS], F32R) for b in range(2)]
        r_lo = [sb(f"f_rlo{b}", [P, KH, GROWS], F32R) for b in range(2)]
        pO = [ps(f"f_pO{b}", [P, KD, GROWS]) for b in range(2)]
        names = "consts step ve_ready rstd_ready affine_ready relu_done hi_done lo_done o_mm o_done".split()
        sem = {n: core.sem("f_" + n) for n in names}
        H1g = H1.rearrange("p k (g c) -> p k g c", c=GROWS)
        loads = [(g1, a["g1"]), (be1, a["be1"]), (b2, a["b2"])]
        with nc.Block() as block:
            @block.sync
            def _(sp):
                for t, src in loads:
                    sp.dma_start(t[:, :], src).then_inc(sem["consts"], 16)

            @block.gpsimd
            def _(pool):
                pool.wait_ge(sem["ve_ready"], 1)
                nc.gpsimd.tensor_tensor(rstd[:, :], ve[:, :], mhalf[:, :], ALU.pow).then_inc(sem["rstd_ready"], 1)

            @block.vector
            def _(dve):
                V = nc.vector
                link = Chain(dve, sem["step"])
                dve.wait_ge(sem["consts"], 16 * len(loads))
                for m in range(KH):
                    link(V.bn_aggr(mv[:, m, :], st1[:, m, :, :].rearrange("p g s -> p (g s)")))
                V.tensor_scalar(ve[:, :], mv[:, :, 1], EPS, None, ALU.add).then_inc(sem["ve_ready"], 1)
                dve.wait_ge(sem["rstd_ready"], 1)
                link(V.tensor_tensor(scale[:, :], g1[:, :], rstd[:, :], ALU.mult))
                link(V.tensor_tensor(moved[:, :], mv[:, :, 0], scale[:, :], ALU.mult))
                V.tensor_tensor(shift[:, :], be1[:, :], moved[:, :], ALU.subtract).then_inc(sem["affine_ready"], 1)

                def split(g, b):
                    dve.wait_ge(sem["relu_done"], g + 1)
                    wait(dve, sem["o_mm"], g - 1)
                    V.tensor_copy(r_hi[b][:, :, :], r[b][:, :, :]).then_inc(sem["hi_done"], 1)
                    dve.wait_ge(sem["hi_done"], g + 1)
                    V.tensor_tensor(r_lo[b][:, :, :], r[b][:, :, :], f32(r_hi[b][:, :, :]), ALU.subtract)\
                        .then_inc(sem["lo_done"], 1)

                def measure(g, b):
                    dve.wait_ge(sem["o_done"], g + 1)
                    for m in range(KD):
                        V.bn_stats(st2[:, m, g, :], H1g[:, m, g, :])

                split(0, 0)

                def body(it):
                    for b in range(2):
                        g = 2 * it + b
                        if not (isinstance(g, int) and g == NG - 1):
                            split(g + 1, 1 - b)
                        measure(g, b)

                both_ends(dve, NI, body)

            @block.scalar
            def _(act):
                act.wait_ge(sem["affine_ready"], 1)

                def relu(g, b):
                    wait(act, sem["lo_done"], g - 1)
                    for m in range(KH):
                        last = nc.scalar.activation(r[b][:, m, :], H1g[:, m, g, :], ACT.Relu, bias=shift[:, m:m + 1],
                                                    scale=scale[:, m:m + 1])
                    last.then_inc(sem["relu_done"], 1)

                def keep(g, b):
                    wait(act, sem["o_done"], g)
                    act.wait_ge(sem["o_mm"], g + 1)
                    nc.scalar.activation(unused[:, :], scale[:, 0:1], ACT.Copy)
                    for m in range(KD):
                        last = nc.scalar.activation(H1g[:, m, g, :], pO[b][:, m, :], ACT.Identity, bias=b2[:, m:m + 1])
                    last.then_inc(sem["o_done"], 1)

                relu(0, 0)
                relu(1, 1)

                def body(it):
                    for b in range(2):
                        g = 2 * it + b
                        if not (isinstance(g, int) and g >= NG - 2):
                            relu(g + 2, b)
                        keep(g, b)

                both_ends(act, NI, body)

            @block.tensor
            def _(pe):
                def body(it):
                    for b in range(2):
                        g = 2 * it + b
                        pe.wait_ge(sem["lo_done"], g + 1)
                        wait(pe, sem["o_done"], g - 1)
                        for m in range(KD):
                            c = slice(m * P, (m + 1) * P)
                            for k in range(KH):
                                last = mm3(nc, pO[b][:, m, :], W2[0][:, k, c], W2[1][:, k, c], r_hi[b][:, k, :],
                                           r_lo[b][:, k, :], k == 0, k == KH - 1)
                        last.then_inc(sem["o_mm"], 1)

                peeled(pe, NI, body)


def dense_attention(core, a, x2, out, H1, st2, mhalf):
    nc = core.nc
    NX = 4
    NI = NG // NX
    MASK = -2.0 ** 127
    with ExitStack() as ctx:
        sb, ps = allocator(nc, ctx)
        ident, ident_r = sb("e_ident", [P, P]), sb("e_ident_r", [P, P], F32R)
        g2, be2 = sb("e_g2", [P, KD]), sb("e_be2", [P, KD])
        mv2, ve2, rstd2 = sb("e_mv2", [P, KD, 2]), sb("e_ve2", [P, KD]), sb("e_rstd2", [P, KD])
        scale, shift, moved = sb("e_scale", [P, KD]), sb("e_shift", [P, KD]), sb("e_moved", [P, KD])
        w_raw = sb("e_w_raw", [P, KD, D])
        w_hi, w_lo = sb("e_w_hi", [P, KD, D], F32R), sb("e_w_lo", [P, KD, D], F32R)
        wa = sb("e_wa", [P, KD, 2])
        wa_hi, wa_lo = sb("e_wa_hi", [P, KD, 2, P], F32R), sb("e_wa_lo", [P, KD, 2, P], F32R)
        a_row = sb("e_a_row", [P, 2, D])
        prod = sb("e_prod", [P, KD, D])
        adj2 = sb("e_adj2", [P, NODES])
        mask = sb("e_mask", [P, GT, P], F32R)
        y = sb("e_y", [P, KD, GROWS])
        free = H1[:, KD:, :].rearrange("p k (g t d) -> p (k g) t d", t=GT, d=D)
        x3, xt, res = ([free[:, at + b] for b in range(n)] for at, n in ((0, NX), (NX, 2), (NX + 2, 2)))
        xn = sb("e_xn", [P, GT, D])
        st, mv, ve, rstd = sb("e_st", [P, GT, 6]), sb("e_mv", [P, GT, 2]), sb("e_ve", [P, GT]), sb("e_rstd", [P, GT])
        off = sb("e_off", [P, GT])
        hT_hi, hT_lo = sb("e_hThi", [P, KD, GROWS], F32R), sb("e_hTlo", [P, KD, GROWS], F32R)
        v_hi = [sb(f"e_vhi{b}", [P, GT, D], F32R) for b in range(2)]
        v_lo = [sb(f"e_vlo{b}", [P, GT, D], F32R) for b in range(2)]
        e = sb("e_e", [P, GT, NODES])
        top, total, inv = sb("e_top", [P, GT]), sb("e_total", [P, GT]), sb("e_inv", [P, GT])
        prob = sb("e_prob", [P, GT, P])
        p_hi, p_lo = sb("e_phi", [P, GT, P], F32R), sb("e_plo", [P, GT, P], F32R)
        pT = ps("e_pT", [P, KD, GROWS])
        pW, pO = ps("e_pW", [P, GT, D]), ps("e_pO", [P, GT, D])
        pS, pP = ps("e_pS", [P, GT, P]), ps("e_pP", [P, GT, P])
        pTr = pT[:, :, :].rearrange("p k (a d) -> p (k a) d", d=D)
        names = ("consts step ve2_ready rstd2_ready ready y_done t1 x3_done stats moments var_eps "
                 "rstd_ready off_ready normed t2 h_hi h_lo w_mm s_mm e_done v_hi_done v_lo_done soft exp_done t3 p_hi_done "
                 "p_lo_done o_mm out_done").split()
        sem = {n: core.sem("e_" + n) for n in names}
        landed = [core.sem(f"e_landed{b}") for b in range(2)]
        stored = [core.sem(f"e_stored{b}") for b in range(2)]
        H1g = H1.rearrange("p k (g c) -> p k g c", c=GROWS)
        loads = [(ident[:, :], a["ident"]), (g2[:, :], a["g2"]), (be2[:, :], a["be2"]), (w_raw[:, :, :], a["w3"]),
                 (a_row[:, :, :], a["a3"].rearrange("p (h d) -> p h d", h=2))]
        for g in range(TILE_GRAPHS):
            loads.append((adj2[g * NODES:(g + 1) * NODES, :], a["adj"]))
        blocks = [slice(h * NODES, (h + 1) * NODES) for h in range(TILE_GRAPHS)]
        SOFT = 5

        def exists(g):
            return not isinstance(g, int) or 0 <= g < NG

        def steps(eng, step):
            def body(it):
                for b in range(NX):
                    step(NX * it + b, b)

            both_ends(eng, NI, body)

        with nc.Block() as block:
            @block.sync
            def _(sp):
                for t, src in loads:
                    sp.dma_start(t, src).then_inc(sem["consts"], 16)
                for b in range(2):
                    sp.dma_start(xt[b], x2[b]).then_inc(landed[b], 16)

                def step(g, b):
                    if exists(g + 2):
                        sp.wait_ge(sem["x3_done"], g + 1)
                        sp.dma_start(xt[b % 2], x2[g + 2]).then_inc(landed[b % 2], 16)
                    if exists(g - 2):
                        sp.wait_ge(sem["out_done"], g - 1)
                        sp.dma_start(out[g - 2], res[b % 2]).then_inc(stored[b % 2], 16)

                steps(sp, step)
                for g in range(NG - 2, NG):
                    sp.wait_ge(sem["out_done"], g + 1)
                    sp.dma_start(out[g], res[g % 2]).then_inc(stored[g % 2], 16)
                for b in range(2):
                    sp.wait_ge(stored[b], 16 * NG // 2)

            @block.gpsimd
            def _(pool):
                pool.wait_ge(sem["ve2_ready"], 1)
                nc.gpsimd.tensor_tensor(rstd2[:, :], ve2[:, :], mhalf[:, 0:KD], ALU.pow).then_inc(sem["rstd2_ready"], 1)

                def root(g):
                    pool.wait_ge(sem["var_eps"], g + 1)
                    wait(pool, sem["normed"], g)
                    nc.gpsimd.tensor_tensor(rstd[:, :], ve[:, :], mhalf[:, :], ALU.pow).then_inc(sem["rstd_ready"], 1)

                peeled(pool, NG, root)

            @block.tensor
            def _(pe):
                def rows(g):
                    pe.wait_ge(sem["y_done"], g + 1)
                    if isinstance(g, int) and g <= 2:
                        wait(pe, sem["h_lo"], min(g, 1))
                        wait(pe, sem["x3_done"], g)
                    else:
                        pe.wait_ge(sem["h_lo"], g - 1)
                    for t in range(GT):
                        for k in range(KD):
                            last = nc.tensor.transpose(pTr[:, t, k * P:(k + 1) * P], y[:, k, t * P:(t + 1) * P], ident[:, :])
                    last.then_inc(sem["t1"], 1)

                def turn(g):
                    pe.wait_ge(sem["normed"], g + 1)
                    if not (isinstance(g, int) and g == 0):
                        pe.wait_ge(sem["x3_done"], g + 2 if exists(g + 1) else NG)
                    for t in range(GT):
                        for k in range(KD):
                            last = nc.tensor.transpose(pT[:, k, t * P:(t + 1) * P], xn[:, t, k * P:(k + 1) * P], ident[:, :])
                    last.then_inc(sem["t2"], 1)

                def score(g):
                    pe.wait_ge(sem["h_lo"], g + 1)
                    pe.wait_ge(sem["h_hi"], g + 1)
                    wait(pe, sem["e_done"], 2 * g)
                    flat = pS[:, :, :].rearrange("p t r -> p (t r)")
                    nc.tensor.matmul(flat, ident_r[:, :], mask[:, :, :].rearrange("p t r -> p (t r)"), start=True, stop=False)
                    for k in range(KD):
                        mm3(nc, flat, wa_hi[:, k, 1, :], wa_lo[:, k, 1, :], hT_hi[:, k, :], hT_lo[:, k, :], False, False)
                    for t in range(GT):
                        c = slice(t * P, (t + 1) * P)
                        for k in range(KD):
                            last = mm3(nc, pS[:, t, :], hT_hi[:, k, c], hT_lo[:, k, c], wa_hi[:, k, 0, :], wa_lo[:, k, 0, :],
                                       False, t == GT - 1 and k == KD - 1)
                    last.then_inc(sem["s_mm"], 1)

                def project(g):
                    wait(pe, sem["v_lo_done"], g)
                    for t in range(GT):
                        c = slice(t * P, (t + 1) * P)
                        for k in range(KD):
                            last = mm3(nc, pW[:, t, :], hT_hi[:, k, c], hT_lo[:, k, c], w_hi[:, k, :], w_lo[:, k, :],
                                       k == 0, k == KD - 1)
                    last.then_inc(sem["w_mm"], 1)

                def attend(g, b):
                    pe.wait_ge(sem["v_lo_done"], g + 1)
                    pe.wait_ge(sem["p_hi_done"], g + 1)
                    pe.wait_ge(sem["p_lo_done"], g + 1)
                    wait(pe, sem["out_done"], g)
                    for t in range(GT):
                        last = mm3(nc, pO[:, t, :], p_hi[:, t, :], p_lo[:, t, :], v_hi[b % 2][:, t, :], v_lo[b % 2][:, t, :],
                                   True, True)
                    last.then_inc(sem["o_mm"], 1)

                def turn_prob(g):
                    pe.wait_ge(sem["exp_done"], 2 * g + 2)
                    wait(pe, sem["p_lo_done"], g)
                    for t in range(GT):
                        last = nc.tensor.transpose(pP[:, t, :], prob[:, t, :], ident[:, :])
                    last.then_inc(sem["t3"], 1)

                pe.wait_ge(sem["consts"], 16 * len(loads))
                rows(0)
                turn(0)
                rows(1)
                rows(2)
                pe.wait_ge(sem["ready"], 1)

                def step(g, b):
                    score(g)
                    project(g)
                    if exists(g + 1):
                        turn(g + 1)
                    if exists(g - 1):
                        attend(g - 1, b - 1)
                    turn_prob(g)
                    if exists(g + 3):
                        rows(g + 3)

                steps(pe, step)
                attend(NG - 1, NX - 1)

            @block.scalar
            def _(act):
                def second_norm(g):
                    wait(act, sem["t1"], g)
                    for k in range(KD):
                        last = nc.scalar.activation(y[:, k, :], H1g[:, k, g, :], ACT.Identity, bias=shift[:, k:k + 1],
                                                    scale=scale[:, k:k + 1])
                    last.then_inc(sem["y_done"], 1)

                def normalise(g, b):
                    act.wait_ge(sem["off_ready"], g + 1)
                    wait(act, sem["t2"], g)
                    for t in range(GT):
                        last = nc.scalar.activation(xn[:, t, :], x3[b % NX][:, t, :], ACT.Identity, bias=off[:, t:t + 1],
                                                    scale=rstd[:, t:t + 1])
                    last.then_inc(sem["normed"], 1)

                def relu(g):
                    act.wait_ge(sem["t2"], g + 1)
                    nc.scalar.activation(hT_hi[:, :, :], pT[:, :, :], ACT.Relu).then_inc(sem["h_hi"], 1)

                act.wait_ge(sem["step"], KD + 3)
                second_norm(0)
                normalise(0, 0)
                second_norm(1)
                relu(0)
                normalise(1, 1)
                second_norm(2)

                def step(g, b):
                    if exists(g + 3):
                        second_norm(g + 3)
                    act.wait_ge(sem["s_mm"], g + 1)
                    wait(act, sem["exp_done"], 2 * g)
                    for r in blocks:
                        nc.scalar.activation(e[r, :, :], pS[r, :, r], ACT.Copy).then_inc(sem["e_done"], 1)
                    act.wait_ge(sem["soft"], SOFT * g + 3)
                    wait(act, sem["t3"], g)
                    for r in blocks:
                        nc.scalar.activation(prob[r, :, r], e[r, :, :], ACT.Exp).then_inc(sem["exp_done"], 1)
                    act.wait_ge(sem["w_mm"], g + 1)
                    wait(act, sem["o_mm"], g - 1)
                    nc.scalar.activation(v_hi[b % 2][:, :, :], pW[:, :, :], ACT.Copy).then_inc(sem["v_hi_done"], 1)
                    if exists(g + 1):
                        relu(g + 1)
                    act.wait_ge(sem["t3"], g + 1)
                    nc.scalar.activation(p_hi[:, :, :], pP[:, :, :], ACT.Copy).then_inc(sem["p_hi_done"], 1)
                    if exists(g + 2):
                        normalise(g + 2, b + 2)

                steps(act, step)

            @block.vector
            def _(dve):
                V = nc.vector
                link = Chain(dve, sem["step"])
                dve.wait_ge(sem["consts"], 16 * len(loads))
                for m in range(KD):
                    link(V.bn_aggr(mv2[:, m, :], st2[:, m, :, :].rearrange("p g s -> p (g s)")))
                V.tensor_scalar(ve2[:, :], mv2[:, :, 1], EPS, None, ALU.add).then_inc(sem["ve2_ready"], 1)
                dve.wait_ge(sem["rstd2_ready"], 1)
                link(V.tensor_tensor(scale[:, :], g2[:, :], rstd2[:, :], ALU.mult))
                link(V.tensor_tensor(moved[:, :], mv2[:, :, 0], scale[:, :], ALU.mult))
                link(V.tensor_tensor(shift[:, :], be2[:, :], moved[:, :], ALU.subtract))

                def fold(i):
                    link(V.tensor_tensor(prod[:, :, :], w_raw[:, :, :], a_row[:, i, :].unsqueeze(1).to_broadcast([P, KD, D]),
                                         ALU.mult))
                    link(V.tensor_reduce(wa[:, :, i:i + 1], prod[:, :, :], AX.X, ALU.add))

                def weights():
                    alike = wa[:, :, :].unsqueeze(3).to_broadcast([P, KD, 2, P])
                    for full, hi, lo in ((alike, wa_hi[:, :, :, :], wa_lo[:, :, :, :]), (w_raw[:, :, :], w_hi[:, :, :], w_lo[:, :, :])):
                        link(V.tensor_copy(hi, full))
                        link(V.tensor_tensor(lo, full, f32(hi), ALU.subtract))
                    link(V.tensor_copy(ident_r[:, :], ident[:, :]))
                    link(V.memset(f32(mask[:, :, :]), 0.0))
                    for r in blocks:
                        link(V.tensor_scalar(mask[r, :, r], adj2[r, :].unsqueeze(1).to_broadcast([NODES, GT, NODES]), 0.0, MASK,
                                             ALU.is_equal, ALU.mult))
                    V.memset(prob[:, :, :], 0.0).then_inc(sem["ready"], 1)

                def add_x(g, b):
                    rows = x3[b % NX]
                    dve.wait_ge(landed[b % 2], 8 * (g - b % 2) + 16)
                    dve.wait_ge(sem["t1"], g + 1)
                    V.tensor_tensor(rows, pTr, xt[b % 2], ALU.add).then_inc(sem["x3_done"], 1)
                    dve.wait_ge(sem["x3_done"], g + 1)
                    for t in range(GT):
                        last = V.bn_stats(st[:, t, :], rows[:, t, :])
                    last.then_inc(sem["stats"], 1)
                    dve.wait_ge(sem["stats"], g + 1)
                    wait(dve, sem["rstd_ready"], g)
                    V.memset(ve[:, :], EPS)
                    for t in range(GT):
                        last = V.bn_aggr(mv[:, t, :], st[:, t, :])
                    last.then_inc(sem["moments"], 1)
                    dve.wait_ge(sem["moments"], g + 1)
                    V.tensor_tensor(ve[:, :], ve[:, :], mv[:, :, 1], ALU.add).then_inc(sem["var_eps"], 1)

                def offset(g):
                    dve.wait_ge(sem["rstd_ready"], g + 1)
                    wait(dve, sem["normed"], g)
                    V.scalar_tensor_tensor(out=off[:, :], in0=mv[:, :, 0], scalar=-1.0, in1=rstd[:, :], op0=ALU.mult,
                                           op1=ALU.mult).then_inc(sem["off_ready"], 1)

                def lo_halves(g):
                    dve.wait_ge(sem["h_hi"], g + 1)
                    V.scalar_tensor_tensor(out=hT_lo[:, :, :], in0=pT[:, :, :], scalar=0.0, in1=f32(hT_hi[:, :, :]),
                                           op0=ALU.max, op1=ALU.subtract).then_inc(sem["h_lo"], 1)

                def add_out(g, b):
                    dve.wait_ge(sem["o_mm"], g + 1)
                    if not (isinstance(g, int) and g < 2):
                        dve.wait_ge(stored[b % 2], 8 * (g - b % 2))
                    for t in range(GT):
                        last = V.scalar_tensor_tensor(out=res[b % 2][:, t, :], in0=pO[:, t, :], scalar=inv[:, t:t + 1],
                                                      in1=x3[b % NX][:, t, :], op0=ALU.mult, op1=ALU.add)
                    last.then_inc(sem["out_done"], 1)

                fold(0)
                add_x(0, 0)
                fold(1)
                offset(0)
                weights()
                lo_halves(0)
                add_x(1, 1)
                offset(1)
                add_x(2, 2)

                def step(g, b):
                    n = [0]

                    def link(ins):
                        n[0] += 1
                        ins.then_inc(sem["soft"], 1)
                        dve.wait_ge(sem["soft"], SOFT * g + n[0])

                    if exists(g + 2):
                        offset(g + 2)
                    dve.wait_ge(sem["e_done"], 2 * g + 2)
                    link(V.scalar_tensor_tensor(out=e[:, :, :], in0=e[:, :, :], scalar=LEAK, in1=e[:, :, :],
                                                op0=ALU.mult, op1=ALU.max))
                    link(V.tensor_reduce(top[:, :], e[:, :, :], AX.X, ALU.max))
                    link(V.tensor_tensor(e[:, :, :], e[:, :, :], top[:, :].unsqueeze(2).to_broadcast([P, GT, NODES]), ALU.subtract))
                    dve.wait_ge(sem["v_hi_done"], g + 1)
                    V.tensor_tensor(v_lo[b % 2][:, :, :], pW[:, :, :], f32(v_hi[b % 2][:, :, :]), ALU.subtract)\
                        .then_inc(sem["v_lo_done"], 1)
                    if exists(g + 1):
                        lo_halves(g + 1)
                    if exists(g - 1):
                        add_out(g - 1, b - 1)
                        dve.wait_ge(sem["out_done"], g)
                    dve.wait_ge(sem["exp_done"], 2 * g + 2)
                    link(V.tensor_reduce(total[:, :], prob[:, :, :], AX.X, ALU.add))
                    link(V.reciprocal(inv[:, :], total[:, :]))
                    dve.wait_ge(sem["p_hi_done"], g + 1)
                    V.tensor_tensor(p_lo[:, :, :], pP[:, :, :], f32(p_hi[:, :, :]), ALU.subtract).then_inc(sem["p_lo_done"], 1)
                    if exists(g + 3):
                        dve.wait_ge(sem["out_done"], g)
                        add_x(g + 3, b + 3)

                steps(dve, step)
                add_out(NG - 1, NX - 1)


def later_layers(core, a, x2, out):
    with ExitStack() as ctx:
        sb, _ = allocator(core.nc, ctx)
        H1 = sb("H1", [P, KH, ROWS])[:, :, :]
        mhalf = sb("half", [P, GT])
        st1, st2 = sb("st1", [P, KH, NG, 6]), sb("st2", [P, KD, NG, 6])
        with ExitStack() as inner:
            sb2, _ = allocator(core.nc, inner)
            W2 = [sb2(f"w2_{n}", [P, KH, D], F32R) for n in ("hi", "lo")]
            conv_first(core, a, x2, H1, st1, W2, mhalf)
            conv_second(core, a, H1, st1, st2, W2, mhalf)
        dense_attention(core, a, x2, out, H1, st2, mhalf)


def build(nc, args):
    with ExitStack() as ctx:
        core = Core(nc, ctx)

        def groups(rows):
            return rows.rearrange("(g t p) d -> g p t d", t=GT, p=P)

        x = groups(args["x"].rearrange("b n d -> (b n) d"))
        out = groups(args["out"].rearrange("b n d -> (b n) d"))
        x2 = groups(nc.dram_tensor("x2_scratch", [ROWS, D], F32).ap())
        with ExitStack() as first:
            HT = first.enter_context(nc.sbuf_tensor("HT", [P, KD, ROWS], F32))[:, :, :]
            with ExitStack() as lstm:
                ahead = lstm_first_weights(allocator(nc, lstm)[0])
                gcn_phase(core, x, args["gcn_w"], args["gcn_b"], args["adj_t"], HT, args["wih"], ahead)
                lstm_phase(core, args["wih"], args["whh"], args["bih"], args["bhh"], HT, ahead)
            attention_layer(core, args, x, x2, HT)
        later_layers(core, args, x2, out)


def layouts(inp):
    import numpy as np

    def chunks(w):
        return np.ascontiguousarray(w.reshape(-1, P, w.shape[1]).transpose(1, 0, 2))

    def alike(v):
        return np.ascontiguousarray(np.broadcast_to(v.reshape(1, -1), (P, v.size)))

    def columns(v):
        return np.ascontiguousarray(v.reshape(-1, P).T)

    def gates(b):
        return np.ascontiguousarray(b.reshape(SKIPS, -1, P).transpose(2, 0, 1))

    i = {k: np.asarray(v) for k, v in inp.items()}
    edge = np.arange(EDGES, dtype=np.float32)
    return {
        "x": i["x"], "adj": i["adj"], "adj_t": np.ascontiguousarray(i["adj"].T), "ident": np.eye(P, dtype=np.float32),
        "gcn_w": np.stack([chunks(i["L0_gnn_Wg0"]), chunks(i["L0_gnn_Wg1"])]),
        "gcn_b": np.stack([alike(i["L0_gnn_bg0"]), alike(i["L0_gnn_bg1"])]),
        "wih": np.stack([chunks(w.T) for w in i["L0_gnn_Wih"]]), "whh": np.stack([chunks(w.T) for w in i["L0_gnn_Whh"]]),
        "bih": gates(i["L0_gnn_bih"]), "bhh": gates(i["L0_gnn_bhh"]),
        "src_row": alike(i["L1_gnn_src"]), "dst_row": alike(i["L1_gnn_dst"]),
        "src_col": columns(i["L1_gnn_src"]), "dst_col": columns(i["L1_gnn_dst"]),
        "iota_row": alike(edge), "iota_col": columns(edge),
        "node_col": np.tile(np.arange(NODES, dtype=np.float32), TILE_GRAPHS).reshape(P, 1),
        "a_row": alike(i["L1_gnn_a"]), "a_col": columns(i["L1_gnn_a"]),
        "w_lin": chunks(i["L1_gnn_W_lin"].T), "w_val": chunks(i["L1_gnn_W_val"].T), "w_out": chunks(i["L1_gnn_W_out"].T),
        "w1": chunks(i["L2_gnn_W1"].T), "w2": chunks(i["L2_gnn_W2"].T),
        "b1": columns(i["L2_gnn_b1"]), "g1": columns(i["L2_gnn_g1"]), "be1": columns(i["L2_gnn_be1"]),
        "b2": columns(i["L2_gnn_b2"]), "g2": columns(i["L2_gnn_g2"]), "be2": columns(i["L2_gnn_be2"]),
        "w3": chunks(i["L3_gnn_W"]), "a3": alike(i["L3_gnn_a"]),
    }


def kernel(**inputs):
    import numpy as np
    import concourse.bacc as bacc
    from concourse.bass_utils import run_bass_kernel_spmd

    nc = bacc.Bacc("TRN2", target_bir_lowering=False, num_devices=1)
    arrays, args = {}, {}
    for name, a in layouts(inputs).items():
        arrays[f"in_{name}"] = a
        args[name] = nc.dram_tensor(f"in_{name}", a.shape, mybir.dt.from_np(a.dtype), kind="ExternalInput").ap()
    args["out"] = nc.dram_tensor("out", [BATCH, NODES, D], F32, kind="ExternalOutput").ap()
    build(nc, args)
    r = run_bass_kernel_spmd(nc, [arrays], core_ids=[0])
    return np.asarray(r.results[0]["out"])
```
